# Optimizing a Trainium2 kernel written in Bass

```python
import numpy as np
import jax
import jax.numpy as jnp

def _softmax(x, axis=-1):
    return jax.nn.softmax(x, axis=axis)

def _gelu(x):
    return jax.nn.gelu(x, approximate=True)

def _silu(x):
    return jax.nn.silu(x)

def _sigmoid(x):
    return jax.nn.sigmoid(x)

def _layernorm(x, axis=-1, eps=1e-05):
    m = jnp.mean(x, axis=axis, keepdims=True)
    v = jnp.var(x, axis=axis, keepdims=True)
    return (x - m) / jnp.sqrt(v + eps)

def _scatter_add(tgt, idx, src, axis=0):
    return tgt.at[idx].add(src)

def _segment_sum(src, seg, n):
    return jax.ops.segment_sum(src, seg, n)
kernel_name = 'mk_adj_resnorm_d4_adj_r2_bd1acd'

def setup_inputs(seed: int=0):
    np.random.seed(seed)
    _w = jnp.asarray

    def _rec_inputs():
        import jax
        import jax.numpy as jnp
        _gk = jax.random.key(seed)
        x = -0.0005207 + 1.001 * jax.random.normal(jax.random.fold_in(_gk, 1), (4096, 128), jnp.float32)
        _a = jax.random.bernoulli(jax.random.fold_in(_gk, 2), 0.000488281, (4096, 4096))
        _a = jnp.logical_or(_a, jnp.eye(4096, dtype=bool))
        _af = _a.astype(jnp.float32)
        _af = _af * jax.random.uniform(jax.random.fold_in(_gk, 3), (4096, 4096), jnp.float32, 0.05, 1)
        adj = _af
        return (x, adj)
    x, adj = _rec_inputs()

    def _L0_gnn_setup():
        import jax, jax.numpy as jnp
        import numpy as np
        D_IN = 128
        D_ATTN = 64
        STEPS = 2
        TOP_P = 0.9
        TAU = 1.0
        LN_EPS = 1e-05
        N_NODES = 4096

        def _top_p_attention(X, W1, W2, W3):
            q = X @ W1.T @ W2.T
            k = X @ W3.T
            logits = q @ k.T / TAU
            probs = jax.nn.softmax(logits, axis=-1)
            idx = jnp.argsort(-probs, axis=-1)
            sp = jnp.take_along_axis(probs, idx, axis=-1)
            cs = jnp.cumsum(sp, axis=-1)
            keep_sorted = cs - sp < TOP_P
            rows = jnp.arange(probs.shape[0])[:, None]
            mask = jnp.zeros(probs.shape, dtype=bool).at[rows, idx].set(keep_sorted)
            A = probs * mask
            return A / jnp.maximum(A.sum(-1, keepdims=True), 1e-12)
        key = jax.random.key(seed)
        ks = jax.random.split(key, 8)
        N, d, da, steps = (N_NODES, D_IN, D_ATTN, STEPS)
        X = jax.random.normal(ks[0], (N, d), dtype=jnp.float32)
        S = jax.random.uniform(ks[1], (N, N), dtype=jnp.float32)
        W1 = jax.random.normal(ks[2], (da, d), dtype=jnp.float32) / np.sqrt(d)
        W2 = jax.random.normal(ks[3], (da, da), dtype=jnp.float32) / np.sqrt(da)
        W3 = jax.random.normal(ks[4], (da, d), dtype=jnp.float32) / np.sqrt(d)
        U1 = jax.random.normal(ks[5], (steps, d, d), dtype=jnp.float32) / np.sqrt(d)
        U2 = jax.random.normal(ks[6], (steps, d, d), dtype=jnp.float32) / np.sqrt(d)
        ln_g = jnp.ones((d,), dtype=jnp.float32)
        ln_b = jnp.zeros((d,), dtype=jnp.float32)
        return {'X': X, 'S': S, 'W1': W1, 'W2': W2, 'W3': W3, 'U1': U1, 'U2': U2, 'ln_g': ln_g, 'ln_b': ln_b}
    _L0_gnn_all = _L0_gnn_setup()
    _L0_gnn_in = {k: v for k, v in _L0_gnn_all.items() if k in ('W1', 'W2', 'W3', 'U1', 'U2', 'ln_g', 'ln_b')}
    del _L0_gnn_all

    def _L1_gnn_setup():
        import jax, jax.numpy as jnp
        import numpy as np
        N = 2048
        IN_F = 128
        OUT_F = 128
        H = 4
        FH = OUT_F // H
        ALPHA = 0.2
        DENSITY = 0.01
        key = jax.random.key(seed)
        k1, k2, k3, k4 = jax.random.split(key, 4)
        h = jax.random.normal(k1, (N, IN_F), dtype=jnp.float32)
        adj = (jax.random.uniform(k2, (N, N)) < DENSITY).astype(jnp.float32)
        adj = adj.at[jnp.arange(N), jnp.arange(N)].set(1.0)
        W = jax.random.normal(k3, (IN_F, H * FH), dtype=jnp.float32) / np.sqrt(IN_F)
        a = jax.random.normal(k4, (H, 2 * FH), dtype=jnp.float32) * 0.1
        return {'h': h, 'adj': adj, 'W': W, 'a': a}
    _L1_gnn_all = _L1_gnn_setup()
    _L1_gnn_in = {k: v for k, v in _L1_gnn_all.items() if k in ('W', 'a')}
    del _L1_gnn_all

    def _L2_gnn_setup():
        import jax, jax.numpy as jnp
        import numpy as np
        N = 4096
        DIM = 128
        HEADS = 4
        HD = DIM // HEADS
        SCALE = HD ** (-0.5)
        key = jax.random.key(seed)
        ks = jax.random.split(key, 8)
        x = jax.random.normal(ks[0], (N, DIM), dtype=jnp.float32)
        adj_matrix = jax.random.uniform(ks[1], (N, N), dtype=jnp.float32)
        attn_mask = jax.random.randint(ks[2], (N, N), 0, 2, dtype=jnp.int32)
        Wqkv = jax.random.normal(ks[3], (DIM, 3 * DIM), dtype=jnp.float32) * DIM ** (-0.5)
        bqkv = jnp.zeros((3 * DIM,), dtype=jnp.float32)
        Wout = jax.random.normal(ks[4], (DIM, DIM), dtype=jnp.float32) * DIM ** (-0.5)
        bout = jnp.zeros((DIM,), dtype=jnp.float32)
        graph_bias = jax.random.normal(ks[5], (1, 1, 1), dtype=jnp.float32) * 0.1
        return {'x': x, 'adj_matrix': adj_matrix, 'attn_mask': attn_mask, 'Wqkv': Wqkv, 'bqkv': bqkv, 'Wout': Wout, 'bout': bout, 'graph_bias': graph_bias}
    _L2_gnn_all = _L2_gnn_setup()
    _L2_gnn_in = {k: v for k, v in _L2_gnn_all.items() if k in ('Wqkv', 'bqkv', 'Wout', 'bout', 'graph_bias')}
    del _L2_gnn_all

    def _L3_gnn_setup():
        import jax, jax.numpy as jnp
        import numpy as np
        N = 4096
        D_IN = 128
        D_OUT = 128
        key = jax.random.key(seed)
        k1, k2, k3 = jax.random.split(key, 3)
        x = jax.random.normal(k1, (N, D_IN), dtype=jnp.float32)
        adj = jax.random.uniform(k2, (N, N), dtype=jnp.float32)
        W = jax.random.normal(k3, (D_OUT, D_IN), dtype=jnp.float32) * (1.0 / np.sqrt(D_IN))
        return {'x': x, 'adj': adj, 'W': W}
    _L3_gnn_all = _L3_gnn_setup()
    _L3_gnn_in = {k: v for k, v in _L3_gnn_all.items() if k in ('W',)}
    del _L3_gnn_all
    return {'x': x, 'adj': adj, 'L0_gnn_W1': _L0_gnn_in['W1'], 'L0_gnn_W2': _L0_gnn_in['W2'], 'L0_gnn_W3': _L0_gnn_in['W3'], 'L0_gnn_U1': _L0_gnn_in['U1'], 'L0_gnn_U2': _L0_gnn_in['U2'], 'L0_gnn_ln_g': _L0_gnn_in['ln_g'], 'L0_gnn_ln_b': _L0_gnn_in['ln_b'], 'L1_gnn_W': _L1_gnn_in['W'], 'L1_gnn_a': _L1_gnn_in['a'], 'L2_gnn_Wqkv': _L2_gnn_in['Wqkv'], 'L2_gnn_bqkv': _L2_gnn_in['bqkv'], 'L2_gnn_Wout': _L2_gnn_in['Wout'], 'L2_gnn_bout': _L2_gnn_in['bout'], 'L2_gnn_graph_bias': _L2_gnn_in['graph_bias'], 'L3_gnn_W': _L3_gnn_in['W']}

def reference(x, adj, L0_gnn_W1, L0_gnn_W2, L0_gnn_W3, L0_gnn_U1, L0_gnn_U2, L0_gnn_ln_g, L0_gnn_ln_b, L1_gnn_W, L1_gnn_a, L2_gnn_Wqkv, L2_gnn_bqkv, L2_gnn_Wout, L2_gnn_bout, L2_gnn_graph_bias, L3_gnn_W):
    import jax
    import jax.numpy as jnp

    def _L0_gnn_ref(X, S, W1, W2, W3, U1, U2, ln_g, ln_b):
        import jax, jax.numpy as jnp
        import numpy as np
        D_IN = 128
        D_ATTN = 64
        STEPS = 2
        TOP_P = 0.9
        TAU = 1.0
        LN_EPS = 1e-05
        N_NODES = 4096

        def _top_p_attention(X, W1, W2, W3):
            q = X @ W1.T @ W2.T
            k = X @ W3.T
            logits = q @ k.T / TAU
            probs = jax.nn.softmax(logits, axis=-1)
            idx = jnp.argsort(-probs, axis=-1)
            sp = jnp.take_along_axis(probs, idx, axis=-1)
            cs = jnp.cumsum(sp, axis=-1)
            keep_sorted = cs - sp < TOP_P
            rows = jnp.arange(probs.shape[0])[:, None]
            mask = jnp.zeros(probs.shape, dtype=bool).at[rows, idx].set(keep_sorted)
            A = probs * mask
            return A / jnp.maximum(A.sum(-1, keepdims=True), 1e-12)
        N = X.shape[0]
        R = S + jnp.eye(N, dtype=X.dtype)
        R = R / R.sum(-1, keepdims=True)
        Z = jnp.zeros_like(X)
        Xf = X
        Xa = X
        for n in range(STEPS):
            A = _top_p_attention(Xa, W1, W2, W3)
            Xf = R @ Xf
            Xa = A @ Xa
            Z = Z + Xf @ U1[n].T + Xa @ U2[n].T
        h = X + Z
        mu = h.mean(-1, keepdims=True)
        var = jnp.mean((h - mu) ** 2, axis=-1, keepdims=True)
        return (h - mu) / jnp.sqrt(var + LN_EPS) * ln_g + ln_b

    def _L1_gnn_ref(h, adj, W, a):
        import jax, jax.numpy as jnp
        import numpy as np
        N = 2048
        IN_F = 128
        OUT_F = 128
        H = 4
        FH = OUT_F // H
        ALPHA = 0.2
        DENSITY = 0.01
        n = h.shape[0]
        hp = (h @ W).reshape(n, H, FH)
        a_src, a_dst = (a[:, :FH], a[:, FH:])
        s = jnp.einsum('nhf,hf->hn', hp, a_src)
        d = jnp.einsum('nhf,hf->hn', hp, a_dst)
        e = jax.nn.leaky_relu(s[:, :, None] + d[:, None, :], ALPHA)
        e = jnp.where(adj[None, :, :] > 0, e, -jnp.inf)
        attn = jax.nn.softmax(e, axis=2)
        out = jnp.einsum('hij,jhf->ihf', attn, hp).reshape(n, H * FH)
        return jax.nn.elu(out)

    def _L2_gnn_ref(x, adj_matrix, attn_mask, Wqkv, bqkv, Wout, bout, graph_bias):
        import jax, jax.numpy as jnp
        import numpy as np
        N = 4096
        DIM = 128
        HEADS = 4
        HD = DIM // HEADS
        SCALE = HD ** (-0.5)
        n, d = x.shape
        qkv = x @ Wqkv + bqkv
        q, k, v = jnp.split(qkv, 3, axis=-1)

        def split_heads(t):
            return t.reshape(n, HEADS, HD).transpose(1, 0, 2)
        qh, kh, vh = (split_heads(q), split_heads(k), split_heads(v))
        scores = jnp.einsum('hnd,hmd->hnm', qh, kh) * SCALE
        scores = scores + graph_bias * adj_matrix[None, :, :]
        scores = jnp.where(attn_mask[None, :, :] == 0, jnp.float32(-1000000000.0), scores)
        attn = jax.nn.softmax(scores, axis=-1)
        out = jnp.einsum('hnm,hmd->hnd', attn, vh)
        out = out.transpose(1, 0, 2).reshape(n, d)
        return out @ Wout + bout

    def _L3_gnn_ref(x, adj, W):
        import jax, jax.numpy as jnp
        import numpy as np
        N = 4096
        D_IN = 128
        D_OUT = 128
        A_hat = adj + jnp.eye(adj.shape[0], dtype=adj.dtype)
        d_inv_sqrt = jnp.sum(A_hat, axis=1) ** (-0.5)
        A_norm = d_inv_sqrt[:, None] * A_hat * d_inv_sqrt[None, :]
        support = x @ W.T
        out = A_norm @ support
        return jax.nn.relu(out)
    x = _layernorm(x + _L0_gnn_ref(x, adj, L0_gnn_W1, L0_gnn_W2, L0_gnn_W3, L0_gnn_U1, L0_gnn_U2, L0_gnn_ln_g, L0_gnn_ln_b), axis=-1)
    x = _layernorm(x + _L1_gnn_ref(x, adj, L1_gnn_W, L1_gnn_a), axis=-1)
    x = _layernorm(x + _L2_gnn_ref(x, adj, adj, L2_gnn_Wqkv, L2_gnn_bqkv, L2_gnn_Wout, L2_gnn_bout, L2_gnn_graph_bias), axis=-1)
    x = _layernorm(x + _L3_gnn_ref(x, adj, L3_gnn_W), axis=-1)
    return x

_drawn_inputs = setup_inputs


def setup_inputs(seed=0):
    import zlib

    import numpy as np

    out = dict(_drawn_inputs(seed))
    spreads = {'L0_gnn_ln_g': (1.0, 0.2),
     'L0_gnn_ln_b': (0.0, 0.1),
     'L2_gnn_bqkv': (0.0, 0.1),
     'L2_gnn_bout': (0.0, 0.1)}
    factors = {}
    for name, (base, spread) in spreads.items():
        noise = np.random.default_rng([zlib.crc32(name.encode()), seed]).standard_normal(out[name].shape)
        drawn = base * np.exp(spread * noise) if base else spread * noise
        out[name] = jnp.asarray(drawn.astype(out[name].dtype))
    for name, factor in factors.items():
        out[name] = (out[name] * factor).astype(out[name].dtype)
    return out
```

```python
import concourse.bass as bass
from concourse import mybir
from contextlib import ExitStack

F32 = mybir.dt.float32
BF16 = mybir.dt.bfloat16
I32 = mybir.dt.int32
U32 = mybir.dt.uint32
ALU = mybir.AluOpType
ACT = mybir.ActivationFunctionType
AX = mybir.AxisListType

P = 128
N = 4096
T = N // P
D = 128
DA = 64
H = 4
HD = D // H
G8 = 8
TILE_COL = 2 * G8
LIST = TILE_COL + 1
MAX_UNITS = T * (N // G8) + 1
CHUNK = 512
TOP_P = 0.9
BIG = 1e30
BISECTIONS = (5, 9)


def node_view(ap):
    return ap.rearrange("(t p) d -> p t d", p=P)


def wait_apart(eng, sem, value):
    value = eng.to_reg(value)
    eng.wait_ge(sem, 1)
    eng.wait_ge(sem, value)


def any_row(dve, nc, flags, flags_t, total, total_i, go, summed, n_summed):
    nc.vector.transpose(flags_t[:, :], flags[:, :])
    nc.vector.drain()
    nc.vector.tensor_reduce(total[:, :], flags_t[:, :], AX.X, ALU.add)
    nc.vector.drain()
    nc.vector.tensor_copy(total_i[:, :], total[:, :]).then_inc(summed, 1)
    dve.reg_mov(n_summed, dve.snap(n_summed) + 1)
    wait_apart(dve, summed, dve.snap(n_summed))
    read_flags(dve, total_i, go)


def read_flags(eng, total_i, go):
    parts = [eng.value_load(total_i[32 * q:32 * q + 1, 0:1]) for q in range(4)]
    eng.reg_mov(go, parts[0] + parts[1] + parts[2] + parts[3])


def find_neighbours(nc, adj, tile_ids, lists, deg, units_i):
    with ExitStack() as ctx:
        def sb(name, shape, dt=F32):
            return ctx.enter_context(nc.sbuf_tensor(name, shape, dt))

        rows = [sb(f"adj_rows{j}", [P, N]) for j in range(2)]
        found = sb("found", [P, LIST], I32)
        ids = sb("ids", [P, T], I32)
        flags = sb("nb_flags", [P, 32])
        flags_t = sb("nb_flags_t", [P, 32])
        total = sb("nb_total", [P, 1])
        total_i = sb("nb_total_i", [P, 1], I32)
        part = sb("nb_part", [P, 1])
        units = sb("units", [P, 1])
        rows_loaded = [ctx.enter_context(nc.semaphore(f"rows_loaded{j}")) for j in range(2)]
        rows_done = ctx.enter_context(nc.semaphore("rows_done"))
        found_ready = ctx.enter_context(nc.semaphore("found_ready"))
        found_free = ctx.enter_context(nc.semaphore("found_free"))
        summed = ctx.enter_context(nc.semaphore("nb_summed"))
        values = found[:, G8:TILE_COL].bitcast(F32)
        indices = found[:, 0:G8].bitcast(U32)
        block = ctx.enter_context(nc.Block())

        @block.scalar
        def _(act):
            def load(t, j):
                act.dma_start(rows[j][:, :], adj[bass.ds(t * P, P), :]).then_inc(rows_loaded[j], 16)

            for j in range(2):
                load(j, j)
            with act.Fori(1, T // 2) as i:
                for j in range(2):
                    act.wait_ge(rows_done, 2 * i + j - 1)
                    load(2 * i + j, j)

        @block.vector
        def _(dve):
            V = nc.vector
            V.memset(flags[:, :], 0.0)
            V.memset(deg[:, :], 0.0)
            V.memset(units[:, :], 0.0)
            V.drain()
            n = dve.alloc_register("nb_n")
            go = dve.alloc_register("nb_go")
            n_summed = dve.alloc_register("nb_n_summed")
            dve.reg_mov(n, 0)
            dve.reg_mov(n_summed, 0)
            with dve.Fori(0, T // 2) as i:
                for j in range(2):
                    t = 2 * i + j
                    wait_apart(dve, rows_loaded[j], 16 * i + 16)
                    dve.reg_mov(go, 1)
                    with dve.While(lambda: dve.snap(go)):
                        wait_apart(dve, found_free, 16 * dve.snap(n) + 16)
                        V.max(values, rows[j][:, :])
                        V.tensor_copy(found[:, TILE_COL:LIST], ids[:, bass.ds(t, 1)])
                        V.drain()
                        V.max_index(indices, values, rows[j][:, :])
                        V.tensor_scalar(flags[:, 0:1], found[:, TILE_COL - 1:TILE_COL].bitcast(F32), 0.0, None,
                                        ALU.is_gt)
                        V.tensor_reduce(part[:, :], values, AX.X, ALU.add)
                        V.tensor_scalar(units[:, :], units[:, :], 1.0, None, ALU.add)
                        V.drain()
                        V.tensor_tensor(deg[:, bass.ds(t, 1)], deg[:, bass.ds(t, 1)], part[:, :], ALU.add)
                        V.match_replace(rows[j][:, :], values, rows[j][:, :], 0.0)
                        any_row(dve, nc, flags, flags_t, total, total_i, go, summed, n_summed)
                        dve.reg_mov(n, dve.snap(n) + 1)
                        V.engine_nop().then_inc(found_ready, 1)
                    V.drain()
                    V.engine_nop().then_inc(rows_done, 1)
            dve.wait_ge(found_free, 16 * dve.snap(n) + 16)
            V.tensor_copy(units_i[:, :], units[:, :])
            V.memset(found[:, :], 0)
            V.drain()
            V.engine_nop().then_inc(found_ready, 1)

        @block.sync
        def _(sp):
            sp.dma_start(ids[:, :], tile_ids).then_inc(found_free, 16)
            n = sp.alloc_register("nb_sp_n")
            go = sp.alloc_register("nb_sp_go")
            sp.reg_mov(n, 0)

            def store():
                sp.dma_start(lists[bass.ds(sp.snap(n), 1), :, :].rearrange("a p c -> p (a c)"),
                             found[:, :]).then_inc(found_free, 16)
                sp.reg_mov(n, sp.snap(n) + 1)

            with sp.Fori(0, T):
                sp.reg_mov(go, 1)
                with sp.While(lambda: sp.snap(go)):
                    wait_apart(sp, found_ready, sp.snap(n) + 1)
                    read_flags(sp, total_i, go)
                    store()
            sp.wait_ge(found_ready, sp.snap(n) + 1)
            store()
            wait_apart(sp, found_free, 16 * sp.snap(n) + 16)


def gather_units(nc, name, table, width, lists, units_i, dve_unit, act_unit=None):
    with ExitStack() as ctx:
        def sb(nm, shape, dt=F32):
            return ctx.enter_context(nc.sbuf_tensor(f"{name}_{nm}", shape, dt))

        def sem(nm):
            return ctx.enter_context(nc.semaphore(f"{name}_{nm}"))

        lst = [sb(f"list{j}", [P, LIST], I32) for j in range(2)]
        got = [sb(f"got{j}", [P, G8 * width]) for j in range(2)]
        listed = [sem(f"listed{j}") for j in range(2)]
        gathered = [sem(f"gathered{j}") for j in range(2)]
        unit_used = sem("unit_used")
        block = ctx.enter_context(nc.Block())

        def pairs(eng):
            units = eng.value_load(units_i[0:1, 0:1])
            return (units + 1) // 2

        @block.sync
        def _(sp):
            def load(u, j):
                sp.dma_start(lst[j][:, :], lists[bass.ds(u, 1), :, :].rearrange("a p c -> p (a c)")
                             ).then_inc(listed[j], 16)

            n = pairs(sp)
            for j in range(2):
                load(j, j)
            with sp.Fori(1, n) as i:
                for j in range(2):
                    sp.wait_ge(unit_used, 2 * i + j - 1)
                    load(2 * i + j, j)

        @block.gpsimd
        def _(pool):
            with pool.Fori(0, pairs(pool)) as i:
                for j in range(2):
                    wait_apart(pool, listed[j], 16 * i + 16)
                    for k in range(G8):
                        pool.indirect_dma_start(
                            got[j][:, k * width:(k + 1) * width], None, table,
                            bass.IndirectOffsetOnAxis(ap=lst[j][:, k:k + 1].bitcast(U32), axis=0),
                        ).then_inc(gathered[j], 16)

        @block.vector
        def _(dve):
            with dve.Fori(0, pairs(dve)) as i:
                for j in range(2):
                    wait_apart(dve, listed[j], 16 * i + 16)
                    t = dve.value_load(lst[j][0:1, TILE_COL:LIST], min_val=0, max_val=T - 1)
                    dve.wait_ge(gathered[j], 16 * G8 * (i + 1))
                    dve_unit(dve, 2 * i + j, t, lst[j][:, G8:TILE_COL].bitcast(F32),
                             got[j][:, :].rearrange("p (k w) -> p k w", k=G8))
                    nc.vector.drain()
                    nc.vector.engine_nop().then_inc(unit_used, 1)

        if act_unit is not None:
            @block.scalar
            def _(act):
                with act.Fori(0, pairs(act)) as i:
                    for j in range(2):
                        act_unit(act, 2 * i + j)


def weighted_sum(nc, name, table, lists, units_i, acc):
    with nc.sbuf_tensor(f"{name}_prod", [P, G8 * D], F32) as prod, \
         nc.sbuf_tensor(f"{name}_sum", [P, D], F32) as part:
        def unit(dve, u, t, values, got):
            V = nc.vector
            p3 = prod[:, :].rearrange("p (k d) -> p k d", k=G8)
            V.tensor_tensor(p3, got, values.unsqueeze(2).to_broadcast([P, G8, D]), ALU.mult)
            V.drain()
            V.tensor_reduce(part[:, :], prod[:, :].rearrange("p (k d) -> p d k", k=G8), AX.X, ALU.add)
            V.drain()
            row = acc[:, bass.ds(t, 1), :].rearrange("p a d -> p (a d)")
            V.tensor_tensor(row, row, part[:, :], ALU.add)

        gather_units(nc, name, table, D, lists, units_i, unit)


def graph_attention(nc, name, table, width, value_at, scores, lists, units_i, acc, denom):
    with ExitStack() as ctx:
        def sb(nm, shape, dt=F32):
            return ctx.enter_context(nc.sbuf_tensor(f"{name}_{nm}", shape, dt))

        top = sb("top", [P, T, H])
        new_top = sb("new_top", [P, H])
        score = sb("score", [P, G8, H])
        absent = sb("absent", [P, G8])
        power = sb("power", [P, (1 + G8) * H])
        raised = sb("raised", [P, (1 + G8) * H])
        psum = sb("psum", [P, H])
        prod = sb("prod", [P, G8 * D])
        part = sb("part", [P, D])
        power_ready = ctx.enter_context(nc.semaphore(f"{name}_power_ready"))
        raised_ready = ctx.enter_context(nc.semaphore(f"{name}_raised_ready"))
        start = ctx.enter_context(nc.semaphore(f"{name}_start"))
        with nc.Block() as first:
            @first.vector
            def _(dve):
                nc.vector.memset(top[:, :, :], -BIG)
                nc.vector.memset(denom[:, :, :], 0.0)
                nc.vector.memset(acc[:, :, :], 0.0).then_inc(start, 1)
                dve.wait_ge(start, 1)

        def unit(dve, u, t, values, got):
            V = nc.vector
            topt = top[:, bass.ds(t, 1), :].rearrange("p a h -> p (a h)")
            dent = denom[:, bass.ds(t, 1), :].rearrange("p a h -> p (a h)")
            acct = acc[:, bass.ds(t, 1), :].rearrange("p a d -> p (a d)")
            V.tensor_scalar(absent[:, :], values, 0.0, -1.0, ALU.is_gt, ALU.add)
            scores(dve, t, values, got, score, prod)
            V.drain()
            V.scalar_tensor_tensor(out=score[:, :, :], in0=absent[:, :].unsqueeze(2).to_broadcast([P, G8, H]),
                                   scalar=BIG, in1=score[:, :, :], op0=ALU.mult, op1=ALU.add)
            V.drain()
            V.tensor_reduce(new_top[:, :], score[:, :, :].rearrange("p k h -> p h k"), AX.X, ALU.max)
            V.drain()
            V.tensor_tensor(new_top[:, :], new_top[:, :], topt, ALU.max)
            V.drain()
            V.tensor_tensor(power[:, 0:H], topt, new_top[:, :], ALU.subtract)
            V.tensor_tensor(power[:, H:].rearrange("p (k h) -> p k h", k=G8), score[:, :, :],
                            new_top[:, :].unsqueeze(1).to_broadcast([P, G8, H]), ALU.subtract)
            V.drain()
            V.tensor_copy(topt, new_top[:, :]).then_inc(power_ready, 1)
            dve.wait_ge(raised_ready, u + 1)
            keep = raised[:, 0:H]
            weight = raised[:, H:].rearrange("p (k h) -> p k h", k=G8)
            V.tensor_reduce(psum[:, :], raised[:, H:].rearrange("p (k h) -> p h k", k=G8), AX.X, ALU.add)
            V.tensor_tensor(dent, dent, keep, ALU.mult)
            V.tensor_tensor(prod[:, :].rearrange("p (k h f) -> p k h f", k=G8, h=H),
                            got[:, :, value_at:value_at + D].rearrange("p k (h f) -> p k h f", h=H),
                            weight.unsqueeze(3).to_broadcast([P, G8, H, HD]), ALU.mult)
            V.tensor_tensor(acct.rearrange("p (h f) -> p h f", h=H), acct.rearrange("p (h f) -> p h f", h=H),
                            keep.unsqueeze(2).to_broadcast([P, H, HD]), ALU.mult)
            V.drain()
            V.tensor_tensor(dent, dent, psum[:, :], ALU.add)
            V.tensor_reduce(part[:, :], prod[:, :].rearrange("p (k d) -> p d k", k=G8), AX.X, ALU.add)
            V.drain()
            V.tensor_tensor(acct, acct, part[:, :], ALU.add)

        def act_unit(act, u):
            act.wait_ge(power_ready, u + 1)
            nc.scalar.activation(raised[:, :], power[:, :], ACT.Exp).then_inc(raised_ready, 1)

        gather_units(nc, name, table, width, lists, units_i, unit, act_unit)


def project(nc, name, src, ident, outs):
    groups = T // 4
    nw = len(outs)
    with ExitStack() as ctx:
        def sem(nm):
            return ctx.enter_context(nc.semaphore(f"{name}_{nm}"))

        stage = [ctx.enter_context(nc.sbuf_tensor(f"{name}_stage{j}", [P, CHUNK], F32)) for j in range(2)]
        turned = [ctx.enter_context(nc.sbuf_tensor(f"{name}_turned{j}", [P, CHUNK], F32)) for j in range(2)]
        turn_ps = [ctx.enter_context(nc.psum_tensor(f"{name}_turn_ps{j}", [P, CHUNK], F32)) for j in range(2)]
        out_ps = [ctx.enter_context(nc.psum_tensor(f"{name}_out_ps{j}", [P, 4, D], F32)) for j in range(2)]
        staged, turned_ps, turned_sb, multiplied, evicted = (
            sem("staged"), sem("turned_ps"), sem("turned_sb"), sem("multiplied"), sem("evicted"))
        block = ctx.enter_context(nc.Block())

        @block.gpsimd
        def _(pool):
            def group(g, j, first):
                if not first:
                    pool.wait_ge(turned_ps, g - 1)
                nc.gpsimd.tensor_copy(stage[j][:, :].rearrange("p (a d) -> p a d", a=4),
                                      src[:, bass.ds(4 * g, 4), :]).then_inc(staged, 1)

            for j in range(2):
                group(j, j, True)
            with pool.Fori(1, groups // 2) as i:
                for j in range(2):
                    group(2 * i + j, j, False)

        @block.scalar
        def _(act):
            def group(g, j, first):
                act.wait_ge(turned_ps, g + 1)
                if not first:
                    act.wait_ge(multiplied, nw * (g - 1))
                nc.scalar.copy(turned[j][:, :], turn_ps[j][:, :]).then_inc(turned_sb, 1)

            for j in range(2):
                group(j, j, True)
            with act.Fori(1, groups // 2) as i:
                for j in range(2):
                    group(2 * i + j, j, False)

        @block.tensor
        def _(pe):
            def group(g, j, first):
                pe.wait_ge(staged, g + 1)
                if not first:
                    pe.wait_ge(turned_sb, g - 1)
                for a in range(4):
                    last = nc.tensor.transpose(turn_ps[j][:, a * P:(a + 1) * P], stage[j][:, a * D:(a + 1) * D],
                                               ident[:, :])
                last.then_inc(turned_ps, 1)
                pe.wait_ge(turned_sb, g + 1)
                for w, (weight, _) in enumerate(outs):
                    m = nw * g + w
                    b = (nw * j + w) % 2
                    if not first or nw * j + w >= 2:
                        pe.wait_ge(evicted, m - 1)
                    for a in range(4):
                        last = nc.tensor.matmul(out_ps[b][:, a, :], turned[j][:, a * P:(a + 1) * P], weight,
                                                start=True, stop=True)
                    last.then_inc(multiplied, 1)

            for j in range(2):
                group(j, j, True)
            with pe.Fori(1, groups // 2) as i:
                for j in range(2):
                    group(2 * i + j, j, False)

        @block.vector
        def _(dve):
            with dve.Fori(0, groups // 2) as i:
                for j in range(2):
                    g = 2 * i + j
                    for w, (_, evict) in enumerate(outs):
                        dve.wait_ge(multiplied, nw * g + w + 1)
                        evict(g, out_ps[(nw * j + w) % 2]).then_inc(evicted, 1)


def layer_norms(nc, name, x, rounds):
    with ExitStack() as ctx:
        square = ctx.enter_context(nc.sbuf_tensor(f"{name}_square", [P, T, D], F32))
        mean = ctx.enter_context(nc.sbuf_tensor(f"{name}_mean", [P, T], F32))
        var = ctx.enter_context(nc.sbuf_tensor(f"{name}_var", [P, T], F32))
        dev = ctx.enter_context(nc.sbuf_tensor(f"{name}_dev", [P, T], F32))
        var_ready = ctx.enter_context(nc.semaphore(f"{name}_var_ready"))
        dev_ready = ctx.enter_context(nc.semaphore(f"{name}_dev_ready"))
        block = ctx.enter_context(nc.Block())

        def wide(a):
            return a[:, :].unsqueeze(2).to_broadcast([P, T, D])

        @block.vector
        def _(dve):
            V = nc.vector
            for r, before in enumerate(rounds):
                before(dve)
                V.drain()
                V.tensor_reduce(mean[:, :], x, AX.X, ALU.add)
                V.drain()
                V.tensor_scalar(mean[:, :], mean[:, :], 1.0 / D, None, ALU.mult)
                V.drain()
                V.tensor_tensor(x, x, wide(mean), ALU.subtract)
                V.drain()
                V.tensor_tensor(square[:, :, :], x, x, ALU.mult)
                V.drain()
                V.tensor_reduce(var[:, :], square[:, :, :], AX.X, ALU.add)
                V.drain()
                V.tensor_scalar(var[:, :], var[:, :], 1.0 / D, 1e-5, ALU.mult, ALU.add).then_inc(var_ready, 1)
                dve.wait_ge(dev_ready, r + 1)
                V.reciprocal(var[:, :], dev[:, :])
                V.drain()
                V.tensor_tensor(x, x, wide(var), ALU.mult)
            V.drain()

        @block.scalar
        def _(act):
            for r in range(len(rounds)):
                act.wait_ge(var_ready, r + 1)
                nc.scalar.activation(dev[:, :], var[:, :], ACT.Sqrt).then_inc(dev_ready, 1)


def copy_dram(nc, name, pairs):
    with nc.semaphore(f"{name}_moved") as moved, nc.Block() as block:
        @block.sync
        def _(sp):
            for out, in_ in pairs:
                sp.dma_start(out, in_).then_inc(moved, 16)
            sp.wait_ge(moved, 16 * len(pairs))


def top_p_step(nc, name, halvings, weights, u2_t, ident, x_t, rows, new_rows, z):
    w1_t, w2_t, w3_t = weights
    with ExitStack() as ctx:
        def sb(nm, shape, dt=F32):
            return ctx.enter_context(nc.sbuf_tensor(f"{name}_{nm}", shape, dt))

        def sem(nm):
            return ctx.enter_context(nc.semaphore(f"{name}_{nm}"))

        q_t = sb("q_t", [DA, N])
        k_t = sb("k_t", [DA, N])

        with ExitStack() as first:
            half = first.enter_context(nc.sbuf_tensor(f"{name}_half", [DA, CHUNK], F32))
            ps = [first.enter_context(nc.psum_tensor(f"{name}_qk_ps{j}", [DA, CHUNK], F32)) for j in range(3)]
            in_ps = first.enter_context(nc.semaphore(f"{name}_in_ps"))
            copied = first.enter_context(nc.semaphore(f"{name}_qk_copied"))
            block = first.enter_context(nc.Block())
            chunks = N // CHUNK

            @block.tensor
            def _(pe):
                for c in range(chunks):
                    cols = x_t[:, c * CHUNK:(c + 1) * CHUNK]
                    if c:
                        pe.wait_ge(copied, 3 * c)
                    nc.tensor.matmul(ps[0][:, :], w1_t, cols, start=True, stop=True).then_inc(in_ps, 1)
                    nc.tensor.matmul(ps[1][:, :], w3_t, cols, start=True, stop=True).then_inc(in_ps, 1)
                    pe.wait_ge(copied, 3 * c + 1)
                    nc.tensor.matmul(ps[2][:, :], w2_t, half[:, :], start=True, stop=True).then_inc(in_ps, 1)

            @block.scalar
            def _(act):
                for c in range(chunks):
                    cols = slice(c * CHUNK, (c + 1) * CHUNK)
                    for b, out in enumerate((half[:, :], k_t[:, cols], q_t[:, cols])):
                        act.wait_ge(in_ps, 3 * c + b + 1)
                        nc.scalar.copy(out, ps[b][:, :]).then_inc(copied, 1)

        q_tile = [sb(f"q_tile{j}", [DA, P]) for j in range(2)]
        prob = [sb(f"prob{j}", [P, N]) for j in range(2)]
        rest = [sb(f"rest{j}", [P, N + G8]) for j in range(2)]
        junk = sb("junk", [P, N], BF16)
        top8 = [sb(f"top8{j}", [P, G8]) for j in range(2)]
        exp8 = [sb(f"exp8{j}", [P, G8]) for j in range(2)]
        neg_top = [sb(f"neg_top{j}", [P, 1]) for j in range(2)]
        mass = [sb(f"mass{j}", [P, 1]) for j in range(2)]
        floor = [sb(f"floor{j}", [P, 1]) for j in range(2)]
        turned = [sb(f"turned{j}", [P, CHUNK]) for j in range(2)]
        out_tile = [sb(f"out_tile{j}", [P, D]) for j in range(2)]
        out_t = [sb(f"out_t{j}", [P, P]) for j in range(2)]
        goal, lo, hi, mid, above, at_least = (sb(nm, [P, 1]) for nm in ("goal", "lo", "hi", "mid", "above", "at_least"))
        hi2, base, below, den, gain = (sb(nm, [P, 1]) for nm in ("hi2", "base", "below", "den", "gain"))
        ends = sb("ends", [P, 1], I32)
        cand, kept, kept_v, chosen, w8 = (sb(nm, [P, G8]) for nm in ("cand", "kept", "kept_v", "chosen", "w8"))
        sums = sb("sums", [P, G8 + 1])
        flags, flags_t = sb("flags", [P, 32]), sb("flags_t", [P, 32])
        total, total_i = sb("total", [P, 1]), sb("total_i", [P, 1], I32)
        logit_ps = [ctx.enter_context(nc.psum_tensor(f"{name}_logit_ps{j}", [P, 2 * CHUNK], F32)) for j in range(2)]
        turn_ps = [ctx.enter_context(nc.psum_tensor(f"{name}_turn_ps{j}", [P, CHUNK], F32)) for j in range(2)]
        acc_ps = ctx.enter_context(nc.psum_tensor(f"{name}_acc_ps", [P, D + 1], F32))
        post_ps = ctx.enter_context(nc.psum_tensor(f"{name}_post_ps", [P, 2, P], F32))
        q_ready, logit_done, logit_copied, top_ready, exp_ready = (
            sem("q_ready"), sem("logit_done"), sem("logit_copied"), sem("top_ready"), sem("exp_ready"))
        rest_ready, kept_ready, turn_done, turn_copied, group_used = (
            sem("rest_ready"), sem("kept_ready"), sem("turn_done"), sem("turn_copied"), sem("group_used"))
        out_ready, out_turned, out_t_ready, z_done, z_added, x_t_done = (
            sem("out_ready"), sem("out_turned"), sem("out_t_ready"), sem("z_done"), sem("z_added"), sem("x_t_done"))
        summed = sem("summed")
        block = ctx.enter_context(nc.Block())
        PARTS = N // (2 * CHUNK)
        GROUPS = N // CHUNK

        def bodies(eng, body):
            for t in range(4):
                body(t, t % 2)
            with eng.Fori(2, T // 2 - 1) as i:
                for j in range(2):
                    body(2 * i + j, j)
            for t in range(T - 2, T):
                body(t, t % 2)

        def static(t, test):
            return test(t) if isinstance(t, int) else True

        @block.gpsimd
        def _(pool):
            def cut_q(t, j):
                if static(t, lambda t: t >= 2):
                    pool.wait_ge(logit_done, PARTS * (t - 1))
                nc.gpsimd.tensor_copy(q_tile[j][:, :], q_t[:, bass.ds(t * P, P)]).then_inc(q_ready, 1)

            def keep(t, j):
                pool.wait_ge(rest_ready, t + 1)
                nc.gpsimd.tensor_tensor(prob[j][:, :], prob[j][:, :], rest[j][:, 0:N], ALU.subtract
                                        ).then_inc(kept_ready, 1)

            def save_t(t, j):
                pool.wait_ge(out_t_ready, t + 1)
                nc.gpsimd.tensor_copy(x_t[:, bass.ds(t * P, P)], out_t[j][:, :])
                nc.gpsimd.tensor_copy(new_rows[:, bass.ds(t, 1), 0:D].rearrange("p a d -> p (a d)"),
                                      out_tile[j][:, :]).then_inc(x_t_done, 1)

            def body(t, j):
                if static(t, lambda t: t + 1 < T):
                    cut_q(t + 1, 1 - j)
                keep(t, j)
                if static(t, lambda t: t >= 2):
                    save_t(t - 2, j)

            cut_q(0, 0)
            bodies(pool, body)
            save_t(T - 2, 0)
            save_t(T - 1, 1)

        @block.tensor
        def _(pe):
            def logits(t, j):
                pe.wait_ge(q_ready, t + 1)
                for c in range(PARTS):
                    if not (isinstance(t, int) and t == 0 and c < 2):
                        pe.wait_ge(logit_copied, PARTS * t + c - 1)
                    for h in range(2):
                        cols = slice((2 * c + h) * CHUNK, (2 * c + h + 1) * CHUNK)
                        last = nc.tensor.matmul(logit_ps[c % 2][:, h * CHUNK:(h + 1) * CHUNK], q_tile[j][:, :],
                                                k_t[:, cols], start=True, stop=True)
                    last.then_inc(logit_done, 1)

            def apply(t, j):
                pe.wait_ge(kept_ready, t + 1)
                if static(t, lambda t: t >= 1):
                    pe.wait_ge(out_ready, t)

                def turn(g):
                    if not (isinstance(t, int) and t == 0 and g < 2):
                        pe.wait_ge(turn_copied, GROUPS * t + g - 1)
                    for a in range(4):
                        blk = slice((4 * g + a) * P, (4 * g + a + 1) * P)
                        last = nc.tensor.transpose(turn_ps[g % 2][:, a * P:(a + 1) * P], prob[j][:, blk], ident[:, :])
                    last.then_inc(turn_done, 1)

                turn(0)
                for g in range(GROUPS):
                    if g + 1 < GROUPS:
                        turn(g + 1)
                    pe.wait_ge(turn_copied, GROUPS * t + g + 1)
                    for a in range(4):
                        last = nc.tensor.matmul(acc_ps[:, :], turned[g % 2][:, a * P:(a + 1) * P],
                                                rows[:, 4 * g + a, :], start=(g == 0 and a == 0),
                                                stop=(g == GROUPS - 1 and a == 3))
                    last.then_inc(group_used, 1)

            def post(t, j):
                pe.wait_ge(out_ready, t + 1)
                if static(t, lambda t: t >= 1):
                    pe.wait_ge(z_added, t)
                nc.tensor.transpose(post_ps[:, 0, :], out_tile[j][:, :], ident[:, :]).then_inc(out_turned, 1)
                pe.wait_ge(out_t_ready, t + 1)
                nc.tensor.matmul(post_ps[:, 1, :], out_t[j][:, :], u2_t, start=True, stop=True).then_inc(z_done, 1)

            def body(t, j):
                if static(t, lambda t: t >= 1):
                    apply(t - 1, 1 - j)
                if static(t, lambda t: t + 1 < T):
                    logits(t + 1, 1 - j)
                if static(t, lambda t: t >= 2):
                    post(t - 2, j)

            logits(0, 0)
            bodies(pe, body)
            apply(T - 1, 1)
            post(T - 2, 0)
            post(T - 1, 1)

        @block.scalar
        def _(act):
            def take(t, j):
                if static(t, lambda t: t >= 2):
                    act.wait_ge(turn_done, GROUPS * (t - 1))
                for c in range(PARTS):
                    act.wait_ge(logit_done, PARTS * t + c + 1)
                    nc.scalar.copy(prob[j][:, c * 2 * CHUNK:(c + 1) * 2 * CHUNK], logit_ps[c % 2][:, :]
                                   ).then_inc(logit_copied, 1)

            def raise_(t, j):
                act.wait_ge(top_ready, t + 1)
                nc.scalar.activation(exp8[j][:, :], top8[j][:, :], ACT.Exp, bias=neg_top[j][:, :]
                                     ).then_inc(exp_ready, 1)
                nc.scalar.activation(prob[j][:, :], prob[j][:, :], ACT.Exp, bias=neg_top[j][:, :],
                                     accum_out=mass[j][:, :]).then_inc(exp_ready, 1)

            def copy_groups(t):
                for g in range(GROUPS):
                    act.wait_ge(turn_done, GROUPS * t + g + 1)
                    if not (isinstance(t, int) and t == 0 and g < 2):
                        act.wait_ge(group_used, GROUPS * t + g - 1)
                    nc.scalar.copy(turned[g % 2][:, :], turn_ps[g % 2][:, :]).then_inc(turn_copied, 1)

            def copy_t(t, j):
                act.wait_ge(out_turned, t + 1)
                if static(t, lambda t: t >= 2):
                    act.wait_ge(x_t_done, t - 1)
                nc.scalar.copy(out_t[j][:, :], post_ps[:, 0, :]).then_inc(out_t_ready, 1)

            def body(t, j):
                if static(t, lambda t: t >= 1):
                    copy_groups(t - 1)
                if static(t, lambda t: t + 1 < T):
                    take(t + 1, 1 - j)
                if static(t, lambda t: t >= 2):
                    copy_t(t - 2, j)
                if static(t, lambda t: t + 1 < T):
                    raise_(t + 1, 1 - j)

            take(0, 0)
            raise_(0, 0)
            bodies(act, body)
            copy_groups(T - 1)
            copy_t(T - 2, 0)
            copy_t(T - 1, 1)

        @block.vector
        def _(dve):
            V = nc.vector
            go = dve.alloc_register(f"{name}_go")
            n_summed = dve.alloc_register(f"{name}_n_summed")
            dve.reg_mov(n_summed, 0)
            V.memset(flags[:, :], 0.0)
            V.drain()

            def find_top(t, j):
                if isinstance(t, int):
                    dve.wait_ge(logit_copied, PARTS * (t + 1))
                else:
                    wait_apart(dve, logit_copied, PARTS * (t + 1))
                V.max(top8[j][:, :], prob[j][:, :])
                V.drain()
                V.tensor_scalar(neg_top[j][:, :], top8[j][:, 0:1], -1.0, None, ALU.mult).then_inc(top_ready, 1)

            def prefix(values):
                V.tensor_tensor_scan(sums[:, 1:G8 + 1], values, values, sums[:, 0:1], ALU.add, ALU.max)
                V.drain()
                V.tensor_scalar(kept[:, :], sums[:, 0:G8], goal[:, :], None, ALU.is_lt)
                V.drain()

            def bisect(t, j):
                dve.wait_ge(exp_ready, 2 * (t + 1))
                V.tensor_scalar(goal[:, :], mass[j][:, :], TOP_P, None, ALU.mult)
                V.tensor_scalar(lo[:, :], mass[j][:, :], (1.0 - TOP_P) / N * 0.99, None, ALU.mult)
                V.tensor_scalar(floor[j][:, :], mass[j][:, :], 1e-12, None, ALU.mult)
                V.memset(sums[:, 0:1], 0.0)
                V.drain()
                prefix(exp8[j][:, :])
                V.tensor_scalar(w8[:, :], kept[:, :], -BIG, BIG, ALU.mult, ALU.add)
                V.drain()
                V.tensor_tensor(w8[:, :], w8[:, :], exp8[j][:, :], ALU.add)
                V.drain()
                V.tensor_reduce(hi[:, :], w8[:, :], AX.X, ALU.min)
                V.drain()
                for _ in range(halvings):
                    V.tensor_tensor(ends[:, :], lo[:, :].bitcast(I32), hi[:, :].bitcast(I32), ALU.add)
                    V.drain()
                    V.tensor_scalar(mid[:, :].bitcast(I32), ends[:, :], 1, None, ALU.arith_shift_right)
                    V.drain()
                    V.scalar_tensor_tensor(out=junk[:, :], in0=prob[j][:, :], scalar=mid[:, :], in1=prob[j][:, :],
                                           op0=ALU.is_gt, op1=ALU.mult, accum_out=above[:, :])
                    V.drain()
                    V.tensor_tensor(at_least[:, :], above[:, :], goal[:, :], ALU.is_ge)
                    V.drain()
                    V.scalar_tensor_tensor(out=lo[:, :], in0=at_least[:, :], scalar=mid[:, :], in1=lo[:, :],
                                           op0=ALU.mult, op1=ALU.max)
                    V.scalar_tensor_tensor(out=hi2[:, :], in0=at_least[:, :], scalar=BIG, in1=mid[:, :],
                                           op0=ALU.mult, op1=ALU.add)
                    V.drain()
                    V.tensor_tensor(hi[:, :], hi[:, :], hi2[:, :], ALU.min)
                    V.drain()

            def cut(t, j):
                if static(t, lambda t: t >= 2):
                    dve.wait_ge(kept_ready, t - 1)
                V.scalar_tensor_tensor(out=rest[j][:, 0:N], in0=prob[j][:, :], scalar=hi[:, :], in1=prob[j][:, :],
                                       op0=ALU.is_le, op1=ALU.mult, accum_out=below[:, :])
                V.drain()
                V.memset(rest[j][:, N:], -1.0)
                V.tensor_tensor(base[:, :], mass[j][:, :], below[:, :], ALU.subtract)
                V.drain()
                V.tensor_copy(sums[:, 0:1], base[:, :])
                dve.reg_mov(go, 1)
                with dve.While(lambda: dve.snap(go)):
                    V.max(cand[:, :], rest[j][:, :])
                    V.drain()
                    prefix(cand[:, :])
                    V.scalar_tensor_tensor(out=kept[:, :], in0=cand[:, :], scalar=lo[:, :], in1=kept[:, :],
                                           op0=ALU.is_gt, op1=ALU.mult)
                    V.drain()
                    V.tensor_tensor(kept_v[:, :], cand[:, :], kept[:, :], ALU.mult)
                    V.tensor_copy(flags[:, 0:1], kept[:, G8 - 1:G8])
                    V.tensor_scalar(chosen[:, :], kept[:, :], -1.0, None, ALU.add)
                    V.drain()
                    V.tensor_tensor(chosen[:, :], chosen[:, :], kept_v[:, :], ALU.add)
                    V.tensor_reduce(gain[:, :], kept_v[:, :], AX.X, ALU.add)
                    V.drain()
                    V.match_replace(rest[j][:, :], chosen[:, :], rest[j][:, :], 0.0)
                    V.tensor_tensor(sums[:, 0:1], sums[:, 0:1], gain[:, :], ALU.add)
                    V.drain()
                    V.memset(rest[j][:, N:], -1.0)
                    any_row(dve, nc, flags, flags_t, total, total_i, go, summed, n_summed)
                V.drain()
                V.engine_nop().then_inc(rest_ready, 1)

            def normalise(t, j):
                dve.wait_ge(group_used, GROUPS * (t + 1))
                V.tensor_tensor(den[:, :], floor[j][:, :], acc_ps[:, D:D + 1], ALU.max)
                V.drain()
                V.reciprocal(gain[:, :], den[:, :])
                V.drain()
                if static(t, lambda t: t >= 2):
                    dve.wait_ge(x_t_done, t - 1)
                V.tensor_scalar(out_tile[j][:, :], acc_ps[:, 0:D], gain[:, :], None, ALU.mult).then_inc(out_ready, 1)

            def add_z(t):
                dve.wait_ge(z_done, t + 1)
                zt = z[:, bass.ds(t, 1), :].rearrange("p a d -> p (a d)")
                V.tensor_tensor(zt, zt, post_ps[:, 1, :], ALU.add).then_inc(z_added, 1)

            def body(t, j):
                bisect(t, j)
                if static(t, lambda t: t + 1 < T):
                    find_top(t + 1, 1 - j)
                if static(t, lambda t: t >= 2):
                    add_z(t - 2)
                cut(t, j)
                if static(t, lambda t: t >= 1):
                    normalise(t - 1, 1 - j)

            find_top(0, 0)
            bodies(dve, body)
            normalise(T - 1, 1)
            add_z(T - 2)
            add_z(T - 1)
            V.drain()


def program(nc, a, out):
    lists = nc.dram_tensor("lists", [MAX_UNITS, P, LIST], I32, kind="Internal").ap()
    xf1_dram = nc.dram_tensor("xf1_dram", [N, D], F32, kind="Internal").ap()
    hp_dram = nc.dram_tensor("hp_dram", [N, D + H], F32, kind="Internal").ap()
    kv_dram = nc.dram_tensor("kv_dram", [N, 2 * D], F32, kind="Internal").ap()
    support_dram = nc.dram_tensor("support_dram", [N, D], F32, kind="Internal").ap()
    with ExitStack() as ctx:
        def sb(name, shape, dt=F32):
            return ctx.enter_context(nc.sbuf_tensor(name, shape, dt))

        ident = sb("unit_matrix", [P, P])
        x = sb("nodes", [P, T, D])
        z = sb("result", [P, T, D])
        deg = sb("deg", [P, T])
        rdeg = sb("rdeg", [P, T])
        units_i = sb("units_i", [P, 1], I32)

        find_neighbours(nc, a["adj"], a["tile_ids"], lists, deg, units_i)

        with nc.sbuf_tensor("u_rows", [P, 4, D], F32) as u_t, \
             nc.sbuf_tensor("ln_gb", [P, 2, D], F32) as ln_gb:
            copy_dram(nc, "in0", [
                (ident[:, :], a["ident"]), (x[:, :, :], node_view(a["x"])), (z[:, :, :], node_view(a["x"])),
                (u_t[:, 0:2, :], a["U1_t"].rearrange("s i o -> i s o")),
                (u_t[:, 2:4, :], a["U2_t"].rearrange("s i o -> i s o")),
                (ln_gb[:, 0, :], a["ln_g"].partition_broadcast(P)), (ln_gb[:, 1, :], a["ln_b"].partition_broadcast(P)),
            ])
            with nc.sbuf_tensor("xf", [P, T, D], F32) as xf:
                def wide(s):
                    return s[:, :].unsqueeze(2).to_broadcast([P, T, D])

                def add_z(weight):
                    def evict(g, ps):
                        part = z[:, bass.ds(4 * g, 4), :]
                        return nc.vector.tensor_tensor(part, part, ps[:, :, :], ALU.add)
                    return [(weight, evict)]

                with nc.Block() as block:
                    @block.vector
                    def _(dve):
                        V = nc.vector
                        V.tensor_copy(xf[:, :, :], x[:, :, :])
                        V.tensor_scalar(rdeg[:, :], deg[:, :], 1.0, None, ALU.add)
                        V.drain()
                        V.reciprocal(rdeg[:, :], rdeg[:, :])
                        V.drain()
                weighted_sum(nc, "r1", a["x"], lists, units_i, xf)

                def scale_xf():
                    with nc.Block() as block:
                        @block.vector
                        def _(dve):
                            nc.vector.tensor_tensor(xf[:, :, :], xf[:, :, :], wide(rdeg), ALU.mult)
                            nc.vector.drain()

                scale_xf()
                copy_dram(nc, "xf1_out", [(node_view(xf1_dram), xf[:, :, :])])
                project(nc, "u10", xf[:, :, :], ident, add_z(u_t[:, 0, :]))
                weighted_sum(nc, "r2", xf1_dram, lists, units_i, xf)
                scale_xf()
                project(nc, "u11", xf[:, :, :], ident, add_z(u_t[:, 1, :]))
            with nc.sbuf_tensor("w_t", [P, 3, DA], F32) as w_t, nc.sbuf_tensor("nodes_t", [P, N], F32) as x_t, \
                 nc.sbuf_tensor("rows_a", [P, T, D + 1], F32) as rows_a:
                copy_dram(nc, "in1", [
                    (x_t[:, :], a["x_t"]), (rows_a[:, :, 0:D], node_view(a["x"])),
                    (w_t[:, 0, :], a["W1_t"]), (w_t[0:DA, 1, :], a["W2_t"]), (w_t[:, 2, :], a["W3_t"]),
                ])
                weights = (w_t[:, 0, :], w_t[0:DA, 1, :], w_t[:, 2, :])
                with nc.sbuf_tensor("rows_b", [P, T, D + 1], F32) as rows_b:
                    with nc.Block() as block:
                        @block.vector
                        def _(dve):
                            nc.vector.memset(rows_a[:, :, D:D + 1], 1.0)
                            nc.vector.memset(rows_b[:, :, D:D + 1], 1.0)
                            nc.vector.drain()

                    top_p_step(nc, "s0", BISECTIONS[0], weights, u_t[:, 2, :], ident, x_t, rows_a, rows_b, z)
                    top_p_step(nc, "s1", BISECTIONS[1], weights, u_t[:, 3, :], ident, x_t, rows_b, rows_a, z)

            def nothing(dve):
                pass

            def add_layer0(dve):
                V = nc.vector
                V.drain()
                V.tensor_tensor(z[:, :, :], z[:, :, :], ln_gb[:, 0:1, :].to_broadcast([P, T, D]), ALU.mult)
                V.drain()
                V.tensor_tensor(z[:, :, :], z[:, :, :], ln_gb[:, 1:2, :].to_broadcast([P, T, D]), ALU.add)
                V.drain()
                V.tensor_tensor(z[:, :, :], z[:, :, :], x[:, :, :], ALU.add)

            layer_norms(nc, "ln0", z[:, :, :], [nothing, add_layer0])

        acc = x
        denom = sb("denom", [P, T, H])

        def normalise_heads(V):
            V.reciprocal(denom[:, :, :], denom[:, :, :])
            V.drain()
            a4 = acc[:, :, :].rearrange("p t (h f) -> p (t h) f", h=H)
            V.tensor_tensor(a4, a4, denom[:, :, :].rearrange("p t h -> p (t h)").unsqueeze(2).to_broadcast(
                [P, T * H, HD]), ALU.mult)
            V.drain()

        with ExitStack() as l1:
            def sb1(name, shape):
                return l1.enter_context(nc.sbuf_tensor(name, shape, F32))

            w = sb1("l1_w", [P, D])
            a_rows = sb1("l1_a", [P, H, 2 * HD])
            hp = sb1("hp", [P, T, D + H])
            prod = sb1("hp_prod", [P, T, D])
            src = sb1("src", [P, T, H])
            copy_dram(nc, "in2", [(w[:, :], a["L1_W"]),
                                  (a_rows[:, :, :], a["L1_a"].rearrange("h f -> (h f)").partition_broadcast(P).rearrange(
                                      "p (h f) -> p h f", h=H))])
            project(nc, "hp", z[:, :, :], ident, [(w[:, :], lambda g, ps: nc.vector.tensor_copy(
                hp[:, bass.ds(4 * g, 4), 0:D], ps[:, :, :]))])
            with nc.Block() as block:
                @block.vector
                def _(dve):
                    V = nc.vector
                    for half, dst in ((0, src[:, :, :]), (1, hp[:, :, D:D + H])):
                        for h in range(H):
                            V.tensor_tensor(prod[:, :, h * HD:(h + 1) * HD], hp[:, :, h * HD:(h + 1) * HD],
                                            a_rows[:, h:h + 1, half * HD:(half + 1) * HD].to_broadcast([P, T, HD]),
                                            ALU.mult)
                        V.drain()
                        V.tensor_reduce(dst, prod[:, :, :].rearrange("p t (h f) -> p t h f", h=H), AX.X, ALU.add)
                        V.drain()
            copy_dram(nc, "hp_out", [(node_view(hp_dram), hp[:, :, :])])

            def scores1(dve, t, values, got, score, prod_):
                V = nc.vector
                V.tensor_tensor(score[:, :, :], got[:, :, D:D + H],
                                src[:, bass.ds(t, 1), :].to_broadcast([P, G8, H]), ALU.add)
                V.drain()
                V.scalar_tensor_tensor(out=score[:, :, :], in0=score[:, :, :], scalar=0.2, in1=score[:, :, :],
                                       op0=ALU.mult, op1=ALU.max)

            graph_attention(nc, "a1", hp_dram, D + H, 0, scores1, lists, units_i, acc, denom)

        def elu_in_place(name):
            with nc.sbuf_tensor(f"{name}_neg", [P, T, D], F32) as neg, nc.semaphore(f"{name}_n") as neg_ready, \
                 nc.semaphore(f"{name}_e") as neg_raised, nc.Block() as block:
                @block.vector
                def _(dve):
                    V = nc.vector
                    normalise_heads(V)
                    V.tensor_scalar(neg[:, :, :], acc[:, :, :], 0.0, None, ALU.min).then_inc(neg_ready, 1)
                    V.tensor_scalar(acc[:, :, :], acc[:, :, :], 0.0, -1.0, ALU.max, ALU.add)
                    V.drain()
                    V.tensor_tensor(z[:, :, :], z[:, :, :], acc[:, :, :], ALU.add)
                    dve.wait_ge(neg_raised, 1)
                    V.drain()
                    V.tensor_tensor(z[:, :, :], z[:, :, :], neg[:, :, :], ALU.add)
                    V.drain()

                @block.scalar
                def _(act):
                    act.wait_ge(neg_ready, 1)
                    nc.scalar.activation(neg[:, :, :], neg[:, :, :], ACT.Exp).then_inc(neg_raised, 1)

        elu_in_place("elu")
        layer_norms(nc, "ln1", z[:, :, :], [lambda dve: None])

        with ExitStack() as l2:
            def sb2(name, shape):
                return l2.enter_context(nc.sbuf_tensor(name, shape, F32))

            w = sb2("l2_w", [P, 4, D])
            bias = sb2("l2_bias", [P, 4, D])
            g_bias = sb2("g_bias", [P, 1])
            q = sb2("q", [P, T, D])
            copy_dram(nc, "in3", [
                (w[:, 0:3, :], a["Wqkv"].rearrange("i (c o) -> i c o", c=3)), (w[:, 3, :], a["Wout"]),
                (bias[:, 0:3, :], a["bqkv"].partition_broadcast(P).rearrange("p (c o) -> p c o", c=3)),
                (bias[:, 3, :], a["bout"].partition_broadcast(P)), (g_bias[:, :], a["graph_bias"].partition_broadcast(P)),
            ])
            with nc.sbuf_tensor("kv", [P, T, 2 * D], F32) as kv:
                def with_bias(c, dst):
                    return (w[:, c, :], lambda g, ps: nc.vector.tensor_tensor(
                        dst[:, bass.ds(4 * g, 4), :], ps[:, :, :], bias[:, c:c + 1, :].to_broadcast([P, 4, D]), ALU.add))

                project(nc, "qkv", z[:, :, :], ident, [with_bias(0, q[:, :, :]), with_bias(1, kv[:, :, 0:D]),
                                                       with_bias(2, kv[:, :, D:2 * D])])
                copy_dram(nc, "kv_out", [(node_view(kv_dram), kv[:, :, :])])
            edge = sb2("edge", [P, G8])

            def scores2(dve, t, values, got, score, prod):
                V = nc.vector
                V.tensor_tensor(prod[:, :].rearrange("p (k d) -> p k d", k=G8), got[:, :, 0:D],
                                q[:, bass.ds(t, 1), :].to_broadcast([P, G8, D]), ALU.mult)
                V.tensor_scalar(edge[:, :], values, g_bias[:, :], None, ALU.mult)
                V.drain()
                V.tensor_reduce(score[:, :, :], prod[:, :].rearrange("p (k h f) -> p k h f", k=G8, h=H), AX.X, ALU.add)
                V.drain()
                V.scalar_tensor_tensor(out=score[:, :, :], in0=score[:, :, :], scalar=HD ** -0.5,
                                       in1=edge[:, :].unsqueeze(2).to_broadcast([P, G8, H]),
                                       op0=ALU.mult, op1=ALU.add)

            graph_attention(nc, "a2", kv_dram, 2 * D, D, scores2, lists, units_i, acc, denom)
            with nc.Block() as block:
                @block.vector
                def _(dve):
                    normalise_heads(nc.vector)

            def add_out(g, ps):
                part = z[:, bass.ds(4 * g, 4), :]
                return nc.vector.tensor_tensor(part, part, ps[:, :, :], ALU.add)

            project(nc, "wout", acc[:, :, :], ident, [(w[:, 3, :], add_out)])
            layer_norms(nc, "ln2", z[:, :, :], [lambda dve: nc.vector.tensor_tensor(
                z[:, :, :], z[:, :, :], bias[:, 3:4, :].to_broadcast([P, T, D]), ALU.add)])

        with ExitStack() as l3:
            w = l3.enter_context(nc.sbuf_tensor("l3_w", [P, D], F32))
            root = l3.enter_context(nc.sbuf_tensor("root", [P, T], F32))
            rooted = l3.enter_context(nc.semaphore("rooted"))
            copy_dram(nc, "in4", [(w[:, :], a["L3_W_t"])])
            project(nc, "support", z[:, :, :], ident, [(w[:, :], lambda g, ps: nc.vector.tensor_copy(
                acc[:, bass.ds(4 * g, 4), :], ps[:, :, :]))])
            with nc.Block() as block:
                @block.scalar
                def _(act):
                    nc.scalar.activation(root[:, :], rdeg[:, :], ACT.Sqrt).then_inc(rooted, 1)

                @block.vector
                def _(dve):
                    dve.wait_ge(rooted, 1)
                    nc.vector.tensor_tensor(acc[:, :, :], acc[:, :, :],
                                            root[:, :].unsqueeze(2).to_broadcast([P, T, D]), ALU.mult)
                    nc.vector.drain()
            copy_dram(nc, "support_out", [(node_view(support_dram), acc[:, :, :])])
            weighted_sum(nc, "l3", support_dram, lists, units_i, acc)

            def finish(dve):
                V = nc.vector
                V.tensor_tensor(acc[:, :, :], acc[:, :, :], root[:, :].unsqueeze(2).to_broadcast([P, T, D]), ALU.mult)
                V.drain()
                V.scalar_tensor_tensor(out=z[:, :, :], in0=acc[:, :, :], scalar=0.0, in1=z[:, :, :],
                                       op0=ALU.max, op1=ALU.add)

            layer_norms(nc, "ln3", z[:, :, :], [finish])
        copy_dram(nc, "result", [(node_view(out), z[:, :, :])])


def kernel(**inputs):
    import numpy as np
    import concourse.bacc as bacc
    from concourse.bass_utils import run_bass_kernel_spmd

    def arr(v):
        return np.ascontiguousarray(v)

    i = {k: np.asarray(v) for k, v in inputs.items()}
    arrays = {
        "x": arr(i["x"]), "x_t": arr(i["x"].T), "adj": arr(i["adj"]),
        "W1_t": arr(i["L0_gnn_W1"].T), "W2_t": arr(i["L0_gnn_W2"].T), "W3_t": arr(i["L0_gnn_W3"].T),
        "U1_t": arr(i["L0_gnn_U1"].transpose(0, 2, 1)), "U2_t": arr(i["L0_gnn_U2"].transpose(0, 2, 1)),
        "ln_g": arr(i["L0_gnn_ln_g"]), "ln_b": arr(i["L0_gnn_ln_b"]),
        "L1_W": arr(i["L1_gnn_W"]), "L1_a": arr(i["L1_gnn_a"]),
        "Wqkv": arr(i["L2_gnn_Wqkv"]), "bqkv": arr(i["L2_gnn_bqkv"]), "Wout": arr(i["L2_gnn_Wout"]),
        "bout": arr(i["L2_gnn_bout"]), "graph_bias": arr(i["L2_gnn_graph_bias"].reshape(1)),
        "L3_W_t": arr(i["L3_gnn_W"].T),
        "ident": np.eye(P, dtype=np.float32),
        "tile_ids": np.tile(np.arange(T, dtype=np.int32), (P, 1)),
    }
    nc = bacc.Bacc("TRN2", target_bir_lowering=False, num_devices=1)
    aps = {n: nc.dram_tensor(n, v.shape, mybir.dt.from_np(v.dtype), kind="ExternalInput").ap()
           for n, v in arrays.items()}
    out = nc.dram_tensor("out", (N, D), F32, kind="ExternalOutput").ap()
    program(nc, aps, out)
    r = run_bass_kernel_spmd(nc, [arrays], core_ids=[0])
    return r.results[0]["out"]
```

```python
import concourse.bass as bass
from concourse import mybir
from contextlib import ExitStack, contextmanager

F32 = mybir.dt.float32
BF16 = mybir.dt.bfloat16
I32 = mybir.dt.int32
U32 = mybir.dt.uint32
ALU = mybir.AluOpType
ACT = mybir.ActivationFunctionType
AX = mybir.AxisListType

P = 128
N = 4096
T = N // P
D = 128
DA = 64
H = 4
HD = D // H
G8 = 8
TILE_COL = 2 * G8
LIST = TILE_COL + 1
MAX_UNITS = T * (N // G8) + 1
CHUNK = 512
TOP_P = 0.9
BIG = 1e30
SEGMENTS = 32
LISTED = (64, 96)
BISECTIONS = (5, 9)


@contextmanager
def phase_semaphores(nc):
    taken = []

    def new(name):
        taken.append(nc.alloc_semaphore(name))
        return taken[-1]

    yield new
    nc.clear_and_free_semaphores(taken)
    nc.all_engine_barrier()


def node_view(ap):
    return ap.rearrange("(t p) d -> p t d", p=P)


def wait_apart(eng, sem, value):
    value = eng.to_reg(value)
    eng.wait_ge(sem, 1)
    eng.wait_ge(sem, value)


def sum_flags(nc, flags, flags_t, total, total_i):
    nc.vector.transpose(flags_t[:, :], flags[:, :])
    nc.vector.drain()
    nc.vector.tensor_reduce(total[:, :], flags_t[:, :], AX.X, ALU.add)
    nc.vector.drain()
    return nc.vector.tensor_copy(total_i[:, :], total[:, :])


def any_row(dve, nc, flags, flags_t, total, total_i, go, summed, n_summed):
    sum_flags(nc, flags, flags_t, total, total_i).then_inc(summed, 1)
    dve.reg_mov(n_summed, dve.snap(n_summed) + 1)
    wait_apart(dve, summed, dve.snap(n_summed))
    read_flags(dve, total_i, go)


def read_flags(eng, total_i, go):
    parts = [eng.value_load(total_i[32 * q:32 * q + 1, 0:1]) for q in range(4)]
    eng.reg_mov(go, parts[0] + parts[1] + parts[2] + parts[3])


def find_neighbours(nc, adj, adj_tiles, tile_ids, lists, units_i, rows, xf_new, rdeg):
    with ExitStack() as ctx:
        new_sem = ctx.enter_context(phase_semaphores(nc))
        def sb(name, shape, dt=F32):
            return ctx.enter_context(nc.sbuf_tensor(name, shape, dt))

        HALF = T // 2
        adj_rows = [sb(f"adj_rows{j}", [P, N]) for j in range(2)]
        adj_t = [sb(f"nb_adj_t{h}", [P, HALF, P]) for h in range(2)]
        junk = sb("nb_junk", [P, N], BF16)
        found = [sb(f"found{j}", [P, LIST], I32) for j in range(2)]
        ids = sb("ids", [P, T], I32)
        nonzeros = sb("nonzeros", [P, T])
        flags = sb("nb_flags", [P, 32])
        flags_t = sb("nb_flags_t", [P, 32])
        total = sb("nb_total", [P, 1])
        more_i = [sb(f"nb_more{j}", [P, 1], I32) for j in range(2)]
        units = sb("units", [P, 1])
        r_ps = [ctx.enter_context(nc.psum_tensor(f"nb_r_ps{j}", [P, D + 1], F32)) for j in range(2)]
        rows_loaded = [new_sem(f"rows_loaded{j}") for j in range(2)]
        rows_done = new_sem("rows_done")
        counted = new_sem("nb_counted")
        more_ready = new_sem("nb_more_ready")
        found_ready = new_sem("found_ready")
        found_free = [new_sem(f"found_free{j}") for j in range(2)]
        adj_loaded = [new_sem(f"nb_adj_loaded{h}") for h in range(2)]
        adj_used = [new_sem(f"nb_adj_used{h}") for h in range(2)]
        r_taken = new_sem("nb_r_taken")
        block = ctx.enter_context(nc.Block())

        @block.sync
        def _(sp):
            def load(t, j, first):
                if not first:
                    sp.wait_ge(rows_done, t - 1)
                sp.dma_start(adj_rows[j][:, :], adj[bass.ds(t * P, P), :]).then_inc(rows_loaded[j], 16)
                for h in range(2):
                    if not (first and j == 0):
                        sp.wait_ge(adj_used[h], t)
                    sp.dma_start(adj_t[h][:, :, :],
                                 adj_tiles[bass.ds(t, 1), :, h * HALF:(h + 1) * HALF, :].rearrange(
                                     "a p b c -> p (a b) c")).then_inc(adj_loaded[h], 16)

            for j in range(2):
                load(j, j, True)
            with sp.Fori(1, T // 2) as i:
                for j in range(2):
                    load(2 * i + j, j, False)

        @block.scalar
        def _(act):
            def body(t, j, first):
                act.wait_ge(rows_loaded[j], 16 * (t // 2) + 16)
                if not (first and j == 0):
                    act.wait_ge(counted, t)
                nc.scalar.activation(junk[:, :], adj_rows[j][:, :], ACT.Sign,
                                     accum_out=nonzeros[:, bass.ds(t, 1)]).then_inc(counted, 1)
                act.wait_ge(adj_used[1], t + 1)
                nc.scalar.copy(xf_new[:, bass.ds(t, 1), :].rearrange("p a d -> p (a d)"), r_ps[j][:, :]
                               ).then_inc(r_taken, 1)

            for j in range(2):
                body(j, j, True)
            with act.Fori(1, T // 2) as i:
                for j in range(2):
                    body(2 * i + j, j, False)

        @block.tensor
        def _(pe):
            def body(t, j, first):
                if not first:
                    pe.wait_ge(r_taken, t - 1)
                for h in range(2):
                    pe.wait_ge(adj_loaded[h], 16 * (t + 1))
                    for b in range(HALF):
                        last = nc.tensor.matmul(r_ps[j][:, :], adj_t[h][:, b, :], rows[:, h * HALF + b, :],
                                                start=(h == 0 and b == 0), stop=(h == 1 and b == HALF - 1))
                    last.then_inc(adj_used[h], 1)

            for j in range(2):
                body(j, j, True)
            with pe.Fori(1, T // 2) as i:
                for j in range(2):
                    body(2 * i + j, j, False)

        @block.vector
        def _(dve):
            V = nc.vector
            V.memset(flags[:, :], 0.0)
            V.memset(units[:, :], 0.0)
            V.drain()
            go = dve.alloc_register("nb_go")
            n = [dve.alloc_register(f"nb_n{j}") for j in range(2)]
            for j in range(2):
                dve.reg_mov(n[j], 0)
            n_all = dve.alloc_register("nb_n_all")
            dve.reg_mov(n_all, 0)
            for j in range(2):
                dve.wait_ge(found_free[j], 16)
            with dve.Fori(0, T // 2) as i:
                for j in range(2):
                    t = 2 * i + j
                    left = nonzeros[:, bass.ds(t, 1)]
                    values = found[j][:, G8:TILE_COL].bitcast(F32)
                    wait_apart(dve, counted, t + 1)
                    dve.reg_mov(go, 1)
                    with dve.While(lambda: dve.snap(go)):
                        wait_apart(dve, found_free[j], 16 * dve.snap(n[j]) + 16)
                        V.tensor_scalar(flags[:, 0:1], left, float(G8), None, ALU.is_gt)
                        V.tensor_copy(found[j][:, TILE_COL:LIST], ids[:, bass.ds(t, 1)])
                        V.tensor_scalar(units[:, :], units[:, :], 1.0, None, ALU.add)
                        V.drain()
                        sum_flags(nc, flags, flags_t, total, more_i[j]).then_inc(more_ready, 1)
                        dve.reg_mov(n[j], dve.snap(n[j]) + 1)
                        dve.reg_mov(n_all, dve.snap(n_all) + 1)
                        V.max(values, adj_rows[j][:, :])
                        V.drain()
                        V.max_index(found[j][:, 0:G8].bitcast(U32), values, adj_rows[j][:, :])
                        V.tensor_scalar(left, left, -float(G8), None, ALU.add)
                        wait_apart(dve, more_ready, dve.snap(n_all))
                        read_flags(dve, more_i[j], go)
                        V.drain()
                        V.engine_nop().then_inc(found_ready, 1)
                        with dve.If(0 < dve.snap(go)):
                            V.match_replace(adj_rows[j][:, :], values, adj_rows[j][:, :], 0.0)
                            V.drain()
                    V.engine_nop().then_inc(rows_done, 1)
            wait_apart(dve, found_free[0], 16 * dve.snap(n[0]) + 16)
            V.tensor_copy(units_i[:, :], units[:, :])
            V.memset(found[0][:, :], 0)
            V.drain()
            V.engine_nop().then_inc(found_ready, 1)
            dve.wait_ge(r_taken, T)
            V.tensor_tensor(xf_new[:, :, :], xf_new[:, :, :], rows[:, :, :], ALU.add)
            V.drain()
            V.reciprocal(rdeg[:, :], xf_new[:, :, D:D + 1].rearrange("p t a -> p (t a)"))
            V.drain()
            V.tensor_tensor(xf_new[:, :, :], xf_new[:, :, :], rdeg[:, :].unsqueeze(2).to_broadcast([P, T, D + 1]),
                            ALU.mult)
            V.drain()

        @block.gpsimd
        def _(pool):
            n = pool.alloc_register("nb_pool_n")
            go = pool.alloc_register("nb_pool_go")
            pool.reg_mov(n, 0)
            for j in range(2):
                half = slice(j * (T // 2), (j + 1) * (T // 2))
                pool.dma_start(ids[:, half], tile_ids[:, half]).then_inc(found_free[j], 16)

            def store(j):
                pool.dma_start(lists[bass.ds(pool.snap(n), 1), :, :].rearrange("a p c -> p (a c)"),
                               found[j][:, :]).then_inc(found_free[j], 16)
                pool.reg_mov(n, pool.snap(n) + 1)

            stores = [pool.alloc_register(f"nb_stores{j}") for j in range(2)]
            for j in range(2):
                pool.reg_mov(stores[j], 0)
            with pool.Fori(0, T // 2):
                for j in range(2):
                    pool.reg_mov(go, 1)
                    with pool.While(lambda: pool.snap(go)):
                        wait_apart(pool, found_ready, pool.snap(n) + 1)
                        read_flags(pool, more_i[j], go)
                        store(j)
                        pool.reg_mov(stores[j], pool.snap(stores[j]) + 1)
            wait_apart(pool, found_ready, pool.snap(n) + 1)
            store(0)
            wait_apart(pool, found_free[0], 16 * pool.snap(stores[0]) + 32)
            wait_apart(pool, found_free[1], 16 * pool.snap(stores[1]) + 16)


def gather_units(nc, name, table, width, lists, units_i, dve_unit, act_unit=None):
    with ExitStack() as ctx:
        new_sem = ctx.enter_context(phase_semaphores(nc))
        def sb(nm, shape, dt=F32):
            return ctx.enter_context(nc.sbuf_tensor(f"{name}_{nm}", shape, dt))

        def sem(nm):
            return new_sem(f"{name}_{nm}")

        lst = [sb(f"list{j}", [P, LIST], I32) for j in range(2)]
        got = [sb(f"got{j}", [P, G8 * width]) for j in range(2)]
        listed = [sem(f"listed{j}") for j in range(2)]
        gathered = [sem(f"gathered{j}") for j in range(2)]
        unit_used = sem("unit_used")
        block = ctx.enter_context(nc.Block())

        def pairs(eng):
            units = eng.value_load(units_i[0:1, 0:1])
            return (units + 1) // 2

        @block.sync
        def _(sp):
            def load(u, j):
                sp.dma_start(lst[j][:, :], lists[bass.ds(u, 1), :, :].rearrange("a p c -> p (a c)")
                             ).then_inc(listed[j], 16)

            n = pairs(sp)
            for j in range(2):
                load(j, j)
            with sp.Fori(1, n) as i:
                for j in range(2):
                    sp.wait_ge(unit_used, 2 * i + j - 1)
                    load(2 * i + j, j)

        @block.gpsimd
        def _(pool):
            with pool.Fori(0, pairs(pool)) as i:
                for j in range(2):
                    wait_apart(pool, listed[j], 16 * i + 16)
                    for k in range(G8):
                        pool.indirect_dma_start(
                            got[j][:, k * width:(k + 1) * width], None, table,
                            bass.IndirectOffsetOnAxis(ap=lst[j][:, k:k + 1].bitcast(U32), axis=0),
                        ).then_inc(gathered[j], 16)

        @block.vector
        def _(dve):
            with dve.Fori(0, pairs(dve)) as i:
                for j in range(2):
                    wait_apart(dve, listed[j], 16 * i + 16)
                    t = dve.value_load(lst[j][0:1, TILE_COL:LIST], min_val=0, max_val=T - 1)
                    dve.wait_ge(gathered[j], 16 * G8 * (i + 1))
                    dve_unit(dve, 2 * i + j, t, lst[j][:, G8:TILE_COL].bitcast(F32),
                             got[j][:, :].rearrange("p (k w) -> p k w", k=G8))
                    nc.vector.drain()
                    nc.vector.engine_nop().then_inc(unit_used, 1)

        if act_unit is not None:
            @block.scalar
            def _(act):
                with act.Fori(0, pairs(act)) as i:
                    for j in range(2):
                        act_unit(act, 2 * i + j)


def adj_times(nc, name, adj_tiles, src, out):
    with ExitStack() as ctx:
        new_sem = ctx.enter_context(phase_semaphores(nc))
        HALF = T // 2
        adj_t = [ctx.enter_context(nc.sbuf_tensor(f"{name}_adj_t{h}", [P, HALF, P], F32)) for h in range(4)]
        ps = [ctx.enter_context(nc.psum_tensor(f"{name}_ps{j}", [P, D], F32)) for j in range(2)]
        adj_loaded = [new_sem(f"{name}_adj_loaded{h}") for h in range(4)]
        adj_used = [new_sem(f"{name}_adj_used{h}") for h in range(2)]
        taken = new_sem(f"{name}_taken")
        block = ctx.enter_context(nc.Block())

        @block.sync
        def _(sp):
            def load(t, j, first):
                for h in range(2):
                    if not first:
                        sp.wait_ge(adj_used[h], t - 1)
                    sp.dma_start(adj_t[2 * j + h][:, :, :],
                                 adj_tiles[bass.ds(t, 1), :, h * HALF:(h + 1) * HALF, :].rearrange(
                                     "a p b c -> p (a b) c")).then_inc(adj_loaded[2 * j + h], 16)

            for j in range(2):
                load(j, j, True)
            with sp.Fori(1, T // 2) as i:
                for j in range(2):
                    load(2 * i + j, j, False)

        @block.tensor
        def _(pe):
            def body(t, j, first):
                if not first:
                    pe.wait_ge(taken, t - 1)
                for h in range(2):
                    pe.wait_ge(adj_loaded[2 * j + h], 16 * (t // 2) + 16)
                    for b in range(HALF):
                        last = nc.tensor.matmul(ps[j][:, :], adj_t[2 * j + h][:, b, :], src[:, h * HALF + b, :],
                                                start=(h == 0 and b == 0), stop=(h == 1 and b == HALF - 1))
                    last.then_inc(adj_used[h], 1)

            for j in range(2):
                body(j, j, True)
            with pe.Fori(1, T // 2) as i:
                for j in range(2):
                    body(2 * i + j, j, False)

        @block.vector
        def _(dve):
            with dve.Fori(0, T // 2) as i:
                for j in range(2):
                    t = 2 * i + j
                    dve.wait_ge(adj_used[1], t + 1)
                    nc.vector.tensor_tensor(out[:, bass.ds(t, 1), :].rearrange("p a d -> p (a d)"), ps[j][:, :],
                                            src[:, bass.ds(t, 1), :].rearrange("p a d -> p (a d)"), ALU.add
                                            ).then_inc(taken, 1)
            nc.vector.drain()


def graph_attention(nc, name, table, width, value_at, scores, lists, units_i, acc, denom):
    with ExitStack() as ctx:
        new_sem = ctx.enter_context(phase_semaphores(nc))
        def sb(nm, shape, dt=F32):
            return ctx.enter_context(nc.sbuf_tensor(f"{name}_{nm}", shape, dt))

        top = sb("top", [P, T, H])
        new_top = sb("new_top", [P, H])
        score = sb("score", [P, G8, H])
        absent = sb("absent", [P, G8])
        power = sb("power", [P, (1 + G8) * H])
        raised = sb("raised", [P, (1 + G8) * H])
        psum = sb("psum", [P, H])
        prod = sb("prod", [P, G8 * D])
        part = sb("part", [P, D])
        power_ready = new_sem(f"{name}_power_ready")
        raised_ready = new_sem(f"{name}_raised_ready")
        start = new_sem(f"{name}_start")
        with nc.Block() as first:
            @first.vector
            def _(dve):
                nc.vector.memset(top[:, :, :], -BIG)
                nc.vector.memset(denom[:, :, :], 0.0)
                nc.vector.memset(acc[:, :, :], 0.0).then_inc(start, 1)
                dve.wait_ge(start, 1)

        def unit(dve, u, t, values, got):
            V = nc.vector
            topt = top[:, bass.ds(t, 1), :].rearrange("p a h -> p (a h)")
            dent = denom[:, bass.ds(t, 1), :].rearrange("p a h -> p (a h)")
            acct = acc[:, bass.ds(t, 1), :].rearrange("p a d -> p (a d)")
            V.tensor_scalar(absent[:, :], values, 0.0, -1.0, ALU.is_gt, ALU.add)
            scores(dve, t, values, got, score, prod)
            V.drain()
            V.scalar_tensor_tensor(out=score[:, :, :], in0=absent[:, :].unsqueeze(2).to_broadcast([P, G8, H]),
                                   scalar=BIG, in1=score[:, :, :], op0=ALU.mult, op1=ALU.add)
            V.drain()
            V.tensor_reduce(new_top[:, :], score[:, :, :].rearrange("p k h -> p h k"), AX.X, ALU.max)
            V.drain()
            V.tensor_tensor(new_top[:, :], new_top[:, :], topt, ALU.max)
            V.drain()
            V.tensor_tensor(power[:, 0:H], topt, new_top[:, :], ALU.subtract)
            V.tensor_tensor(power[:, H:].rearrange("p (k h) -> p k h", k=G8), score[:, :, :],
                            new_top[:, :].unsqueeze(1).to_broadcast([P, G8, H]), ALU.subtract)
            V.drain()
            V.tensor_copy(topt, new_top[:, :]).then_inc(power_ready, 1)
            dve.wait_ge(raised_ready, u + 1)
            keep = raised[:, 0:H]
            weight = raised[:, H:].rearrange("p (k h) -> p k h", k=G8)
            V.tensor_reduce(psum[:, :], raised[:, H:].rearrange("p (k h) -> p h k", k=G8), AX.X, ALU.add)
            V.tensor_tensor(dent, dent, keep, ALU.mult)
            V.tensor_tensor(prod[:, :].rearrange("p (k h f) -> p k h f", k=G8, h=H),
                            got[:, :, value_at:value_at + D].rearrange("p k (h f) -> p k h f", h=H),
                            weight.unsqueeze(3).to_broadcast([P, G8, H, HD]), ALU.mult)
            V.tensor_tensor(acct.rearrange("p (h f) -> p h f", h=H), acct.rearrange("p (h f) -> p h f", h=H),
                            keep.unsqueeze(2).to_broadcast([P, H, HD]), ALU.mult)
            V.drain()
            V.tensor_tensor(dent, dent, psum[:, :], ALU.add)
            V.tensor_reduce(part[:, :], prod[:, :].rearrange("p (k d) -> p d k", k=G8), AX.X, ALU.add)
            V.drain()
            V.tensor_tensor(acct, acct, part[:, :], ALU.add)

        def act_unit(act, u):
            act.wait_ge(power_ready, u + 1)
            nc.scalar.activation(raised[:, :], power[:, :], ACT.Exp).then_inc(raised_ready, 1)

        gather_units(nc, name, table, width, lists, units_i, unit, act_unit)


def project(nc, name, src, ident, outs):
    groups = T // 4
    nw = len(outs)
    with ExitStack() as ctx:
        new_sem = ctx.enter_context(phase_semaphores(nc))
        def sem(nm):
            return new_sem(f"{name}_{nm}")

        stage = [ctx.enter_context(nc.sbuf_tensor(f"{name}_stage{j}", [P, CHUNK], F32)) for j in range(2)]
        turned = [ctx.enter_context(nc.sbuf_tensor(f"{name}_turned{j}", [P, CHUNK], F32)) for j in range(2)]
        turn_ps = [ctx.enter_context(nc.psum_tensor(f"{name}_turn_ps{j}", [P, CHUNK], F32)) for j in range(2)]
        out_ps = [ctx.enter_context(nc.psum_tensor(f"{name}_out_ps{j}", [P, 4, D], F32)) for j in range(2)]
        staged, turned_ps, turned_sb, multiplied, evicted = (
            sem("staged"), sem("turned_ps"), sem("turned_sb"), sem("multiplied"), sem("evicted"))
        block = ctx.enter_context(nc.Block())

        @block.gpsimd
        def _(pool):
            def group(g, j, first):
                if not first:
                    pool.wait_ge(turned_ps, g - 1)
                nc.gpsimd.tensor_copy(stage[j][:, :].rearrange("p (a d) -> p a d", a=4),
                                      src[:, bass.ds(4 * g, 4), :]).then_inc(staged, 1)

            for j in range(2):
                group(j, j, True)
            with pool.Fori(1, groups // 2) as i:
                for j in range(2):
                    group(2 * i + j, j, False)

        @block.scalar
        def _(act):
            def group(g, j, first):
                act.wait_ge(turned_ps, g + 1)
                if not first:
                    act.wait_ge(multiplied, nw * (g - 1))
                nc.scalar.copy(turned[j][:, :], turn_ps[j][:, :]).then_inc(turned_sb, 1)

            for j in range(2):
                group(j, j, True)
            with act.Fori(1, groups // 2) as i:
                for j in range(2):
                    group(2 * i + j, j, False)

        @block.tensor
        def _(pe):
            def group(g, j, first):
                pe.wait_ge(staged, g + 1)
                if not first:
                    pe.wait_ge(turned_sb, g - 1)
                for a in range(4):
                    last = nc.tensor.transpose(turn_ps[j][:, a * P:(a + 1) * P], stage[j][:, a * D:(a + 1) * D],
                                               ident[:, :])
                last.then_inc(turned_ps, 1)
                pe.wait_ge(turned_sb, g + 1)
                for w, (weight, _) in enumerate(outs):
                    m = nw * g + w
                    b = (nw * j + w) % 2
                    if not first or nw * j + w >= 2:
                        pe.wait_ge(evicted, m - 1)
                    for a in range(4):
                        last = nc.tensor.matmul(out_ps[b][:, a, :], turned[j][:, a * P:(a + 1) * P], weight,
                                                start=True, stop=True)
                    last.then_inc(multiplied, 1)

            for j in range(2):
                group(j, j, True)
            with pe.Fori(1, groups // 2) as i:
                for j in range(2):
                    group(2 * i + j, j, False)

        @block.vector
        def _(dve):
            with dve.Fori(0, groups // 2) as i:
                for j in range(2):
                    g = 2 * i + j
                    for w, (_, evict) in enumerate(outs):
                        dve.wait_ge(multiplied, nw * g + w + 1)
                        evict(g, out_ps[(nw * j + w) % 2]).then_inc(evicted, 1)


def layer_norms(nc, name, x, rounds):
    with ExitStack() as ctx:
        new_sem = ctx.enter_context(phase_semaphores(nc))
        square = ctx.enter_context(nc.sbuf_tensor(f"{name}_square", [P, T, D], F32))
        mean = ctx.enter_context(nc.sbuf_tensor(f"{name}_mean", [P, T], F32))
        var = ctx.enter_context(nc.sbuf_tensor(f"{name}_var", [P, T], F32))
        dev = ctx.enter_context(nc.sbuf_tensor(f"{name}_dev", [P, T], F32))
        var_ready = new_sem(f"{name}_var_ready")
        dev_ready = new_sem(f"{name}_dev_ready")
        block = ctx.enter_context(nc.Block())

        def wide(a):
            return a[:, :].unsqueeze(2).to_broadcast([P, T, D])

        @block.vector
        def _(dve):
            V = nc.vector
            for r, before in enumerate(rounds):
                before(dve)
                V.drain()
                V.tensor_reduce(mean[:, :], x, AX.X, ALU.add)
                V.drain()
                V.tensor_scalar(mean[:, :], mean[:, :], 1.0 / D, None, ALU.mult)
                V.drain()
                V.tensor_tensor(x, x, wide(mean), ALU.subtract)
                V.drain()
                V.tensor_tensor(square[:, :, :], x, x, ALU.mult)
                V.drain()
                V.tensor_reduce(var[:, :], square[:, :, :], AX.X, ALU.add)
                V.drain()
                V.tensor_scalar(var[:, :], var[:, :], 1.0 / D, 1e-5, ALU.mult, ALU.add).then_inc(var_ready, 1)
                dve.wait_ge(dev_ready, r + 1)
                V.reciprocal(var[:, :], dev[:, :])
                V.drain()
                V.tensor_tensor(x, x, wide(var), ALU.mult)
            V.drain()

        @block.scalar
        def _(act):
            for r in range(len(rounds)):
                act.wait_ge(var_ready, r + 1)
                nc.scalar.activation(dev[:, :], var[:, :], ACT.Sqrt).then_inc(dev_ready, 1)


def copy_dram(nc, name, pairs):
    with phase_semaphores(nc) as new_sem, nc.Block() as block:
        moved = new_sem(f"{name}_moved")

        @block.sync
        def _(sp):
            for out, in_ in pairs:
                sp.dma_start(out, in_).then_inc(moved, 16)
            sp.wait_ge(moved, 16 * len(pairs))


def attention_inputs(nc, name, rows, ident, weights, q_t, k_t, z, u2_t):
    w1_t, w2_t, w3_t = weights
    groups = T // 4
    with ExitStack() as ctx:
        new_sem = ctx.enter_context(phase_semaphores(nc))
        def sem(nm):
            return new_sem(f"{name}_{nm}")

        turned = [ctx.enter_context(nc.sbuf_tensor(f"{name}_turned{j}", [P, CHUNK], F32)) for j in range(2)]
        half = ctx.enter_context(nc.sbuf_tensor(f"{name}_half", [DA, CHUNK], F32))
        turn_ps = [ctx.enter_context(nc.psum_tensor(f"{name}_turn_ps{j}", [P, CHUNK], F32)) for j in range(2)]
        half_ps, q_ps, k_ps = (ctx.enter_context(nc.psum_tensor(f"{name}_{nm}", [DA, CHUNK], F32))
                               for nm in ("half_ps", "q_ps", "k_ps"))
        z_ps = ctx.enter_context(nc.psum_tensor(f"{name}_z_ps", [P, 4, D], F32))
        turn_done, turned_sb, half_done, half_sb, q_done, k_done, z_done, q_sb, k_sb, z_added = (
            sem(nm) for nm in ("turn_done", "turned_sb", "half_done", "half_sb", "q_done", "k_done", "z_done",
                               "q_sb", "k_sb", "z_added"))
        block = ctx.enter_context(nc.Block())

        @block.tensor
        def _(pe):
            def turn(g):
                if g >= 2:
                    pe.wait_ge(turned_sb, g - 1)
                for a in range(4):
                    last = nc.tensor.transpose(turn_ps[g % 2][:, a * P:(a + 1) * P], rows[:, 4 * g + a, 0:D],
                                               ident[:, :])
                last.then_inc(turn_done, 1)

            turn(0)
            for g in range(groups):
                pe.wait_ge(turned_sb, g + 1)
                if g:
                    pe.wait_ge(half_sb, g)
                    pe.wait_ge(k_sb, g)
                nc.tensor.matmul(half_ps[:, :], w1_t, turned[g % 2][:, :], start=True, stop=True
                                 ).then_inc(half_done, 1)
                nc.tensor.matmul(k_ps[:, :], w3_t, turned[g % 2][:, :], start=True, stop=True).then_inc(k_done, 1)
                if g + 1 < groups:
                    turn(g + 1)
                if u2_t is not None:
                    if g:
                        pe.wait_ge(z_added, g)
                    for a in range(4):
                        last = nc.tensor.matmul(z_ps[:, a, :], turned[g % 2][:, a * P:(a + 1) * P], u2_t,
                                                start=True, stop=True)
                    last.then_inc(z_done, 1)
                pe.wait_ge(half_sb, g + 1)
                if g:
                    pe.wait_ge(q_sb, g)
                nc.tensor.matmul(q_ps[:, :], w2_t, half[:, :], start=True, stop=True).then_inc(q_done, 1)

        @block.scalar
        def _(act):
            for g in range(groups):
                act.wait_ge(turn_done, g + 1)
                if g >= 2:
                    act.wait_ge(half_done, g - 1)
                    act.wait_ge(k_done, g - 1)
                    if u2_t is not None:
                        act.wait_ge(z_done, g - 1)
                nc.scalar.copy(turned[g % 2][:, :], turn_ps[g % 2][:, :]).then_inc(turned_sb, 1)
                act.wait_ge(half_done, g + 1)
                if g:
                    act.wait_ge(q_done, g)
                nc.scalar.copy(half[:, :], half_ps[:, :]).then_inc(half_sb, 1)

        @block.vector
        def _(dve):
            for g in range(groups):
                cols = slice(g * CHUNK, (g + 1) * CHUNK)
                dve.wait_ge(k_done, g + 1)
                nc.vector.tensor_copy(k_t[:, cols], k_ps[:, :]).then_inc(k_sb, 1)
                if u2_t is not None:
                    dve.wait_ge(z_done, g + 1)
                    nc.vector.tensor_tensor(z[:, 4 * g:4 * g + 4, :], z[:, 4 * g:4 * g + 4, :], z_ps[:, :, :],
                                            ALU.add).then_inc(z_added, 1)
                dve.wait_ge(q_done, g + 1)
                nc.vector.tensor_copy(q_t[:, cols], q_ps[:, :]).then_inc(q_sb, 1)


def top_p_rows(nc, name, listed, ident, q_dram, k_t, rows, xa_out, unresolved, beside):
    adj_tiles, xf, xf_new, rdeg = beside or (None,) * 4
    with ExitStack() as ctx:
        new_sem = ctx.enter_context(phase_semaphores(nc))
        def sb(nm, shape, dt=F32):
            return ctx.enter_context(nc.sbuf_tensor(f"{name}_{nm}", shape, dt))

        def sem(nm):
            return new_sem(f"{name}_{nm}")

        PARTS = N // (2 * CHUNK)
        GROUPS = N // CHUNK
        HALF = T // 2

        q_tile = [sb(f"q_tile{j}", [DA, P]) for j in range(2)]
        logit = [sb(f"logit{j}", [P, N + G8]) for j in range(2)]
        prob = [sb(f"prob{j}", [P, N]) for j in range(2)]
        adj_t = [sb(f"adj_t{h}", [P, HALF, P]) for h in range(2)] if beside else None
        cand = sb("cand", [P, SEGMENTS * G8])
        ordered = sb("ordered", [P, listed])
        raised = sb("raised", [P, listed])
        sums = sb("sums", [P, listed + 1])
        level = sb("level", [P, listed])
        dropped = sb("dropped", [P, listed])
        limit = sb("limit", [P, 1])
        split = sb("split", [P, 1])
        tied = sb("tied", [P, listed])
        neg_top = sb("neg_top", [P, 1])
        mass = [sb(f"mass{j}", [P, 1]) for j in range(2)]
        goal, den, gain = (sb(nm, [P, 1]) for nm in ("goal", "den", "gain"))
        eighth, least, ties, last_level = (sb(nm, [P, T]) for nm in ("eighth", "least", "ties", "last_level"))
        count8 = sb("count8", [P, G8])
        chosen = sb("chosen", [P, G8])
        turned = [sb(f"turned{j}", [P, CHUNK]) for j in range(2)]
        out_tile = [sb(f"out_tile{j}", [P, D]) for j in range(2)]
        r_sum = sb("r_sum", [P, D])
        logit_ps = [ctx.enter_context(nc.psum_tensor(f"{name}_logit_ps{j}", [P, 2 * CHUNK], F32)) for j in range(2)]
        turn_ps = [ctx.enter_context(nc.psum_tensor(f"{name}_turn_ps{j}", [P, CHUNK], F32)) for j in range(2)]
        acc_ps = ctx.enter_context(nc.psum_tensor(f"{name}_acc_ps", [P, D + 1], F32))
        r_ps = ctx.enter_context(nc.psum_tensor(f"{name}_r_ps", [P, D], F32))
        logit_done, logit_copied, top_ready, order_ready, exp_ready, kept_ready = (
            sem(nm) for nm in ("logit_done", "logit_copied", "top_ready", "order_ready", "exp_ready", "kept_ready"))
        turn_done, turn_copied, group_used, out_ready, r_taken = (
            sem(nm) for nm in ("turn_done", "turn_copied", "group_used", "out_ready", "r_taken"))
        q_loaded = [sem(f"q_loaded{j}") for j in range(2)]
        adj_loaded = [sem(f"adj_loaded{h}") for h in range(2)]
        adj_used = [sem(f"adj_used{h}") for h in range(2)]
        stored = [sem(f"stored{j}") for j in range(2)]
        block = ctx.enter_context(nc.Block())

        def bodies(eng, body):
            for t in range(2):
                body(t, t % 2)
            with eng.Fori(1, T // 2 - 1) as i:
                for j in range(2):
                    body(2 * i + j, j)
            for t in range(T - 2, T):
                body(t, t % 2)

        def static(t, test):
            return test(t) if isinstance(t, int) else True

        def wait(eng, t, sem_, value):
            if isinstance(t, int):
                eng.wait_ge(sem_, value)
            else:
                wait_apart(eng, sem_, value)

        @block.sync
        def _(sp):
            def load_q(t, j):
                if static(t, lambda t: t >= 2):
                    sp.wait_ge(logit_done, PARTS * (t - 1))
                sp.dma_start(q_tile[j][:, :], q_dram[:, bass.ds(t * P, P)]).then_inc(q_loaded[j], 16)

            def body(t, j):
                for h in range(2 if beside else 0):
                    if static(t, lambda t: t >= 1):
                        sp.wait_ge(adj_used[h], t)
                    sp.dma_start(adj_t[h][:, :, :],
                                 adj_tiles[bass.ds(t, 1), :, h * HALF:(h + 1) * HALF, :].rearrange(
                                     "a p b c -> p (a b) c")).then_inc(adj_loaded[h], 16)
                if static(t, lambda t: t + 2 < T):
                    load_q(t + 2, j)

            for j in range(2):
                load_q(j, j)
            bodies(sp, body)

        @block.gpsimd
        def _(pool):
            def body(t, j):
                pool.wait_ge(out_ready, t + 1)
                pool.dma_start(xa_out[bass.ds(t * P, P), :], out_tile[j][:, :]).then_inc(stored[j], 16)

            bodies(pool, body)
            for j in range(2):
                pool.wait_ge(stored[j], 16 * (T // 2))

        @block.scalar
        def _(act):
            def take(t, j):
                for c in range(PARTS):
                    act.wait_ge(logit_done, PARTS * t + c + 1)
                    if c == 0 and static(t, lambda t: t >= 2):
                        act.wait_ge(kept_ready, t - 1)
                    nc.scalar.copy(logit[j][:, c * 2 * CHUNK:(c + 1) * 2 * CHUNK], logit_ps[c % 2][:, :]
                                   ).then_inc(logit_copied, 1)

            def copy_groups(t):
                for g in range(GROUPS):
                    act.wait_ge(turn_done, GROUPS * t + g + 1)
                    if static(t, lambda t: t >= 1) or g >= 2:
                        act.wait_ge(group_used, GROUPS * t + g - 1)
                    nc.scalar.copy(turned[g % 2][:, :], turn_ps[g % 2][:, :]).then_inc(turn_copied, 1)

            def body(t, j):
                if static(t, lambda t: t >= 1):
                    copy_groups(t - 1)
                act.wait_ge(top_ready, t + 1)
                if static(t, lambda t: t >= 2):
                    act.wait_ge(out_ready, t - 1)
                nc.scalar.activation(prob[j][:, :], logit[j][:, 0:N], ACT.Exp, bias=neg_top[:, :],
                                     accum_out=mass[j][:, :]).then_inc(exp_ready, 1)
                act.wait_ge(order_ready, t + 1)
                nc.scalar.activation(raised[:, :], ordered[:, :], ACT.Exp, bias=neg_top[:, :]
                                     ).then_inc(exp_ready, 1)
                if static(t, lambda t: t + 1 < T):
                    take(t + 1, 1 - j)

            take(0, 0)
            bodies(act, body)
            copy_groups(T - 1)

        @block.tensor
        def _(pe):
            def logits(t, j):
                pe.wait_ge(q_loaded[j], 16 * (t // 2) + 16)
                for c in range(PARTS):
                    if static(t, lambda t: t >= 1) or c >= 2:
                        pe.wait_ge(logit_copied, PARTS * t + c - 1)
                    for h in range(2):
                        cols = slice((2 * c + h) * CHUNK, (2 * c + h + 1) * CHUNK)
                        last = nc.tensor.matmul(logit_ps[c % 2][:, h * CHUNK:(h + 1) * CHUNK], q_tile[j][:, :],
                                                k_t[:, cols], start=True, stop=True)
                    last.then_inc(logit_done, 1)

            def apply(t, j):
                pe.wait_ge(kept_ready, t + 1)

                def turn(g):
                    if static(t, lambda t: t >= 1) or g >= 2:
                        pe.wait_ge(turn_copied, GROUPS * t + g - 1)
                    for a in range(4):
                        blk = slice((4 * g + a) * P, (4 * g + a + 1) * P)
                        last = nc.tensor.transpose(turn_ps[g % 2][:, a * P:(a + 1) * P], prob[j][:, blk], ident[:, :])
                    last.then_inc(turn_done, 1)

                turn(0)
                if static(t, lambda t: t >= 1):
                    pe.wait_ge(out_ready, t)
                for g in range(GROUPS):
                    if g + 1 < GROUPS:
                        turn(g + 1)
                    pe.wait_ge(turn_copied, GROUPS * t + g + 1)
                    for a in range(4):
                        last = nc.tensor.matmul(acc_ps[:, :], turned[g % 2][:, a * P:(a + 1) * P],
                                                rows[:, 4 * g + a, :], start=(g == 0 and a == 0),
                                                stop=(g == GROUPS - 1 and a == 3))
                    last.then_inc(group_used, 1)

            def add_neighbours(t):
                if static(t, lambda t: t >= 1):
                    pe.wait_ge(r_taken, t)
                for h in range(2):
                    pe.wait_ge(adj_loaded[h], 16 * (t + 1))
                    for b in range(HALF):
                        last = nc.tensor.matmul(r_ps[:, :], adj_t[h][:, b, :], xf[:, h * HALF + b, 0:D],
                                                start=(h == 0 and b == 0), stop=(h == 1 and b == HALF - 1))
                    last.then_inc(adj_used[h], 1)

            def body(t, j):
                if static(t, lambda t: t >= 1):
                    apply(t - 1, 1 - j)
                if static(t, lambda t: t + 1 < T):
                    logits(t + 1, 1 - j)
                if beside:
                    add_neighbours(t)

            logits(0, 0)
            bodies(pe, body)
            apply(T - 1, 1)

        @block.vector
        def _(dve):
            V = nc.vector
            V.memset(sums[:, 0:1], 0.0)
            for j in range(2):
                V.memset(logit[j][:, N:], -BIG)
            for k in range(G8):
                V.memset(count8[:, k:k + 1], float(k))
            V.drain()

            def find(t, j):
                wait(dve, t, logit_copied, PARTS * (t + 1))
                for s in range(SEGMENTS):
                    V.max(cand[:, s * G8:(s + 1) * G8], logit[j][:, s * (N // SEGMENTS):(s + 1) * (N // SEGMENTS)])
                V.drain()
                V.tensor_reduce(eighth[:, bass.ds(t, 1)],
                                cand[:, :].rearrange("p (s k) -> p k s", k=G8)[:, G8 - 1:G8, :], AX.X, ALU.max)
                for r in range(0, listed, G8):
                    V.max(ordered[:, r:r + G8], cand[:, :])
                    V.drain()
                    if r == 0:
                        V.tensor_scalar(neg_top[:, :], ordered[:, 0:1], -1.0, None, ALU.mult).then_inc(top_ready, 1)
                    if r + G8 < listed:
                        V.match_replace(cand[:, :], ordered[:, r:r + G8], cand[:, :], -BIG)
                        V.drain()
                V.engine_nop().then_inc(order_ready, 1)

            def keep(t, j):
                low = least[:, bass.ds(t, 1)]
                tie = ties[:, bass.ds(t, 1)]
                dve.wait_ge(exp_ready, 2 * (t + 1))
                V.tensor_scalar(goal[:, :], mass[j][:, :], TOP_P, None, ALU.mult)
                V.tensor_tensor_scan(sums[:, 1:], raised[:, :], raised[:, :], sums[:, 0:1], ALU.add, ALU.max)
                V.drain()
                V.tensor_scalar(level[:, :], sums[:, 0:listed], goal[:, :], BIG, ALU.is_ge, ALU.mult)
                V.tensor_scalar(dropped[:, :], sums[:, 0:listed], goal[:, :], -BIG, ALU.is_lt, ALU.mult)
                V.drain()
                V.tensor_tensor(level[:, :], level[:, :], ordered[:, :], ALU.add)
                V.tensor_tensor(dropped[:, :], dropped[:, :], ordered[:, :], ALU.add)
                V.drain()
                V.tensor_reduce(low, level[:, :], AX.X, ALU.min)
                V.tensor_reduce(limit[:, :], dropped[:, :], AX.X, ALU.max)
                V.tensor_copy(last_level[:, bass.ds(t, 1)], level[:, listed - 1:listed])
                V.drain()
                V.tensor_scalar(tied[:, :], level[:, :], low, None, ALU.is_equal)
                V.tensor_tensor(split[:, :], limit[:, :], low, ALU.is_equal)
                V.drain()
                V.tensor_reduce(tie, tied[:, :], AX.X, ALU.add)
                V.drain()
                V.tensor_tensor(tie, tie, split[:, :], ALU.mult)
                V.drain()
                V.tensor_scalar(chosen[:, :], count8[:, :], tie, -BIG, ALU.is_ge, ALU.mult)
                V.drain()
                V.tensor_scalar(chosen[:, :], chosen[:, :], low, None, ALU.add)
                V.drain()
                V.match_replace(logit[j][:, :], chosen[:, :], logit[j][:, :], BIG)
                V.drain()
                V.scalar_tensor_tensor(out=prob[j][:, :], in0=logit[j][:, 0:N], scalar=limit[:, :], in1=prob[j][:, :],
                                       op0=ALU.is_gt, op1=ALU.mult).then_inc(kept_ready, 1)
                V.memset(logit[j][:, N:], -BIG)

            def normalise(t, j):
                dve.wait_ge(group_used, GROUPS * (t + 1))
                V.tensor_scalar(den[:, :], mass[j][:, :], 1e-12, None, ALU.mult)
                V.drain()
                V.tensor_tensor(den[:, :], den[:, :], acc_ps[:, D:D + 1], ALU.max)
                V.drain()
                V.reciprocal(gain[:, :], den[:, :])
                V.drain()
                if static(t, lambda t: t >= 2):
                    dve.wait_ge(stored[j], 16 * (t // 2))
                V.tensor_scalar(out_tile[j][:, :], acc_ps[:, 0:D], gain[:, :], None, ALU.mult).then_inc(out_ready, 1)

            def take_r(t):
                dve.wait_ge(adj_used[1], t + 1)
                V.tensor_tensor(r_sum[:, :], r_ps[:, :], xf[:, bass.ds(t, 1), 0:D].rearrange("p a d -> p (a d)"),
                                ALU.add).then_inc(r_taken, 1)
                V.drain()
                V.tensor_scalar(xf_new[:, bass.ds(t, 1), :].rearrange("p a d -> p (a d)"), r_sum[:, :],
                                rdeg[:, bass.ds(t, 1)], None, ALU.mult)

            def body(t, j):
                find(t, j)
                if static(t, lambda t: t >= 1):
                    normalise(t - 1, 1 - j)
                    if beside:
                        take_r(t - 1)
                keep(t, j)

            bodies(dve, body)
            normalise(T - 1, 1)
            if beside:
                take_r(T - 1)
            V.tensor_tensor(unresolved[:, :], eighth[:, :], least[:, :], ALU.is_ge)
            V.tensor_scalar(last_level[:, :], last_level[:, :], 0.5 * BIG, None, ALU.is_lt)
            V.tensor_scalar(ties[:, :], ties[:, :], float(G8), None, ALU.is_gt)
            V.drain()
            V.tensor_tensor(unresolved[:, :], unresolved[:, :], last_level[:, :], ALU.max)
            V.drain()
            V.tensor_tensor(unresolved[:, :], unresolved[:, :], ties[:, :], ALU.max)
            V.drain()


def unresolved_first(nc, name, unresolved, consts, order, count_i):
    below_ones, node_f, node_i = consts
    with ExitStack() as ctx:
        new_sem = ctx.enter_context(phase_semaphores(nc))
        def sb(nm, shape, dt=F32):
            return ctx.enter_context(nc.sbuf_tensor(f"{name}_{nm}", shape, dt))

        def sem(nm):
            return new_sem(f"{name}_{nm}")

        before, totals, offsets, other = (sb(nm, [P, T]) for nm in ("before", "totals", "offsets", "other"))
        place = sb("place", [P, T], I32)
        zeros = sb("zeros", [P, 2], I32)
        ps = ctx.enter_context(nc.psum_tensor(f"{name}_ps", [P, 2, T], F32))
        counted, placed, scattered, cleared = sem("counted"), sem("placed"), sem("scattered"), sem("cleared")
        block = ctx.enter_context(nc.Block())

        @block.tensor
        def _(pe):
            for h in range(2):
                last = nc.tensor.matmul(ps[:, h, :], below_ones[:, h, :], unresolved[:, :], start=True, stop=True)
            last.then_inc(counted, 1)

        @block.vector
        def _(dve):
            V = nc.vector
            V.memset(zeros[:, :], 0).then_inc(cleared, 1)
            dve.wait_ge(counted, 1)
            V.tensor_copy(before[:, :], ps[:, 0, :])
            V.tensor_copy(totals[:, :], ps[:, 1, :])
            V.drain()
            V.tensor_tensor_scan(offsets[:, :], totals[:, :], totals[:, :], 0.0, ALU.add, ALU.max)
            V.drain()
            V.tensor_copy(count_i[:, :], offsets[:, T - 1:T])
            V.tensor_tensor(other[:, :], offsets[:, :], totals[:, :], ALU.subtract)
            V.drain()
            V.tensor_tensor(before[:, :], before[:, :], other[:, :], ALU.add)
            V.drain()
            V.tensor_tensor(other[:, :], node_f, before[:, :], ALU.subtract)
            V.drain()
            V.tensor_scalar(other[:, :], other[:, :], offsets[:, T - 1:T], None, ALU.add)
            V.drain()
            V.tensor_tensor(before[:, :], before[:, :], other[:, :], ALU.subtract)
            V.drain()
            V.tensor_tensor(before[:, :], before[:, :], unresolved[:, :], ALU.mult)
            V.drain()
            V.tensor_tensor(before[:, :], before[:, :], other[:, :], ALU.add)
            V.drain()
            V.tensor_copy(place[:, :], before[:, :]).then_inc(placed, 1)

        @block.gpsimd
        def _(pool):
            pool.wait_ge(cleared, 1)
            pool.dma_start(order[N:N + 2 * P, :].rearrange("(p a) b -> p (a b)", p=P), zeros[:, :]
                           ).then_inc(scattered, 16)
            pool.wait_ge(placed, 1)
            with pool.If(0 < pool.value_load(count_i[0:1, 0:1], min_val=0, max_val=N)):
                for t in range(T):
                    pool.indirect_dma_start(
                        order, bass.IndirectOffsetOnAxis(ap=place[:, t:t + 1].bitcast(U32), axis=0),
                        node_i[:, t:t + 1], None).then_inc(scattered, 16)
                pool.wait_ge(scattered, 16 * (T + 1))
            pool.wait_ge(scattered, 16)


def full_rows(nc, name, halvings, weights, ident, k_t, rows, table, order, count_i, xa_out):
    w1_t, w2_t = weights
    with ExitStack() as ctx:
        new_sem = ctx.enter_context(phase_semaphores(nc))
        def sb(nm, shape, dt=F32):
            return ctx.enter_context(nc.sbuf_tensor(f"{name}_{nm}", shape, dt))

        def sem(nm):
            return new_sem(f"{name}_{nm}")

        ids = [sb(f"ids{j}", [P, 1], I32) for j in range(2)]
        out_ids = [sb(f"out_ids{j}", [P, 1], I32) for j in range(2)]
        own = [sb(f"own{j}", [P, D]) for j in range(2)]
        own_t = sb("own_t", [D, P])
        half = sb("half", [DA, P])
        q_tile = [sb(f"q_tile{j}", [DA, P]) for j in range(2)]
        logit = sb("logit", [P, N])
        prob = [sb(f"prob{j}", [P, N]) for j in range(2)]
        rest = sb("rest", [P, N + G8])
        junk = sb("junk", [P, N], BF16)
        top8 = [sb(f"top8{j}", [P, G8]) for j in range(2)]
        exp8 = [sb(f"exp8{j}", [P, G8]) for j in range(2)]
        neg_top = [sb(f"neg_top{j}", [P, 1]) for j in range(2)]
        mass = [sb(f"mass{j}", [P, 1]) for j in range(2)]
        floor = [sb(f"floor{j}", [P, 1]) for j in range(2)]
        turned = [sb(f"turned{j}", [P, CHUNK]) for j in range(2)]
        out_tile = [sb(f"out_tile{j}", [P, D]) for j in range(2)]
        goal, lo, hi, mid, above, at_least = (sb(nm, [P, 1]) for nm in ("goal", "lo", "hi", "mid", "above", "at_least"))
        hi2, base, below, den, gain = (sb(nm, [P, 1]) for nm in ("hi2", "base", "below", "den", "gain"))
        ends = sb("ends", [P, 1], I32)
        cand, kept, kept_v, chosen, w8 = (sb(nm, [P, G8]) for nm in ("cand", "kept", "kept_v", "chosen", "w8"))
        sums = sb("sums", [P, G8 + 1])
        flags, flags_t = sb("flags", [P, 32]), sb("flags_t", [P, 32])
        total, total_i = sb("total", [P, 1]), sb("total_i", [P, 1], I32)
        logit_ps = [ctx.enter_context(nc.psum_tensor(f"{name}_logit_ps{j}", [P, 2 * CHUNK], F32)) for j in range(2)]
        turn_ps = [ctx.enter_context(nc.psum_tensor(f"{name}_turn_ps{j}", [P, CHUNK], F32)) for j in range(2)]
        acc_ps = ctx.enter_context(nc.psum_tensor(f"{name}_acc_ps", [P, D + 1], F32))
        q_ps = ctx.enter_context(nc.psum_tensor(f"{name}_q_ps", [P, 3, P], F32))
        ids_loaded = [sem(f"ids_loaded{j}") for j in range(2)]
        out_ids_loaded = [sem(f"out_ids_loaded{j}") for j in range(2)]
        own_loaded = [sem(f"own_loaded{j}") for j in range(2)]
        scattered = [sem(f"scattered{j}") for j in range(2)]
        own_turned, own_t_ready, half_done, half_ready, q_done, q_ready = (
            sem(nm) for nm in ("own_turned", "own_t_ready", "half_done", "half_ready", "q_done", "q_ready"))
        logit_done, logit_copied, top_ready, exp_ready, rest_ready, kept_ready = (
            sem(nm) for nm in ("logit_done", "logit_copied", "top_ready", "exp_ready", "rest_ready", "kept_ready"))
        turn_done, turn_copied, group_used, out_ready, out_free, summed = (
            sem(nm) for nm in ("turn_done", "turn_copied", "group_used", "out_ready", "out_free", "summed"))
        acc_free = sem("acc_free")
        block = ctx.enter_context(nc.Block())
        PARTS = N // (2 * CHUNK)
        GROUPS = N // CHUNK

        def if_any(engine_program):
            def run(eng):
                with eng.If(0 < eng.value_load(count_i[0:1, 0:1], min_val=0, max_val=N)):
                    engine_program(eng)
            return run

        def tile_loop(eng, body):
            pairs = (eng.value_load(count_i[0:1, 0:1], min_val=0, max_val=N) + (2 * P - 1)) // (2 * P)
            with eng.Fori(0, pairs) as i:
                body(2 * i, 0, lambda step: step(2 * i + 1, 1))

                def more(step):
                    with eng.If(i + 1 < pairs):
                        step(2 * i + 2, 0)

                body(2 * i + 1, 1, more)

        @block.sync
        @if_any
        def _(sp):
            def load_ids(t, j):
                sp.dma_start(ids[j][:, :], order[bass.ds(t * P, P), :]).then_inc(ids_loaded[j], 16)

            def body(t, j, more):
                i = t // 2
                sp.wait_ge(own_loaded[j], 16 * i + 16)
                load_ids(t + 2, j)
                sp.wait_ge(out_free, t + 1)
                sp.dma_start(out_ids[j][:, :], order[bass.ds(t * P, P), :]).then_inc(out_ids_loaded[j], 16)

            for j in range(2):
                load_ids(j, j)
            tile_loop(sp, body)

        @block.gpsimd
        @if_any
        def _(pool):
            def gather(t, j, i):
                if isinstance(t, int):
                    pool.wait_ge(ids_loaded[j], 16 * (i + 1))
                else:
                    wait_apart(pool, ids_loaded[j], 16 * (i + 1))
                pool.indirect_dma_start(own[j][:, :], None, table,
                                        bass.IndirectOffsetOnAxis(ap=ids[j][:, :].bitcast(U32), axis=0)
                                        ).then_inc(own_loaded[j], 16)

            def body(t, j, more):
                i = t // 2
                pool.wait_ge(rest_ready, t + 1)
                nc.gpsimd.tensor_tensor(prob[j][:, :], prob[j][:, :], rest[:, 0:N], ALU.subtract
                                        ).then_inc(kept_ready, 1)
                wait_apart(pool, own_turned, t + 1)
                gather(t + 2, j, i + 1)
                wait_apart(pool, out_ids_loaded[j], 16 * i + 16)
                wait_apart(pool, out_ready, t + 1)
                pool.indirect_dma_start(xa_out, bass.IndirectOffsetOnAxis(ap=out_ids[j][:, :].bitcast(U32), axis=0),
                                        out_tile[j][:, :], None).then_inc(scattered[j], 16)
                wait_apart(pool, scattered[j], 16 * i + 16)
                nc.gpsimd.engine_nop().then_inc(out_free, 1)

            nc.gpsimd.engine_nop().then_inc(out_free, 2)
            nc.gpsimd.engine_nop().then_inc(kept_ready, 1)
            for j in range(2):
                gather(j, j, 0)
            tile_loop(pool, body)

        @block.tensor
        @if_any
        def _(pe):
            def make_q(t, j, i):
                pe.wait_ge(own_loaded[j], 16 * (i + 1))
                if not (isinstance(t, int) and t == 0):
                    pe.wait_ge(q_ready, t)
                nc.tensor.transpose(q_ps[:, 0, :], own[j][:, :], ident[:, :]).then_inc(own_turned, 1)
                pe.wait_ge(own_t_ready, t + 1)
                nc.tensor.matmul(q_ps[0:DA, 1, :], w1_t, own_t[:, :], start=True, stop=True).then_inc(half_done, 1)
                if isinstance(t, int):
                    pe.wait_ge(half_ready, t + 1)
                else:
                    wait_apart(pe, half_ready, t + 1)
                nc.tensor.matmul(q_ps[0:DA, 2, :], w2_t, half[:, :], start=True, stop=True).then_inc(q_done, 1)

            def logits(t, j):
                pe.wait_ge(q_ready, t + 1)
                for c in range(PARTS):
                    if not (isinstance(t, int) and t == 0 and c < 2):
                        pe.wait_ge(logit_copied, PARTS * t + c - 1)
                    for h in range(2):
                        cols = slice((2 * c + h) * CHUNK, (2 * c + h + 1) * CHUNK)
                        last = nc.tensor.matmul(logit_ps[c % 2][:, h * CHUNK:(h + 1) * CHUNK], q_tile[j][:, :],
                                                k_t[:, cols], start=True, stop=True)
                    last.then_inc(logit_done, 1)

            def apply(t, j):
                pe.wait_ge(kept_ready, t + 2)

                def turn(g):
                    pe.wait_ge(turn_copied, GROUPS * t + g + 1)
                    for a in range(4):
                        blk = slice((4 * g + a) * P, (4 * g + a + 1) * P)
                        last = nc.tensor.transpose(turn_ps[g % 2][:, a * P:(a + 1) * P], prob[j][:, blk], ident[:, :])
                    last.then_inc(turn_done, 1)

                turn(0)
                pe.wait_ge(acc_free, t + 1)
                for g in range(GROUPS):
                    if g + 1 < GROUPS:
                        turn(g + 1)
                    pe.wait_ge(turn_copied, GROUPS * t + g + 3)
                    for a in range(4):
                        last = nc.tensor.matmul(acc_ps[:, :], turned[g % 2][:, a * P:(a + 1) * P],
                                                rows[:, 4 * g + a, :], start=(g == 0 and a == 0),
                                                stop=(g == GROUPS - 1 and a == 3))
                    last.then_inc(group_used, 1)

            def body(t, j, more):
                more(logits)
                make_q(t + 2, j, t // 2 + 1)
                apply(t, j)

            for j in range(2):
                make_q(j, j, 0)
            logits(0, 0)
            tile_loop(pe, body)

        @block.scalar
        @if_any
        def _(act):
            def make_q(t, j):
                act.wait_ge(own_turned, t + 1)
                if not (isinstance(t, int) and t == 0):
                    act.wait_ge(half_done, t)
                nc.scalar.copy(own_t[:, :], q_ps[:, 0, :]).then_inc(own_t_ready, 1)
                act.wait_ge(half_done, t + 1)
                if not (isinstance(t, int) and t == 0):
                    act.wait_ge(q_done, t)
                nc.scalar.copy(half[:, :], q_ps[0:DA, 1, :]).then_inc(half_ready, 1)
                act.wait_ge(q_done, t + 1)
                if not (isinstance(t, int) and t < 2):
                    act.wait_ge(logit_done, PARTS * (t - 1))
                nc.scalar.copy(q_tile[j][:, :], q_ps[0:DA, 2, :]).then_inc(q_ready, 1)

            def take(t, j):
                if not (isinstance(t, int) and t == 0):
                    act.wait_ge(exp_ready, 2 * t)
                for c in range(PARTS):
                    act.wait_ge(logit_done, PARTS * t + c + 1)
                    nc.scalar.copy(logit[:, c * 2 * CHUNK:(c + 1) * 2 * CHUNK], logit_ps[c % 2][:, :]
                                   ).then_inc(logit_copied, 1)

            def raise_(t, j):
                act.wait_ge(top_ready, t + 1)
                nc.scalar.activation(exp8[j][:, :], top8[j][:, :], ACT.Exp, bias=neg_top[j][:, :]
                                     ).then_inc(exp_ready, 1)
                nc.scalar.activation(prob[j][:, :], logit[:, :], ACT.Exp, bias=neg_top[j][:, :],
                                     accum_out=mass[j][:, :]).then_inc(exp_ready, 1)

            def copy_groups(t, j):
                for g in range(GROUPS):
                    act.wait_ge(turn_done, GROUPS * t + g + 1)
                    act.wait_ge(group_used, GROUPS * t + g + 1)
                    nc.scalar.copy(turned[g % 2][:, :], turn_ps[g % 2][:, :]).then_inc(turn_copied, 1)

            def body(t, j, more):
                more(take)
                make_q(t + 2, j)
                more(raise_)
                copy_groups(t, j)

            act_spare = sb("act_spare", [P, 1])
            nc.scalar.copy(act_spare[:, :], ident[:, 0:1]).then_inc(turn_copied, 2)
            for j in range(2):
                make_q(j, j)
            take(0, 0)
            raise_(0, 0)
            tile_loop(act, body)

        @block.vector
        @if_any
        def _(dve):
            V = nc.vector
            go = dve.alloc_register(f"{name}_go")
            n_summed = dve.alloc_register(f"{name}_n_summed")
            dve.reg_mov(n_summed, 0)
            V.memset(flags[:, :], 0.0).then_inc(group_used, 2)
            V.memset(at_least[:, :], 0.0).then_inc(acc_free, 1)
            V.drain()

            def find_top(t, j):
                if isinstance(t, int):
                    dve.wait_ge(logit_copied, PARTS * (t + 1))
                else:
                    wait_apart(dve, logit_copied, PARTS * (t + 1))
                V.max(top8[j][:, :], logit[:, :])
                V.drain()
                V.tensor_scalar(neg_top[j][:, :], top8[j][:, 0:1], -1.0, None, ALU.mult).then_inc(top_ready, 1)

            def prefix(values):
                V.tensor_tensor_scan(sums[:, 1:G8 + 1], values, values, sums[:, 0:1], ALU.add, ALU.max)
                V.drain()
                V.tensor_scalar(kept[:, :], sums[:, 0:G8], goal[:, :], None, ALU.is_lt)
                V.drain()

            def bisect(t, j):
                dve.wait_ge(exp_ready, 2 * (t + 1))
                V.tensor_scalar(goal[:, :], mass[j][:, :], TOP_P, None, ALU.mult)
                V.tensor_scalar(lo[:, :], mass[j][:, :], (1.0 - TOP_P) / N * 0.99, None, ALU.mult)
                V.tensor_scalar(floor[j][:, :], mass[j][:, :], 1e-12, None, ALU.mult)
                V.memset(sums[:, 0:1], 0.0)
                V.drain()
                prefix(exp8[j][:, :])
                V.tensor_scalar(w8[:, :], kept[:, :], -BIG, BIG, ALU.mult, ALU.add)
                V.drain()
                V.tensor_tensor(w8[:, :], w8[:, :], exp8[j][:, :], ALU.add)
                V.drain()
                V.tensor_reduce(hi[:, :], w8[:, :], AX.X, ALU.min)
                V.drain()
                for _ in range(halvings):
                    V.tensor_tensor(ends[:, :], lo[:, :].bitcast(I32), hi[:, :].bitcast(I32), ALU.add)
                    V.drain()
                    V.tensor_scalar(mid[:, :].bitcast(I32), ends[:, :], 1, None, ALU.arith_shift_right)
                    V.drain()
                    V.scalar_tensor_tensor(out=junk[:, :], in0=prob[j][:, :], scalar=mid[:, :], in1=prob[j][:, :],
                                           op0=ALU.is_gt, op1=ALU.mult, accum_out=above[:, :])
                    V.drain()
                    V.tensor_tensor(at_least[:, :], above[:, :], goal[:, :], ALU.is_ge)
                    V.drain()
                    V.scalar_tensor_tensor(out=lo[:, :], in0=at_least[:, :], scalar=mid[:, :], in1=lo[:, :],
                                           op0=ALU.mult, op1=ALU.max)
                    V.scalar_tensor_tensor(out=hi2[:, :], in0=at_least[:, :], scalar=BIG, in1=mid[:, :],
                                           op0=ALU.mult, op1=ALU.add)
                    V.drain()
                    V.tensor_tensor(hi[:, :], hi[:, :], hi2[:, :], ALU.min)
                    V.drain()

            def cut(t, j):
                dve.wait_ge(kept_ready, t + 1)
                V.scalar_tensor_tensor(out=rest[:, 0:N], in0=prob[j][:, :], scalar=hi[:, :], in1=prob[j][:, :],
                                       op0=ALU.is_le, op1=ALU.mult, accum_out=below[:, :])
                V.drain()
                V.memset(rest[:, N:], -1.0)
                V.tensor_tensor(base[:, :], mass[j][:, :], below[:, :], ALU.subtract)
                V.drain()
                V.tensor_copy(sums[:, 0:1], base[:, :])
                dve.reg_mov(go, 1)
                with dve.While(lambda: dve.snap(go)):
                    V.max(cand[:, :], rest[:, :])
                    V.drain()
                    prefix(cand[:, :])
                    V.scalar_tensor_tensor(out=kept[:, :], in0=cand[:, :], scalar=lo[:, :], in1=kept[:, :],
                                           op0=ALU.is_gt, op1=ALU.mult)
                    V.drain()
                    V.tensor_tensor(kept_v[:, :], cand[:, :], kept[:, :], ALU.mult)
                    V.tensor_copy(flags[:, 0:1], kept[:, G8 - 1:G8])
                    V.tensor_scalar(chosen[:, :], kept[:, :], -1.0, None, ALU.add)
                    V.drain()
                    V.tensor_tensor(chosen[:, :], chosen[:, :], kept_v[:, :], ALU.add)
                    V.tensor_reduce(gain[:, :], kept_v[:, :], AX.X, ALU.add)
                    V.drain()
                    V.match_replace(rest[:, :], chosen[:, :], rest[:, :], 0.0)
                    V.tensor_tensor(sums[:, 0:1], sums[:, 0:1], gain[:, :], ALU.add)
                    V.drain()
                    V.memset(rest[:, N:], -1.0)
                    any_row(dve, nc, flags, flags_t, total, total_i, go, summed, n_summed)
                V.drain()
                V.engine_nop().then_inc(rest_ready, 1)

            def normalise(t, j):
                dve.wait_ge(group_used, GROUPS * (t + 1) + 2)
                V.tensor_tensor(den[:, :], floor[j][:, :], acc_ps[:, D:D + 1], ALU.max)
                V.drain()
                V.reciprocal(gain[:, :], den[:, :])
                V.drain()
                dve.wait_ge(out_free, t + 1)
                V.tensor_scalar(out_tile[j][:, :], acc_ps[:, 0:D], gain[:, :], None, ALU.mult).then_inc(out_ready, 1)
                V.drain()
                V.engine_nop().then_inc(acc_free, 1)

            def body(t, j, more):
                more(find_top)
                cut(t, j)
                more(bisect)
                normalise(t, j)

            find_top(0, 0)
            bisect(0, 0)
            tile_loop(dve, body)
            V.drain()


def program(nc, a, out):
    lists = nc.dram_tensor("lists", [MAX_UNITS, P, LIST], I32, kind="Internal").ap()
    xa_dram = [nc.dram_tensor(f"xa_dram{s}", [N, D], F32, kind="Internal").ap() for s in range(2)]
    order = [nc.dram_tensor(f"order{s}", [N + 2 * P, 1], I32, kind="Internal").ap() for s in range(2)]
    q_dram = nc.dram_tensor("q_dram", [DA, N], F32, kind="Internal").ap()
    hp_dram = nc.dram_tensor("hp_dram", [N, D + H], F32, kind="Internal").ap()
    kv_dram = nc.dram_tensor("kv_dram", [N, 2 * D], F32, kind="Internal").ap()
    with ExitStack() as ctx:
        def sb(name, shape, dt=F32):
            return ctx.enter_context(nc.sbuf_tensor(name, shape, dt))

        ident = sb("unit_matrix", [P, P])
        z = sb("result", [P, T, D])
        rdeg = sb("rdeg", [P, T])
        units_i = sb("units_i", [P, 1], I32)

        with nc.sbuf_tensor("u_rows", [P, 4, D], F32) as u_t, \
             nc.sbuf_tensor("ln_gb", [P, 2, D], F32) as ln_gb:
            copy_dram(nc, "in0", [
                (ident[:, :], a["ident"]), (z[:, :, :], node_view(a["x"])),
                (u_t[:, 0:2, :], a["U1_t"].rearrange("s i o -> i s o")),
                (u_t[:, 2:4, :], a["U2_t"].rearrange("s i o -> i s o")),
                (ln_gb[:, 0, :], a["ln_g"].partition_broadcast(P)), (ln_gb[:, 1, :], a["ln_b"].partition_broadcast(P)),
            ])
            def add_z(weight):
                def evict(g, ps):
                    part = z[:, bass.ds(4 * g, 4), :]
                    return nc.vector.tensor_tensor(part, part, ps[:, :, :], ALU.add)
                return [(weight, evict)]

            with ExitStack() as l0:
                def sb0(name, shape, dt=F32):
                    return l0.enter_context(nc.sbuf_tensor(name, shape, dt))

                w_t = sb0("w_t", [P, 3, DA])
                rows = sb0("rows", [P, T, D + 1])
                xf1 = sb0("xf1", [P, T, D + 1])
                k_t = sb0("k_t", [DA, N])
                below_ones = sb0("below_and_ones", [P, 2, P])
                node_f = sb0("node_numbers", [P, T])
                node_i = sb0("node_numbers_i", [P, T], I32)
                unresolved = sb0("unresolved", [P, T])
                count_i = sb0("count_i", [P, 1], I32)
                copy_dram(nc, "in1", [
                    (rows[:, :, 0:D], node_view(a["x"])), (below_ones[:, :, :], a["below_ones"]),
                    (node_f[:, :], a["node_f"]), (node_i[:, :], a["node_i"]),
                    (w_t[:, 0, :], a["W1_t"]), (w_t[0:DA, 1, :], a["W2_t"]), (w_t[:, 2, :], a["W3_t"]),
                ])
                weights = (w_t[:, 0, :], w_t[0:DA, 1, :], w_t[:, 2, :])
                with nc.Block() as block:
                    @block.vector
                    def _(dve):
                        V = nc.vector
                        V.memset(rows[:, :, D:D + 1], 1.0)
                        V.drain()

                find_neighbours(nc, a["adj"], a["adj_tiles"], a["tile_ids"], lists, units_i, rows, xf1, rdeg)

                def step(s, table, beside, xa_out):
                    with nc.sbuf_tensor(f"q_t{s}", [DA, N], F32) as q_t:
                        attention_inputs(nc, f"in_s{s}", rows, ident, weights, q_t, k_t, z,
                                         u_t[:, 2, :] if s else None)
                        copy_dram(nc, f"q_out{s}", [(q_dram, q_t[:, :])])
                    top_p_rows(nc, f"l{s}", LISTED[s], ident, q_dram, k_t, rows, xa_out, unresolved, beside)
                    unresolved_first(nc, f"o{s}", unresolved, (below_ones, node_f[:, :], node_i), order[s], count_i)
                    full_rows(nc, f"f{s}", BISECTIONS[s], weights[:2], ident, k_t, rows, table, order[s], count_i,
                              xa_out)
                    copy_dram(nc, f"xa{s}", [(rows[:, :, 0:D], node_view(xa_out))])

                step(0, a["x"], None, xa_dram[0])
                project(nc, "u10", xf1[:, :, 0:D], ident, add_z(u_t[:, 0, :]))
                with nc.sbuf_tensor("xf2", [P, T, D], F32) as xf2:
                    step(1, xa_dram[0], (a["adj_tiles"], xf1, xf2, rdeg), xa_dram[1])
                    project(nc, "u11", xf2[:, :, :], ident, add_z(u_t[:, 1, :]))
                project(nc, "u21", rows[:, :, 0:D], ident, add_z(u_t[:, 3, :]))

            def nothing(dve):
                pass

            with nc.sbuf_tensor("nodes", [P, T, D], F32) as x:
                copy_dram(nc, "in_x", [(x[:, :, :], node_view(a["x"]))])

                def add_layer0(dve):
                    V = nc.vector
                    V.drain()
                    V.tensor_tensor(z[:, :, :], z[:, :, :], ln_gb[:, 0:1, :].to_broadcast([P, T, D]), ALU.mult)
                    V.drain()
                    V.tensor_tensor(z[:, :, :], z[:, :, :], ln_gb[:, 1:2, :].to_broadcast([P, T, D]), ALU.add)
                    V.drain()
                    V.tensor_tensor(z[:, :, :], z[:, :, :], x[:, :, :], ALU.add)

                layer_norms(nc, "ln0", z[:, :, :], [nothing, add_layer0])

        acc = sb("acc", [P, T, D])
        denom = sb("denom", [P, T, H])

        def normalise_heads(V):
            V.reciprocal(denom[:, :, :], denom[:, :, :])
            V.drain()
            a4 = acc[:, :, :].rearrange("p t (h f) -> p (t h) f", h=H)
            V.tensor_tensor(a4, a4, denom[:, :, :].rearrange("p t h -> p (t h)").unsqueeze(2).to_broadcast(
                [P, T * H, HD]), ALU.mult)
            V.drain()

        with ExitStack() as l1:
            def sb1(name, shape):
                return l1.enter_context(nc.sbuf_tensor(name, shape, F32))

            w = sb1("l1_w", [P, D])
            a_rows = sb1("l1_a", [P, H, 2 * HD])
            hp = sb1("hp", [P, T, D + H])
            prod = sb1("hp_prod", [P, T, D])
            src = sb1("src", [P, T, H])
            copy_dram(nc, "in2", [(w[:, :], a["L1_W"]),
                                  (a_rows[:, :, :], a["L1_a"].rearrange("h f -> (h f)").partition_broadcast(P).rearrange(
                                      "p (h f) -> p h f", h=H))])
            project(nc, "hp", z[:, :, :], ident, [(w[:, :], lambda g, ps: nc.vector.tensor_copy(
                hp[:, bass.ds(4 * g, 4), 0:D], ps[:, :, :]))])
            with nc.Block() as block:
                @block.vector
                def _(dve):
                    V = nc.vector
                    for half, dst in ((0, src[:, :, :]), (1, hp[:, :, D:D + H])):
                        for h in range(H):
                            V.tensor_tensor(prod[:, :, h * HD:(h + 1) * HD], hp[:, :, h * HD:(h + 1) * HD],
                                            a_rows[:, h:h + 1, half * HD:(half + 1) * HD].to_broadcast([P, T, HD]),
                                            ALU.mult)
                        V.drain()
                        V.tensor_reduce(dst, prod[:, :, :].rearrange("p t (h f) -> p t h f", h=H), AX.X, ALU.add)
                        V.drain()
            copy_dram(nc, "hp_out", [(node_view(hp_dram), hp[:, :, :])])

            def scores1(dve, t, values, got, score, prod_):
                V = nc.vector
                V.tensor_tensor(score[:, :, :], got[:, :, D:D + H],
                                src[:, bass.ds(t, 1), :].to_broadcast([P, G8, H]), ALU.add)
                V.drain()
                V.scalar_tensor_tensor(out=score[:, :, :], in0=score[:, :, :], scalar=0.2, in1=score[:, :, :],
                                       op0=ALU.mult, op1=ALU.max)

            graph_attention(nc, "a1", hp_dram, D + H, 0, scores1, lists, units_i, acc, denom)

        def elu_in_place(name):
            with nc.sbuf_tensor(f"{name}_neg", [P, T, D], F32) as neg, phase_semaphores(nc) as new_sem, \
                 nc.Block() as block:
                neg_ready, neg_raised = new_sem(f"{name}_n"), new_sem(f"{name}_e")

                @block.vector
                def _(dve):
                    V = nc.vector
                    normalise_heads(V)
                    V.tensor_scalar(neg[:, :, :], acc[:, :, :], 0.0, None, ALU.min).then_inc(neg_ready, 1)
                    V.tensor_scalar(acc[:, :, :], acc[:, :, :], 0.0, -1.0, ALU.max, ALU.add)
                    V.drain()
                    V.tensor_tensor(z[:, :, :], z[:, :, :], acc[:, :, :], ALU.add)
                    dve.wait_ge(neg_raised, 1)
                    V.drain()
                    V.tensor_tensor(z[:, :, :], z[:, :, :], neg[:, :, :], ALU.add)
                    V.drain()

                @block.scalar
                def _(act):
                    act.wait_ge(neg_ready, 1)
                    nc.scalar.activation(neg[:, :, :], neg[:, :, :], ACT.Exp).then_inc(neg_raised, 1)

        elu_in_place("elu")
        layer_norms(nc, "ln1", z[:, :, :], [lambda dve: None])

        with ExitStack() as l2:
            def sb2(name, shape):
                return l2.enter_context(nc.sbuf_tensor(name, shape, F32))

            w = sb2("l2_w", [P, 4, D])
            bias = sb2("l2_bias", [P, 4, D])
            g_bias = sb2("g_bias", [P, 1])
            q = sb2("q", [P, T, D])
            copy_dram(nc, "in3", [
                (w[:, 0:3, :], a["Wqkv"].rearrange("i (c o) -> i c o", c=3)), (w[:, 3, :], a["Wout"]),
                (bias[:, 0:3, :], a["bqkv"].partition_broadcast(P).rearrange("p (c o) -> p c o", c=3)),
                (bias[:, 3, :], a["bout"].partition_broadcast(P)), (g_bias[:, :], a["graph_bias"].partition_broadcast(P)),
            ])
            with nc.sbuf_tensor("kv", [P, T, 2 * D], F32) as kv:
                def with_bias(c, dst):
                    return (w[:, c, :], lambda g, ps: nc.vector.tensor_tensor(
                        dst[:, bass.ds(4 * g, 4), :], ps[:, :, :], bias[:, c:c + 1, :].to_broadcast([P, 4, D]), ALU.add))

                project(nc, "qkv", z[:, :, :], ident, [with_bias(0, q[:, :, :]), with_bias(1, kv[:, :, 0:D]),
                                                       with_bias(2, kv[:, :, D:2 * D])])
                copy_dram(nc, "kv_out", [(node_view(kv_dram), kv[:, :, :])])
            edge = sb2("edge", [P, G8])

            def scores2(dve, t, values, got, score, prod):
                V = nc.vector
                V.tensor_tensor(prod[:, :].rearrange("p (k d) -> p k d", k=G8), got[:, :, 0:D],
                                q[:, bass.ds(t, 1), :].to_broadcast([P, G8, D]), ALU.mult)
                V.tensor_scalar(edge[:, :], values, g_bias[:, :], None, ALU.mult)
                V.drain()
                V.tensor_reduce(score[:, :, :], prod[:, :].rearrange("p (k h f) -> p k h f", k=G8, h=H), AX.X, ALU.add)
                V.drain()
                V.scalar_tensor_tensor(out=score[:, :, :], in0=score[:, :, :], scalar=HD ** -0.5,
                                       in1=edge[:, :].unsqueeze(2).to_broadcast([P, G8, H]),
                                       op0=ALU.mult, op1=ALU.add)

            graph_attention(nc, "a2", kv_dram, 2 * D, D, scores2, lists, units_i, acc, denom)
            with nc.Block() as block:
                @block.vector
                def _(dve):
                    normalise_heads(nc.vector)

            def add_out(g, ps):
                part = z[:, bass.ds(4 * g, 4), :]
                return nc.vector.tensor_tensor(part, part, ps[:, :, :], ALU.add)

            project(nc, "wout", acc[:, :, :], ident, [(w[:, 3, :], add_out)])
            layer_norms(nc, "ln2", z[:, :, :], [lambda dve: nc.vector.tensor_tensor(
                z[:, :, :], z[:, :, :], bias[:, 3:4, :].to_broadcast([P, T, D]), ALU.add)])

        with ExitStack() as l3:
            w = l3.enter_context(nc.sbuf_tensor("l3_w", [P, D], F32))
            root = l3.enter_context(nc.sbuf_tensor("root", [P, T], F32))
            rooted = l3.enter_context(phase_semaphores(nc))("rooted")
            copy_dram(nc, "in4", [(w[:, :], a["L3_W_t"])])
            project(nc, "support", z[:, :, :], ident, [(w[:, :], lambda g, ps: nc.vector.tensor_copy(
                acc[:, bass.ds(4 * g, 4), :], ps[:, :, :]))])
            with nc.Block() as block:
                @block.scalar
                def _(act):
                    nc.scalar.activation(root[:, :], rdeg[:, :], ACT.Sqrt).then_inc(rooted, 1)

                @block.vector
                def _(dve):
                    dve.wait_ge(rooted, 1)
                    nc.vector.tensor_tensor(acc[:, :, :], acc[:, :, :],
                                            root[:, :].unsqueeze(2).to_broadcast([P, T, D]), ALU.mult)
                    nc.vector.drain()
            out3 = l3.enter_context(nc.sbuf_tensor("out3", [P, T, D], F32))
            adj_times(nc, "l3", a["adj_tiles"], acc[:, :, :], out3)

            def finish(dve):
                V = nc.vector
                V.tensor_tensor(out3[:, :, :], out3[:, :, :], root[:, :].unsqueeze(2).to_broadcast([P, T, D]),
                                ALU.mult)
                V.drain()
                V.scalar_tensor_tensor(out=z[:, :, :], in0=out3[:, :, :], scalar=0.0, in1=z[:, :, :],
                                       op0=ALU.max, op1=ALU.add)

            layer_norms(nc, "ln3", z[:, :, :], [finish])
        copy_dram(nc, "result", [(node_view(out), z[:, :, :])])


def kernel(**inputs):
    import numpy as np
    import concourse.bacc as bacc
    from concourse.bass_utils import run_bass_kernel_spmd

    def arr(v):
        return np.ascontiguousarray(v)

    i = {k: np.asarray(v) for k, v in inputs.items()}
    arrays = {
        "x": arr(i["x"]), "adj": arr(i["adj"]),
        "adj_tiles": arr(i["adj"].reshape(T, P, T, P).transpose(0, 3, 2, 1)),
        "W1_t": arr(i["L0_gnn_W1"].T), "W2_t": arr(i["L0_gnn_W2"].T), "W3_t": arr(i["L0_gnn_W3"].T),
        "U1_t": arr(i["L0_gnn_U1"].transpose(0, 2, 1)), "U2_t": arr(i["L0_gnn_U2"].transpose(0, 2, 1)),
        "ln_g": arr(i["L0_gnn_ln_g"]), "ln_b": arr(i["L0_gnn_ln_b"]),
        "L1_W": arr(i["L1_gnn_W"]), "L1_a": arr(i["L1_gnn_a"]),
        "Wqkv": arr(i["L2_gnn_Wqkv"]), "bqkv": arr(i["L2_gnn_bqkv"]), "Wout": arr(i["L2_gnn_Wout"]),
        "bout": arr(i["L2_gnn_bout"]), "graph_bias": arr(i["L2_gnn_graph_bias"].reshape(1)),
        "L3_W_t": arr(i["L3_gnn_W"].T),
        "ident": np.eye(P, dtype=np.float32),
        "below_ones": np.stack([np.triu(np.ones((P, P), np.float32), 1), np.ones((P, P), np.float32)], 1),
        "node_f": np.arange(N, dtype=np.float32).reshape(T, P).T.copy(),
        "node_i": np.arange(N, dtype=np.int32).reshape(T, P).T.copy(),
        "tile_ids": np.tile(np.arange(T, dtype=np.int32), (P, 1)),
    }
    nc = bacc.Bacc("TRN2", target_bir_lowering=False, num_devices=1)
    aps = {n: nc.dram_tensor(n, v.shape, mybir.dt.from_np(v.dtype), kind="ExternalInput").ap()
           for n, v in arrays.items()}
    out = nc.dram_tensor("out", (N, D), F32, kind="ExternalOutput").ap()
    program(nc, aps, out)
    r = run_bass_kernel_spmd(nc, [arrays], core_ids=[0])
    return r.results[0]["out"]
```

```python
import concourse.bass as bass
from concourse import mybir
from contextlib import ExitStack, contextmanager

F32 = mybir.dt.float32
BF16 = mybir.dt.bfloat16
I32 = mybir.dt.int32
U32 = mybir.dt.uint32
ALU = mybir.AluOpType
ACT = mybir.ActivationFunctionType
AX = mybir.AxisListType

P = 128
N = 4096
T = N // P
D = 128
DA = 64
H = 4
HD = D // H
G8 = 8
TILE_COL = 2 * G8
LIST = TILE_COL + 1
DEPTH = 4
MAX_UNITS = T * (N // G8) + DEPTH - 1
CHUNK = 512
TOP_P = 0.9
BIG = 1e30
SEGMENTS = 32
LISTED = (64, 96)
SKIP_TIES = (True, False)
SHARES = ((4, 8), (3, 6, 8))
BISECTIONS = (5, 8)


@contextmanager
def phase_semaphores(nc):
    taken = []

    def new(name):
        taken.append(nc.alloc_semaphore(name))
        return taken[-1]

    yield new
    nc.clear_and_free_semaphores(taken)
    nc.all_engine_barrier()


def node_view(ap):
    return ap.rearrange("(t p) d -> p t d", p=P)


def wait_apart(eng, sem, value):
    value = eng.to_reg(value)
    eng.wait_ge(sem, 1)
    eng.wait_ge(sem, value)


def sum_flags(nc, flags, flags_t, total, total_i):
    nc.vector.transpose(flags_t[:, :], flags[:, :])
    nc.vector.drain()
    nc.vector.tensor_reduce(total[:, :], flags_t[:, :], AX.X, ALU.add)
    nc.vector.drain()
    return nc.vector.tensor_copy(total_i[:, :], total[:, :])


def any_row(dve, nc, flags, flags_t, total, total_i, go, summed, n_summed):
    sum_flags(nc, flags, flags_t, total, total_i).then_inc(summed, 1)
    dve.reg_mov(n_summed, dve.snap(n_summed) + 1)
    wait_apart(dve, summed, dve.snap(n_summed))
    read_flags(dve, total_i, go)


def read_flags(eng, total_i, go):
    parts = [eng.value_load(total_i[32 * q:32 * q + 1, 0:1]) for q in range(4)]
    eng.reg_mov(go, parts[0] + parts[1] + parts[2] + parts[3])


def find_neighbours(nc, adj, adj_tiles, tile_ids, ident, lists, units_i, rows, xf_new, rdeg):
    with ExitStack() as ctx:
        new_sem = ctx.enter_context(phase_semaphores(nc))
        def sb(name, shape, dt=F32):
            return ctx.enter_context(nc.sbuf_tensor(name, shape, dt))

        HALF = T // 2
        AHEAD = 4
        adj_rows = [sb(f"adj_rows{j}", [P, N]) for j in range(AHEAD)]
        adj_t = [sb(f"nb_adj_t{h}", [P, HALF, P]) for h in range(4)]
        junk = sb("nb_junk", [P, N], BF16)
        found = [sb(f"found{j}", [P, LIST], I32) for j in range(2)]
        ids = sb("ids", [P, T], I32)
        nonzeros = [sb(f"nonzeros{j}", [P, 1]) for j in range(2)]
        most = sb("nb_most", [1, 1])
        most_i = [sb(f"nb_most_i{j}", [1, 1], I32) for j in range(2)]
        units = sb("units", [P, 1])
        count_ps = [ctx.enter_context(nc.psum_tensor(f"nb_count_ps{j}", [1, P], F32)) for j in range(2)]
        r_ps = [ctx.enter_context(nc.psum_tensor(f"nb_r_ps{j}", [P, D + 1], F32)) for j in range(2)]
        rows_loaded = [new_sem(f"rows_loaded{j}") for j in range(AHEAD)]
        rows_done = new_sem("rows_done")
        counted = new_sem("nb_counted")
        count_turned = new_sem("nb_count_turned")
        most_ready = new_sem("nb_most_ready")
        found_ready = new_sem("found_ready")
        found_free = [new_sem(f"found_free{j}") for j in range(2)]
        adj_loaded = [new_sem(f"nb_adj_loaded{h}") for h in range(4)]
        adj_used = [new_sem(f"nb_adj_used{h}") for h in range(2)]
        r_taken = new_sem("nb_r_taken")
        block = ctx.enter_context(nc.Block())

        @block.sync
        def _(sp):
            def load(t, j, first):
                p = j % 2
                if not first:
                    sp.wait_ge(rows_done, t - AHEAD + 1)
                sp.dma_start(adj_rows[j][:, :], adj[bass.ds(t * P, P), :]).then_inc(rows_loaded[j], 16)
                for h in range(2):
                    if not first or j >= 2:
                        sp.wait_ge(adj_used[h], t - 1)
                    sp.dma_start(adj_t[2 * p + h][:, :, :],
                                 adj_tiles[bass.ds(t, 1), :, h * HALF:(h + 1) * HALF, :].rearrange(
                                     "a p b c -> p (a b) c")).then_inc(adj_loaded[2 * p + h], 16)

            for j in range(AHEAD):
                load(j, j, True)
            with sp.Fori(1, T // AHEAD) as i:
                for j in range(AHEAD):
                    load(AHEAD * i + j, j, False)

        @block.scalar
        def _(act):
            def body(t, j, first):
                p = j % 2
                act.wait_ge(rows_loaded[j], 16 * (t // AHEAD) + 16)
                if not (first and j == 0):
                    act.wait_ge(counted, t)
                if not first or j >= 2:
                    act.wait_ge(count_turned, t - 1)
                nc.scalar.activation(junk[:, :], adj_rows[j][:, :], ACT.Sign,
                                     accum_out=nonzeros[p][:, :]).then_inc(counted, 1)
                act.wait_ge(adj_used[1], t + 1)
                nc.scalar.copy(xf_new[:, bass.ds(t, 1), :].rearrange("p a d -> p (a d)"), r_ps[p][:, :]
                               ).then_inc(r_taken, 1)

            for j in range(AHEAD):
                body(j, j, True)
            with act.Fori(1, T // AHEAD) as i:
                for j in range(AHEAD):
                    body(AHEAD * i + j, j, False)

        @block.tensor
        def _(pe):
            def body(t, j, first):
                p = j % 2
                pe.wait_ge(counted, t + 1)
                if not first or j >= 2:
                    pe.wait_ge(most_ready, t - 1)
                nc.tensor.transpose(count_ps[p][:, :], nonzeros[p][:, :], ident[:, :]).then_inc(count_turned, 1)
                if not first or j >= 2:
                    pe.wait_ge(r_taken, t - 1)
                for h in range(2):
                    pe.wait_ge(adj_loaded[2 * p + h], 16 * (t // 2) + 16)
                    for b in range(HALF):
                        last = nc.tensor.matmul(r_ps[p][:, :], adj_t[2 * p + h][:, b, :], rows[:, h * HALF + b, :],
                                                start=(h == 0 and b == 0), stop=(h == 1 and b == HALF - 1))
                    last.then_inc(adj_used[h], 1)

            for j in range(AHEAD):
                body(j, j, True)
            with pe.Fori(1, T // AHEAD) as i:
                for j in range(AHEAD):
                    body(AHEAD * i + j, j, False)

        @block.vector
        def _(dve):
            V = nc.vector
            V.memset(units[:, :], 0.0)
            V.drain()
            go = dve.alloc_register("nb_go")
            n = [dve.alloc_register(f"nb_n{j}") for j in range(2)]
            for j in range(2):
                dve.reg_mov(n[j], 0)
            for j in range(2):
                dve.wait_ge(found_free[j], 16)

            def unit(t, j, p):
                values = found[p][:, G8:TILE_COL].bitcast(F32)
                V.max(values, adj_rows[j][:, :])
                V.tensor_copy(found[p][:, TILE_COL:LIST], ids[:, bass.ds(t, 1)])
                V.tensor_scalar(units[:, :], units[:, :], 1.0, None, ALU.add)
                V.drain()
                V.max_index(found[p][:, 0:G8].bitcast(U32), values, adj_rows[j][:, :])
                dve.reg_mov(n[p], dve.snap(n[p]) + 1)
                V.drain()
                V.engine_nop().then_inc(found_ready, 1)

            with dve.Fori(0, T // AHEAD) as i:
                for j in range(AHEAD):
                    p = j % 2
                    t = AHEAD * i + j
                    wait_apart(dve, found_free[p], 16 * dve.snap(n[p]) + 16)
                    dve.wait_ge(count_turned, t + 1)
                    V.tensor_reduce(most[:, :], count_ps[p][:, :], AX.X, ALU.max)
                    V.drain()
                    V.tensor_scalar(most_i[p][:, :], most[:, :], 1.0, None, ALU.max).then_inc(most_ready, 1)
                    unit(t, j, p)
                    wait_apart(dve, most_ready, t + 1)
                    dve.reg_mov(go, (dve.value_load(most_i[p][0:1, 0:1], min_val=1, max_val=N) - 1) // G8)
                    with dve.While(lambda: dve.snap(go)):
                        V.match_replace(adj_rows[j][:, :], found[p][:, G8:TILE_COL].bitcast(F32), adj_rows[j][:, :],
                                        0.0)
                        V.drain()
                        wait_apart(dve, found_free[p], 16 * dve.snap(n[p]) + 16)
                        unit(t, j, p)
                        dve.reg_mov(go, dve.snap(go) - 1)
                    V.engine_nop().then_inc(rows_done, 1)
            wait_apart(dve, found_free[0], 16 * dve.snap(n[0]) + 16)
            V.tensor_copy(units_i[:, :], units[:, :])
            V.memset(found[0][:, :], 0)
            V.drain()
            V.engine_nop().then_inc(found_ready, 1)
            dve.wait_ge(r_taken, T)
            V.tensor_tensor(xf_new[:, :, :], xf_new[:, :, :], rows[:, :, :], ALU.add)
            V.drain()
            V.reciprocal(rdeg[:, :], xf_new[:, :, D:D + 1].rearrange("p t a -> p (t a)"))
            V.drain()
            V.tensor_tensor(xf_new[:, :, :], xf_new[:, :, :], rdeg[:, :].unsqueeze(2).to_broadcast([P, T, D + 1]),
                            ALU.mult)
            V.drain()

        @block.gpsimd
        def _(pool):
            n = pool.alloc_register("nb_pool_n")
            go = pool.alloc_register("nb_pool_go")
            pool.reg_mov(n, 0)
            for j in range(2):
                half = slice(j * (T // 2), (j + 1) * (T // 2))
                pool.dma_start(ids[:, half], tile_ids[:, half]).then_inc(found_free[j], 16)

            def store(j):
                pool.dma_start(lists[bass.ds(pool.snap(n), 1), :, :].rearrange("a p c -> p (a c)"),
                               found[j][:, :]).then_inc(found_free[j], 16)
                pool.reg_mov(n, pool.snap(n) + 1)

            stores = [pool.alloc_register(f"nb_stores{j}") for j in range(2)]
            for j in range(2):
                pool.reg_mov(stores[j], 0)
            with pool.Fori(0, T // 2):
                for j in range(2):
                    wait_apart(pool, found_ready, pool.snap(n) + 1)
                    pool.reg_mov(go, (pool.value_load(most_i[j][0:1, 0:1], min_val=1, max_val=N) - 1) // G8)
                    store(j)
                    pool.reg_mov(stores[j], pool.snap(stores[j]) + 1)
                    with pool.While(lambda: pool.snap(go)):
                        wait_apart(pool, found_ready, pool.snap(n) + 1)
                        store(j)
                        pool.reg_mov(stores[j], pool.snap(stores[j]) + 1)
                        pool.reg_mov(go, pool.snap(go) - 1)
            wait_apart(pool, found_ready, pool.snap(n) + 1)
            for _ in range(DEPTH - 1):
                store(0)
            wait_apart(pool, found_free[0], 16 * pool.snap(stores[0]) + 16 * DEPTH)
            wait_apart(pool, found_free[1], 16 * pool.snap(stores[1]) + 16)


def gather_units(nc, name, table, width, lists, units_i, dve_unit, act_unit=None):
    with ExitStack() as ctx:
        new_sem = ctx.enter_context(phase_semaphores(nc))
        def sb(nm, shape, dt=F32):
            return ctx.enter_context(nc.sbuf_tensor(f"{name}_{nm}", shape, dt))

        def sem(nm):
            return new_sem(f"{name}_{nm}")

        lst = [sb(f"list{j}", [P, LIST], I32) for j in range(DEPTH)]
        got = [sb(f"got{j}", [P, G8 * width]) for j in range(DEPTH)]
        listed = [sem(f"listed{j}") for j in range(DEPTH)]
        gathered = [sem(f"gathered{j}") for j in range(DEPTH)]
        unit_used = sem("unit_used")
        block = ctx.enter_context(nc.Block())

        def rounds(eng):
            units = eng.value_load(units_i[0:1, 0:1])
            return (units + (DEPTH - 1)) // DEPTH

        @block.sync
        def _(sp):
            def load(u, j):
                sp.dma_start(lst[j][:, :], lists[bass.ds(u, 1), :, :].rearrange("a p c -> p (a c)")
                             ).then_inc(listed[j], 16)

            n = rounds(sp)
            for j in range(DEPTH):
                load(j, j)
            with sp.Fori(1, n) as i:
                for j in range(DEPTH):
                    sp.wait_ge(unit_used, DEPTH * (i - 1) + j + 1)
                    load(DEPTH * i + j, j)

        @block.gpsimd
        def _(pool):
            with pool.Fori(0, rounds(pool)) as i:
                for j in range(DEPTH):
                    wait_apart(pool, listed[j], 16 * i + 16)
                    for k in range(G8):
                        pool.indirect_dma_start(
                            got[j][:, k * width:(k + 1) * width], None, table,
                            bass.IndirectOffsetOnAxis(ap=lst[j][:, k:k + 1].bitcast(U32), axis=0),
                        ).then_inc(gathered[j], 16)

        @block.vector
        def _(dve):
            with dve.Fori(0, rounds(dve)) as i:
                for j in range(DEPTH):
                    wait_apart(dve, listed[j], 16 * i + 16)
                    t = dve.value_load(lst[j][0:1, TILE_COL:LIST], min_val=0, max_val=T - 1)
                    dve.wait_ge(gathered[j], 16 * G8 * (i + 1))
                    dve_unit(dve, DEPTH * i + j, t, lst[j][:, G8:TILE_COL].bitcast(F32),
                             got[j][:, :].rearrange("p (k w) -> p k w", k=G8))
                    nc.vector.drain()
                    nc.vector.engine_nop().then_inc(unit_used, 1)

        if act_unit is not None:
            @block.scalar
            def _(act):
                with act.Fori(0, rounds(act)) as i:
                    for j in range(DEPTH):
                        act_unit(act, DEPTH * i + j)


def adj_times(nc, name, adj_tiles, src, out):
    with ExitStack() as ctx:
        new_sem = ctx.enter_context(phase_semaphores(nc))
        HALF = T // 2
        adj_t = [ctx.enter_context(nc.sbuf_tensor(f"{name}_adj_t{h}", [P, HALF, P], F32)) for h in range(4)]
        ps = [ctx.enter_context(nc.psum_tensor(f"{name}_ps{j}", [P, D], F32)) for j in range(2)]
        adj_loaded = [new_sem(f"{name}_adj_loaded{h}") for h in range(4)]
        adj_used = [new_sem(f"{name}_adj_used{h}") for h in range(2)]
        taken = new_sem(f"{name}_taken")
        block = ctx.enter_context(nc.Block())

        @block.sync
        def _(sp):
            def load(t, j, first):
                for h in range(2):
                    if not first:
                        sp.wait_ge(adj_used[h], t - 1)
                    sp.dma_start(adj_t[2 * j + h][:, :, :],
                                 adj_tiles[bass.ds(t, 1), :, h * HALF:(h + 1) * HALF, :].rearrange(
                                     "a p b c -> p (a b) c")).then_inc(adj_loaded[2 * j + h], 16)

            for j in range(2):
                load(j, j, True)
            with sp.Fori(1, T // 2) as i:
                for j in range(2):
                    load(2 * i + j, j, False)

        @block.tensor
        def _(pe):
            def body(t, j, first):
                if not first:
                    pe.wait_ge(taken, t - 1)
                for h in range(2):
                    pe.wait_ge(adj_loaded[2 * j + h], 16 * (t // 2) + 16)
                    for b in range(HALF):
                        last = nc.tensor.matmul(ps[j][:, :], adj_t[2 * j + h][:, b, :], src[:, h * HALF + b, :],
                                                start=(h == 0 and b == 0), stop=(h == 1 and b == HALF - 1))
                    last.then_inc(adj_used[h], 1)

            for j in range(2):
                body(j, j, True)
            with pe.Fori(1, T // 2) as i:
                for j in range(2):
                    body(2 * i + j, j, False)

        @block.vector
        def _(dve):
            with dve.Fori(0, T // 2) as i:
                for j in range(2):
                    t = 2 * i + j
                    dve.wait_ge(adj_used[1], t + 1)
                    nc.vector.tensor_tensor(out[:, bass.ds(t, 1), :].rearrange("p a d -> p (a d)"), ps[j][:, :],
                                            src[:, bass.ds(t, 1), :].rearrange("p a d -> p (a d)"), ALU.add
                                            ).then_inc(taken, 1)
            nc.vector.drain()


def graph_attention(nc, name, table, width, value_at, scores, lists, units_i, acc, denom):
    with ExitStack() as ctx:
        new_sem = ctx.enter_context(phase_semaphores(nc))
        def sb(nm, shape, dt=F32):
            return ctx.enter_context(nc.sbuf_tensor(f"{name}_{nm}", shape, dt))

        top = sb("top", [P, T, H])
        new_top = sb("new_top", [P, H])
        score = sb("score", [P, G8, H])
        absent = sb("absent", [P, G8])
        power = sb("power", [P, (1 + G8) * H])
        raised = sb("raised", [P, (1 + G8) * H])
        psum = sb("psum", [P, H])
        prod = sb("prod", [P, G8 * D])
        part = sb("part", [P, D])
        power_ready = new_sem(f"{name}_power_ready")
        raised_ready = new_sem(f"{name}_raised_ready")
        start = new_sem(f"{name}_start")
        with nc.Block() as first:
            @first.vector
            def _(dve):
                nc.vector.memset(top[:, :, :], -BIG)
                nc.vector.memset(denom[:, :, :], 0.0)
                nc.vector.memset(acc[:, :, :], 0.0).then_inc(start, 1)
                dve.wait_ge(start, 1)

        def unit(dve, u, t, values, got):
            V = nc.vector
            topt = top[:, bass.ds(t, 1), :].rearrange("p a h -> p (a h)")
            dent = denom[:, bass.ds(t, 1), :].rearrange("p a h -> p (a h)")
            acct = acc[:, bass.ds(t, 1), :].rearrange("p a d -> p (a d)")
            V.tensor_scalar(absent[:, :], values, 0.0, -1.0, ALU.is_gt, ALU.add)
            scores(dve, t, values, got, score, prod)
            V.drain()
            V.scalar_tensor_tensor(out=score[:, :, :], in0=absent[:, :].unsqueeze(2).to_broadcast([P, G8, H]),
                                   scalar=BIG, in1=score[:, :, :], op0=ALU.mult, op1=ALU.add)
            V.drain()
            V.tensor_reduce(new_top[:, :], score[:, :, :].rearrange("p k h -> p h k"), AX.X, ALU.max)
            V.drain()
            V.tensor_tensor(new_top[:, :], new_top[:, :], topt, ALU.max)
            V.drain()
            V.tensor_tensor(power[:, 0:H], topt, new_top[:, :], ALU.subtract)
            V.tensor_tensor(power[:, H:].rearrange("p (k h) -> p k h", k=G8), score[:, :, :],
                            new_top[:, :].unsqueeze(1).to_broadcast([P, G8, H]), ALU.subtract)
            V.drain()
            V.tensor_copy(topt, new_top[:, :]).then_inc(power_ready, 1)
            dve.wait_ge(raised_ready, u + 1)
            keep = raised[:, 0:H]
            weight = raised[:, H:].rearrange("p (k h) -> p k h", k=G8)
            V.tensor_reduce(psum[:, :], raised[:, H:].rearrange("p (k h) -> p h k", k=G8), AX.X, ALU.add)
            V.tensor_tensor(dent, dent, keep, ALU.mult)
            V.tensor_tensor(prod[:, :].rearrange("p (k h f) -> p k h f", k=G8, h=H),
                            got[:, :, value_at:value_at + D].rearrange("p k (h f) -> p k h f", h=H),
                            weight.unsqueeze(3).to_broadcast([P, G8, H, HD]), ALU.mult)
            V.tensor_tensor(acct.rearrange("p (h f) -> p h f", h=H), acct.rearrange("p (h f) -> p h f", h=H),
                            keep.unsqueeze(2).to_broadcast([P, H, HD]), ALU.mult)
            V.drain()
            V.tensor_tensor(dent, dent, psum[:, :], ALU.add)
            V.tensor_reduce(part[:, :], prod[:, :].rearrange("p (k d) -> p d k", k=G8), AX.X, ALU.add)
            V.drain()
            V.tensor_tensor(acct, acct, part[:, :], ALU.add)

        def act_unit(act, u):
            act.wait_ge(power_ready, u + 1)
            nc.scalar.activation(raised[:, :], power[:, :], ACT.Exp).then_inc(raised_ready, 1)

        gather_units(nc, name, table, width, lists, units_i, unit, act_unit)


def project(nc, name, srcs, ident, outs):
    per_src = T // 4
    groups = len(srcs) * per_src
    nw = len(outs[0])
    with ExitStack() as ctx:
        new_sem = ctx.enter_context(phase_semaphores(nc))
        def sem(nm):
            return new_sem(f"{name}_{nm}")

        turned = [ctx.enter_context(nc.sbuf_tensor(f"{name}_turned{j}", [P, CHUNK], F32)) for j in range(2)]
        turn_ps = [ctx.enter_context(nc.psum_tensor(f"{name}_turn_ps{j}", [P, CHUNK], F32)) for j in range(2)]
        out_ps = [ctx.enter_context(nc.psum_tensor(f"{name}_out_ps{j}", [P, 4, D], F32)) for j in range(2)]
        turn_done, turned_sb, multiplied, evicted = (
            sem("turn_done"), sem("turned_sb"), sem("multiplied"), sem("evicted"))
        block = ctx.enter_context(nc.Block())

        @block.scalar
        def _(act):
            for g in range(groups):
                act.wait_ge(turn_done, g + 1)
                if g >= 2:
                    act.wait_ge(multiplied, nw * (g - 1))
                nc.scalar.copy(turned[g % 2][:, :], turn_ps[g % 2][:, :]).then_inc(turned_sb, 1)

        @block.tensor
        def _(pe):
            def turn(g):
                if g >= 2:
                    pe.wait_ge(turned_sb, g - 1)
                for a in range(4):
                    last = nc.tensor.transpose(turn_ps[g % 2][:, a * P:(a + 1) * P],
                                               srcs[g // per_src][:, 4 * (g % per_src) + a, :], ident[:, :])
                last.then_inc(turn_done, 1)

            turn(0)
            for g in range(groups):
                if g + 1 < groups:
                    turn(g + 1)
                pe.wait_ge(turned_sb, g + 1)
                for w, (weight, _) in enumerate(outs[g // per_src]):
                    m = nw * g + w
                    if m >= 2:
                        pe.wait_ge(evicted, m - 1)
                    for a in range(4):
                        last = nc.tensor.matmul(out_ps[m % 2][:, a, :], turned[g % 2][:, a * P:(a + 1) * P], weight,
                                                start=True, stop=True)
                    last.then_inc(multiplied, 1)

        @block.vector
        def _(dve):
            for g in range(groups):
                for w, (_, evict) in enumerate(outs[g // per_src]):
                    m = nw * g + w
                    dve.wait_ge(multiplied, m + 1)
                    evict(g % per_src, out_ps[m % 2]).then_inc(evicted, 1)


def layer_norms(nc, name, x, rounds):
    with ExitStack() as ctx:
        new_sem = ctx.enter_context(phase_semaphores(nc))
        square = ctx.enter_context(nc.sbuf_tensor(f"{name}_square", [P, T, D], F32))
        mean = ctx.enter_context(nc.sbuf_tensor(f"{name}_mean", [P, T], F32))
        var = ctx.enter_context(nc.sbuf_tensor(f"{name}_var", [P, T], F32))
        dev = ctx.enter_context(nc.sbuf_tensor(f"{name}_dev", [P, T], F32))
        halves = [slice(h * (T // 2), (h + 1) * (T // 2)) for h in range(2)]
        centred = new_sem(f"{name}_centred")
        squared = new_sem(f"{name}_squared")
        var_ready = new_sem(f"{name}_var_ready")
        dev_ready = new_sem(f"{name}_dev_ready")
        block = ctx.enter_context(nc.Block())

        def wide(a):
            return a[:, :].unsqueeze(2).to_broadcast([P, T, D])

        @block.vector
        def _(dve):
            V = nc.vector
            for r, before in enumerate(rounds):
                before(dve)
                V.drain()
                V.tensor_reduce(mean[:, :], x, AX.X, ALU.add)
                V.drain()
                V.tensor_scalar(mean[:, :], mean[:, :], 1.0 / D, None, ALU.mult)
                V.drain()
                for h, part in enumerate(halves):
                    V.tensor_tensor(x[:, part, :], x[:, part, :],
                                    mean[:, part].unsqueeze(2).to_broadcast([P, T // 2, D]), ALU.subtract
                                    ).then_inc(centred, 1)
                for h, part in enumerate(halves):
                    dve.wait_ge(squared, 2 * r + h + 1)
                    V.tensor_reduce(var[:, part], square[:, part, :], AX.X, ALU.add)
                V.drain()
                V.tensor_scalar(var[:, :], var[:, :], 1.0 / D, 1e-5, ALU.mult, ALU.add).then_inc(var_ready, 1)
                dve.wait_ge(dev_ready, r + 1)
                V.reciprocal(var[:, :], dev[:, :])
                V.drain()
                V.tensor_tensor(x, x, wide(var), ALU.mult)
            V.drain()

        @block.scalar
        def _(act):
            for r in range(len(rounds)):
                for h, part in enumerate(halves):
                    act.wait_ge(centred, 2 * r + h + 1)
                    nc.scalar.activation(square[:, part, :], x[:, part, :], ACT.Square).then_inc(squared, 1)
                act.wait_ge(var_ready, r + 1)
                nc.scalar.activation(dev[:, :], var[:, :], ACT.Sqrt).then_inc(dev_ready, 1)


def copy_dram(nc, name, pairs):
    with phase_semaphores(nc) as new_sem, nc.Block() as block:
        moved = new_sem(f"{name}_moved")

        @block.sync
        def _(sp):
            for out, in_ in pairs:
                sp.dma_start(out, in_).then_inc(moved, 16)
            sp.wait_ge(moved, 16 * len(pairs))


def attention_inputs(nc, name, rows, ident, weights, q_t, k_t, z, u2_t):
    w31_t, w2_t = weights
    groups = T // 4
    with ExitStack() as ctx:
        new_sem = ctx.enter_context(phase_semaphores(nc))
        def sem(nm):
            return new_sem(f"{name}_{nm}")

        turned = [ctx.enter_context(nc.sbuf_tensor(f"{name}_turned{j}", [P, CHUNK], F32)) for j in range(2)]
        both = ctx.enter_context(nc.sbuf_tensor(f"{name}_both", [2 * DA, CHUNK], F32))
        turn_ps = [ctx.enter_context(nc.psum_tensor(f"{name}_turn_ps{j}", [P, CHUNK], F32)) for j in range(2)]
        both_ps = ctx.enter_context(nc.psum_tensor(f"{name}_both_ps", [2 * DA, CHUNK], F32))
        q_ps = ctx.enter_context(nc.psum_tensor(f"{name}_q_ps", [DA, CHUNK], F32))
        z_ps = ctx.enter_context(nc.psum_tensor(f"{name}_z_ps", [P, 4, D], F32))
        turn_done, turned_sb, both_done, both_sb, q_done, z_done, q_sb, k_sb, z_added = (
            sem(nm) for nm in ("turn_done", "turned_sb", "both_done", "both_sb", "q_done", "z_done",
                               "q_sb", "k_sb", "z_added"))
        block = ctx.enter_context(nc.Block())

        @block.tensor
        def _(pe):
            def turn(g):
                if g >= 2:
                    pe.wait_ge(turned_sb, g - 1)
                for a in range(4):
                    last = nc.tensor.transpose(turn_ps[g % 2][:, a * P:(a + 1) * P], rows[:, 4 * g + a, 0:D],
                                               ident[:, :])
                last.then_inc(turn_done, 1)

            turn(0)
            for g in range(groups):
                pe.wait_ge(turned_sb, g + 1)
                if g:
                    pe.wait_ge(both_sb, g)
                nc.tensor.matmul(both_ps[:, :], w31_t, turned[g % 2][:, :], start=True, stop=True
                                 ).then_inc(both_done, 1)
                if g + 1 < groups:
                    turn(g + 1)
                if u2_t is not None:
                    if g:
                        pe.wait_ge(z_added, g)
                    for a in range(4):
                        last = nc.tensor.matmul(z_ps[:, a, :], turned[g % 2][:, a * P:(a + 1) * P], u2_t,
                                                start=True, stop=True)
                    last.then_inc(z_done, 1)
                pe.wait_ge(both_sb, g + 1)
                if g:
                    pe.wait_ge(q_sb, g)
                nc.tensor.matmul(q_ps[:, :], w2_t, both[DA:2 * DA, :], start=True, stop=True).then_inc(q_done, 1)

        @block.scalar
        def _(act):
            for g in range(groups):
                act.wait_ge(turn_done, g + 1)
                if g >= 2:
                    act.wait_ge(both_done, g - 1)
                    if u2_t is not None:
                        act.wait_ge(z_done, g - 1)
                nc.scalar.copy(turned[g % 2][:, :], turn_ps[g % 2][:, :]).then_inc(turned_sb, 1)
                act.wait_ge(both_done, g + 1)
                if g:
                    act.wait_ge(q_done, g)
                    act.wait_ge(k_sb, g)
                nc.scalar.copy(both[:, :], both_ps[:, :]).then_inc(both_sb, 1)

        @block.vector
        def _(dve):
            for g in range(groups):
                cols = slice(g * CHUNK, (g + 1) * CHUNK)
                dve.wait_ge(both_sb, g + 1)
                nc.vector.tensor_copy(k_t[:, cols], both[0:DA, :]).then_inc(k_sb, 1)
                if u2_t is not None:
                    dve.wait_ge(z_done, g + 1)
                    nc.vector.tensor_tensor(z[:, 4 * g:4 * g + 4, :], z[:, 4 * g:4 * g + 4, :], z_ps[:, :, :],
                                            ALU.add).then_inc(z_added, 1)
                dve.wait_ge(q_done, g + 1)
                nc.vector.tensor_copy(q_t[:, cols], q_ps[:, :]).then_inc(q_sb, 1)


def top_p_rows(nc, name, listed, skip_ties, shares, ident, q_dram, k_t, rows, attended, unresolved, beside):
    half, adj_tiles, xf, product = beside
    with ExitStack() as ctx:
        new_sem = ctx.enter_context(phase_semaphores(nc))
        def sb(nm, shape, dt=F32):
            return ctx.enter_context(nc.sbuf_tensor(f"{name}_{nm}", shape, dt))

        def sem(nm):
            return new_sem(f"{name}_{nm}")

        PARTS = N // (2 * CHUNK)
        GROUPS = N // CHUNK
        HALF = T // 2
        own = shares[0]
        parts = list(zip(shares[:-1], shares[1:]))

        q_tile = [sb(f"q_tile{j}", [DA, P]) for j in range(2)]
        logit = [sb(f"logit{j}", [P, N + G8]) for j in range(2)]
        prob = [sb(f"prob{j}", [P, N]) for j in range(2)]
        adj_t = [sb(f"adj_t{j}", [P, HALF, P]) for j in range(2)]
        cand = sb("cand", [P, SEGMENTS * G8])
        ordered = sb("ordered", [P, listed])
        raised = sb("raised", [P, listed])
        sums = sb("sums", [P, listed + 1])
        level = sb("level", [P, listed])
        dropped = sb("dropped", [P, listed])
        limit = sb("limit", [P, 1])
        tied = sb("tied", [P, listed])
        neg_top = sb("neg_top", [P, 1])
        masses = sb("masses", [P, PARTS])
        mass = sb("mass", [P, 1])
        goal = sb("goal", [P, 1])
        ones = sb("ones", [P, listed])
        floor = sb("floor", [P, T])
        flags, flags_t = sb("flags", [P, 32]), sb("flags_t", [P, 32])
        total, total_i = sb("total", [P, 1]), sb("total_i", [P, 1], I32)
        eighth, least, ties, last_level = (sb(nm, [P, T]) for nm in ("eighth", "least", "ties", "last_level"))
        count8 = sb("count8", [P, G8])
        chosen = sb("chosen", [P, G8])
        turned = [sb(f"turned{j}", [P, CHUNK]) for j in range(2)]
        logit_ps = [ctx.enter_context(nc.psum_tensor(f"{name}_logit_ps{j}", [P, 2 * CHUNK], F32)) for j in range(2)]
        turn_ps = [ctx.enter_context(nc.psum_tensor(f"{name}_turn_ps{j}", [P, CHUNK], F32)) for j in range(2)]
        acc_ps = ctx.enter_context(nc.psum_tensor(f"{name}_acc_ps", [P, D + 1], F32))
        r_ps = ctx.enter_context(nc.psum_tensor(f"{name}_r_ps", [P, D], F32))
        logit_done, logit_copied, top_ready, order_ready, exp_ready, kept_ready = (
            sem(nm) for nm in ("logit_done", "logit_copied", "top_ready", "order_ready", "exp_ready", "kept_ready"))
        turn_done, turn_copied, group_used, out_ready, r_taken = (
            sem(nm) for nm in ("turn_done", "turn_copied", "group_used", "out_ready", "r_taken"))
        q_loaded = [sem(f"q_loaded{j}") for j in range(2)]
        adj_loaded = [sem(f"adj_loaded{j}") for j in range(2)]
        adj_used = sem("adj_used")
        limit_ready = sem("limit_ready")
        flagged = sem("flagged")
        last_kept = sem("last_kept")
        summed = sem("summed")
        block = ctx.enter_context(nc.Block())

        def bodies(eng, body):
            for t in range(2):
                body(t, t % 2)
            with eng.Fori(1, T // 2 - 1) as i:
                for j in range(2):
                    body(2 * i + j, j)
            for t in range(T - 2, T):
                body(t, t % 2)

        def static(t, test):
            return test(t) if isinstance(t, int) else True

        def wait(eng, t, sem_, value):
            if isinstance(t, int):
                eng.wait_ge(sem_, value)
            else:
                wait_apart(eng, sem_, value)

        @block.sync
        def _(sp):
            def load_q(t, j):
                if static(t, lambda t: t >= 2):
                    sp.wait_ge(logit_done, PARTS * (t - 1))
                sp.dma_start(q_tile[j][:, :], q_dram[:, bass.ds(t * P, P)]).then_inc(q_loaded[j], 16)

            def body(t, j):
                if static(t, lambda t: t >= 2):
                    sp.wait_ge(adj_used, t - 1)
                sp.dma_start(adj_t[j][:, :, :],
                             adj_tiles[bass.ds(t, 1), :, half * HALF:(half + 1) * HALF, :].rearrange(
                                 "a p b c -> p (a b) c")).then_inc(adj_loaded[j], 16)
                if static(t, lambda t: t + 2 < T):
                    load_q(t + 2, j)

            for j in range(2):
                load_q(j, j)
            bodies(sp, body)

        @block.gpsimd
        def _(pool):
            def body(t, j):
                wait(pool, t, limit_ready, t + 1)
                for n, (begin, end) in enumerate(parts):
                    cols = slice(begin * CHUNK, end * CHUNK)
                    nc.gpsimd.tensor_scalar(logit[j][:, cols], logit[j][:, cols], limit[:, :], None, ALU.is_gt
                                            ).then_inc(flagged, 1)
                    wait(pool, t, flagged, len(parts) * t + n + 1)
                    nc.gpsimd.tensor_tensor(prob[j][:, cols], prob[j][:, cols], logit[j][:, cols], ALU.mult
                                            ).then_inc(last_kept, 1)

            bodies(pool, body)

        @block.scalar
        def _(act):
            def take(t, j):
                for c in range(PARTS):
                    act.wait_ge(logit_done, PARTS * t + c + 1)
                    if c == 0 and static(t, lambda t: t >= 2):
                        act.wait_ge(kept_ready, t - 1)
                        act.wait_ge(last_kept, len(parts) * (t - 1))
                    nc.scalar.copy(logit[j][:, c * 2 * CHUNK:(c + 1) * 2 * CHUNK], logit_ps[c % 2][:, :]
                                   ).then_inc(logit_copied, 1)

            def copy_groups(t, groups):
                for g in groups:
                    act.wait_ge(turn_done, GROUPS * t + g + 1)
                    if static(t, lambda t: t >= 1) or g >= 2:
                        act.wait_ge(group_used, GROUPS * t + g - 1)
                    nc.scalar.copy(turned[g % 2][:, :], turn_ps[g % 2][:, :]).then_inc(turn_copied, 1)

            def take_product(t):
                act.wait_ge(group_used, GROUPS * (t + 1))
                nc.scalar.copy(attended[:, bass.ds(t, 1), :].rearrange("p a d -> p (a d)"), acc_ps[:, :]
                               ).then_inc(out_ready, 1)

            def body(t, j):
                first = GROUPS - PARTS + 1
                if static(t, lambda t: t >= 1):
                    copy_groups(t - 1, range(first))
                act.wait_ge(top_ready, t + 1)
                for c in range(PARTS):
                    if c and static(t, lambda t: t >= 1):
                        copy_groups(t - 1, range(first + c - 1, first + c))
                    cols = slice(c * 2 * CHUNK, (c + 1) * 2 * CHUNK)
                    nc.scalar.activation(prob[j][:, cols], logit[j][:, cols], ACT.Exp, bias=neg_top[:, :],
                                         accum_out=masses[:, c:c + 1]).then_inc(exp_ready, 1)
                act.wait_ge(order_ready, t + 1)
                nc.scalar.activation(raised[:, :], ordered[:, :], ACT.Exp, bias=neg_top[:, :]
                                     ).then_inc(exp_ready, 1)
                if static(t, lambda t: t >= 1):
                    take_product(t - 1)
                if static(t, lambda t: t + 1 < T):
                    take(t + 1, 1 - j)

            take(0, 0)
            bodies(act, body)
            copy_groups(T - 1, range(GROUPS))
            take_product(T - 1)

        @block.tensor
        def _(pe):
            def logits(t, j):
                pe.wait_ge(q_loaded[j], 16 * (t // 2) + 16)
                for c in range(PARTS):
                    if static(t, lambda t: t >= 1) or c >= 2:
                        pe.wait_ge(logit_copied, PARTS * t + c - 1)
                    for h in range(2):
                        cols = slice((2 * c + h) * CHUNK, (2 * c + h + 1) * CHUNK)
                        last = nc.tensor.matmul(logit_ps[c % 2][:, h * CHUNK:(h + 1) * CHUNK], q_tile[j][:, :],
                                                k_t[:, cols], start=True, stop=True)
                    last.then_inc(logit_done, 1)

            def apply(t, j):
                pe.wait_ge(kept_ready, t + 1)

                def turn(g):
                    for n, (begin, _) in enumerate(parts):
                        if g == begin:
                            pe.wait_ge(last_kept, len(parts) * t + n + 1)
                    if static(t, lambda t: t >= 1) or g >= 2:
                        pe.wait_ge(turn_copied, GROUPS * t + g - 1)
                    for a in range(4):
                        blk = slice((4 * g + a) * P, (4 * g + a + 1) * P)
                        last = nc.tensor.transpose(turn_ps[g % 2][:, a * P:(a + 1) * P], prob[j][:, blk], ident[:, :])
                    last.then_inc(turn_done, 1)

                turn(0)
                if static(t, lambda t: t >= 1):
                    pe.wait_ge(out_ready, t)
                for g in range(GROUPS):
                    if g + 1 < GROUPS:
                        turn(g + 1)
                    pe.wait_ge(turn_copied, GROUPS * t + g + 1)
                    for a in range(4):
                        last = nc.tensor.matmul(acc_ps[:, :], turned[g % 2][:, a * P:(a + 1) * P],
                                                rows[:, 4 * g + a, :], start=(g == 0 and a == 0),
                                                stop=(g == GROUPS - 1 and a == 3))
                    last.then_inc(group_used, 1)

            def add_neighbours(t, j):
                if static(t, lambda t: t >= 1):
                    pe.wait_ge(r_taken, t)
                pe.wait_ge(adj_loaded[j], 16 * (t // 2) + 16)
                for b in range(HALF):
                    last = nc.tensor.matmul(r_ps[:, :], adj_t[j][:, b, :], xf[:, half * HALF + b, 0:D],
                                            start=b == 0, stop=b == HALF - 1)
                last.then_inc(adj_used, 1)

            def body(t, j):
                if static(t, lambda t: t >= 1):
                    apply(t - 1, 1 - j)
                if static(t, lambda t: t + 1 < T):
                    logits(t + 1, 1 - j)
                add_neighbours(t, j)

            logits(0, 0)
            bodies(pe, body)
            apply(T - 1, 1)

        @block.vector
        def _(dve):
            V = nc.vector
            V.memset(sums[:, 0:1], 0.0)
            V.memset(ones[:, :], 1.0)
            V.memset(flags[:, :], 0.0)
            V.memset(ties[:, :], 0.0)
            if skip_ties:
                go = dve.alloc_register(f"{name}_go")
                n_summed = dve.alloc_register(f"{name}_n_summed")
                dve.reg_mov(n_summed, 0)
            for j in range(2):
                V.memset(logit[j][:, N:], -BIG)
            for k in range(G8):
                V.memset(count8[:, k:k + 1], float(k))
            V.drain()

            def find(t, j):
                wait(dve, t, logit_copied, PARTS * (t + 1))
                for s in range(SEGMENTS):
                    V.max(cand[:, s * G8:(s + 1) * G8], logit[j][:, s * (N // SEGMENTS):(s + 1) * (N // SEGMENTS)])
                V.drain()
                V.tensor_reduce(eighth[:, bass.ds(t, 1)],
                                cand[:, :].rearrange("p (s k) -> p k s", k=G8)[:, G8 - 1:G8, :], AX.X, ALU.max)
                for r in range(0, listed, G8):
                    V.max(ordered[:, r:r + G8], cand[:, :])
                    V.drain()
                    if r == 0:
                        V.tensor_scalar(neg_top[:, :], ordered[:, 0:1], -1.0, None, ALU.mult).then_inc(top_ready, 1)
                    if r + G8 < listed:
                        V.match_replace(cand[:, :], ordered[:, r:r + G8], cand[:, :], -BIG)
                        V.drain()
                V.engine_nop().then_inc(order_ready, 1)

            def raise_ties(t, j, low):
                tie = ties[:, bass.ds(t, 1)]
                V.scalar_tensor_tensor(out=tied[:, :], in0=level[:, :], scalar=low, in1=ones[:, :],
                                       op0=ALU.is_equal, op1=ALU.mult, accum_out=tie)
                V.drain()
                V.tensor_tensor(tie, tie, flags[:, 0:1], ALU.mult)
                V.drain()
                V.tensor_scalar(chosen[:, :], count8[:, :], tie, -BIG, ALU.is_ge, ALU.mult)
                V.drain()
                V.tensor_scalar(chosen[:, :], chosen[:, :], low, None, ALU.add)
                V.drain()
                V.match_replace(logit[j][:, :], chosen[:, :], logit[j][:, :], BIG)
                V.drain()
                V.memset(logit[j][:, N:], -BIG)

            def keep(t, j):
                low = least[:, bass.ds(t, 1)]
                dve.wait_ge(exp_ready, (PARTS + 1) * (t + 1))
                V.tensor_reduce(mass[:, :], masses[:, :], AX.X, ALU.add)
                V.tensor_tensor_scan(sums[:, 1:], raised[:, :], raised[:, :], sums[:, 0:1], ALU.add, ALU.max)
                V.drain()
                V.tensor_scalar(goal[:, :], mass[:, :], TOP_P, None, ALU.mult)
                V.tensor_scalar(floor[:, bass.ds(t, 1)], mass[:, :], 1e-12, None, ALU.mult)
                V.drain()
                V.tensor_scalar(level[:, :], sums[:, 0:listed], goal[:, :], BIG, ALU.is_ge, ALU.mult)
                V.tensor_scalar(dropped[:, :], sums[:, 0:listed], goal[:, :], -BIG, ALU.is_lt, ALU.mult)
                V.drain()
                V.tensor_tensor(level[:, :], level[:, :], ordered[:, :], ALU.add)
                V.tensor_tensor(dropped[:, :], dropped[:, :], ordered[:, :], ALU.add)
                V.drain()
                if static(t, lambda t: t >= 1):
                    dve.wait_ge(last_kept, len(parts) * t)
                V.tensor_reduce(low, level[:, :], AX.X, ALU.min)
                V.tensor_reduce(limit[:, :], dropped[:, :], AX.X, ALU.max)
                V.tensor_copy(last_level[:, bass.ds(t, 1)], level[:, listed - 1:listed])
                V.drain()
                V.tensor_tensor(flags[:, 0:1], limit[:, :], low, ALU.is_equal)
                if skip_ties:
                    V.drain()
                    any_row(dve, nc, flags, flags_t, total, total_i, go, summed, n_summed)
                    with dve.If(0 < dve.snap(go)):
                        raise_ties(t, j, low)
                else:
                    raise_ties(t, j, low)
                V.engine_nop().then_inc(limit_ready, 1)
                cols = slice(0, own * CHUNK)
                V.scalar_tensor_tensor(out=prob[j][:, cols], in0=logit[j][:, cols], scalar=limit[:, :],
                                       in1=prob[j][:, cols], op0=ALU.is_gt, op1=ALU.mult).then_inc(kept_ready, 1)

            def take_r(t):
                dve.wait_ge(adj_used, t + 1)
                part = product[:, bass.ds(t, 1), :].rearrange("p a d -> p (a d)")
                if half:
                    V.tensor_tensor(part, part, r_ps[:, :], ALU.add).then_inc(r_taken, 1)
                else:
                    V.tensor_copy(part, r_ps[:, :]).then_inc(r_taken, 1)

            def body(t, j):
                find(t, j)
                if static(t, lambda t: t >= 1):
                    take_r(t - 1)
                keep(t, j)

            bodies(dve, body)
            take_r(T - 1)
            V.tensor_tensor(unresolved[:, :], eighth[:, :], least[:, :], ALU.is_ge)
            V.tensor_scalar(last_level[:, :], last_level[:, :], 0.5 * BIG, None, ALU.is_lt)
            V.tensor_scalar(ties[:, :], ties[:, :], float(G8), None, ALU.is_gt)
            V.drain()
            V.tensor_tensor(unresolved[:, :], unresolved[:, :], last_level[:, :], ALU.max)
            V.drain()
            V.tensor_tensor(unresolved[:, :], unresolved[:, :], ties[:, :], ALU.max)
            dve.wait_ge(out_ready, T)
            V.tensor_tensor(floor[:, :], floor[:, :], attended[:, :, D:D + 1].rearrange("p t a -> p (t a)"), ALU.max)
            V.drain()
            V.reciprocal(floor[:, :], floor[:, :])
            V.drain()
            V.tensor_tensor(attended[:, :, :], attended[:, :, :],
                            floor[:, :].unsqueeze(2).to_broadcast([P, T, D + 1]), ALU.mult)
            V.drain()


def unresolved_first(nc, name, unresolved, consts, order, count_i, beside):
    below_ones, node_f, node_i = consts
    with ExitStack() as ctx:
        new_sem = ctx.enter_context(phase_semaphores(nc))
        def sb(nm, shape, dt=F32):
            return ctx.enter_context(nc.sbuf_tensor(f"{name}_{nm}", shape, dt))

        def sem(nm):
            return new_sem(f"{name}_{nm}")

        before, totals, offsets, other = (sb(nm, [P, T]) for nm in ("before", "totals", "offsets", "other"))
        place = sb("place", [P, T], I32)
        zeros = sb("zeros", [P, 2], I32)
        ps = ctx.enter_context(nc.psum_tensor(f"{name}_ps", [P, 2, T], F32))
        counted, placed, scattered, cleared = sem("counted"), sem("placed"), sem("scattered"), sem("cleared")
        block = ctx.enter_context(nc.Block())

        @block.tensor
        def _(pe):
            for h in range(2):
                last = nc.tensor.matmul(ps[:, h, :], below_ones[:, h, :], unresolved[:, :], start=True, stop=True)
            last.then_inc(counted, 1)

        @block.vector
        def _(dve):
            V = nc.vector
            V.memset(zeros[:, :], 0).then_inc(cleared, 1)
            dve.wait_ge(counted, 1)
            V.tensor_copy(before[:, :], ps[:, 0, :])
            V.tensor_copy(totals[:, :], ps[:, 1, :])
            V.drain()
            V.tensor_tensor_scan(offsets[:, :], totals[:, :], totals[:, :], 0.0, ALU.add, ALU.max)
            V.drain()
            V.tensor_copy(count_i[:, :], offsets[:, T - 1:T])
            V.tensor_tensor(other[:, :], offsets[:, :], totals[:, :], ALU.subtract)
            V.drain()
            V.tensor_tensor(before[:, :], before[:, :], other[:, :], ALU.add)
            V.drain()
            V.tensor_tensor(other[:, :], node_f, before[:, :], ALU.subtract)
            V.drain()
            V.tensor_scalar(other[:, :], other[:, :], offsets[:, T - 1:T], None, ALU.add)
            V.drain()
            V.tensor_tensor(before[:, :], before[:, :], other[:, :], ALU.subtract)
            V.drain()
            V.tensor_tensor(before[:, :], before[:, :], unresolved[:, :], ALU.mult)
            V.drain()
            V.tensor_tensor(before[:, :], before[:, :], other[:, :], ALU.add)
            V.drain()
            V.tensor_copy(place[:, :], before[:, :]).then_inc(placed, 1)
            beside(dve)
            V.drain()

        @block.gpsimd
        def _(pool):
            pool.wait_ge(cleared, 1)
            pool.dma_start(order[N:N + 2 * P, :].rearrange("(p a) b -> p (a b)", p=P), zeros[:, :]
                           ).then_inc(scattered, 16)
            pool.wait_ge(placed, 1)
            with pool.If(0 < pool.value_load(count_i[0:1, 0:1], min_val=0, max_val=N)):
                for t in range(T):
                    pool.indirect_dma_start(
                        order, bass.IndirectOffsetOnAxis(ap=place[:, t:t + 1].bitcast(U32), axis=0),
                        node_i[:, t:t + 1], None).then_inc(scattered, 16)
                pool.wait_ge(scattered, 16 * (T + 1))
            pool.wait_ge(scattered, 16)


def full_rows(nc, name, halvings, weights, ident, k_t, rows, table, order, count_i, xa_out):
    w1_t, w2_t = weights
    with ExitStack() as ctx:
        new_sem = ctx.enter_context(phase_semaphores(nc))
        def sb(nm, shape, dt=F32):
            return ctx.enter_context(nc.sbuf_tensor(f"{name}_{nm}", shape, dt))

        def sem(nm):
            return new_sem(f"{name}_{nm}")

        ids = [sb(f"ids{j}", [P, 1], I32) for j in range(2)]
        out_ids = [sb(f"out_ids{j}", [P, 1], I32) for j in range(2)]
        own = [sb(f"own{j}", [P, D]) for j in range(2)]
        own_t = sb("own_t", [D, P])
        half = sb("half", [DA, P])
        q_tile = [sb(f"q_tile{j}", [DA, P]) for j in range(2)]
        logit = sb("logit", [P, N])
        prob = [sb(f"prob{j}", [P, N]) for j in range(2)]
        rest = sb("rest", [P, N + G8])
        junk = sb("junk", [P, N], BF16)
        top8 = [sb(f"top8{j}", [P, G8]) for j in range(2)]
        exp8 = [sb(f"exp8{j}", [P, G8]) for j in range(2)]
        neg_top = [sb(f"neg_top{j}", [P, 1]) for j in range(2)]
        mass = [sb(f"mass{j}", [P, 1]) for j in range(2)]
        floor = [sb(f"floor{j}", [P, 1]) for j in range(2)]
        turned = [sb(f"turned{j}", [P, CHUNK]) for j in range(2)]
        out_tile = [sb(f"out_tile{j}", [P, D]) for j in range(2)]
        goal, lo, hi, mid, above, at_least = (sb(nm, [P, 1]) for nm in ("goal", "lo", "hi", "mid", "above", "at_least"))
        hi2, base, below, den, gain = (sb(nm, [P, 1]) for nm in ("hi2", "base", "below", "den", "gain"))
        ends = sb("ends", [P, 1], I32)
        cand, kept, kept_v, chosen, w8 = (sb(nm, [P, G8]) for nm in ("cand", "kept", "kept_v", "chosen", "w8"))
        sums = sb("sums", [P, G8 + 1])
        flags, flags_t = sb("flags", [P, 32]), sb("flags_t", [P, 32])
        total, total_i = sb("total", [P, 1]), sb("total_i", [P, 1], I32)
        logit_ps = [ctx.enter_context(nc.psum_tensor(f"{name}_logit_ps{j}", [P, 2 * CHUNK], F32)) for j in range(2)]
        turn_ps = [ctx.enter_context(nc.psum_tensor(f"{name}_turn_ps{j}", [P, CHUNK], F32)) for j in range(2)]
        acc_ps = ctx.enter_context(nc.psum_tensor(f"{name}_acc_ps", [P, D + 1], F32))
        q_ps = ctx.enter_context(nc.psum_tensor(f"{name}_q_ps", [P, 3, P], F32))
        ids_loaded = [sem(f"ids_loaded{j}") for j in range(2)]
        out_ids_loaded = [sem(f"out_ids_loaded{j}") for j in range(2)]
        own_loaded = [sem(f"own_loaded{j}") for j in range(2)]
        scattered = [sem(f"scattered{j}") for j in range(2)]
        own_turned, own_t_ready, half_done, half_ready, q_done, q_ready = (
            sem(nm) for nm in ("own_turned", "own_t_ready", "half_done", "half_ready", "q_done", "q_ready"))
        logit_done, logit_copied, top_ready, exp_ready, rest_ready, kept_ready = (
            sem(nm) for nm in ("logit_done", "logit_copied", "top_ready", "exp_ready", "rest_ready", "kept_ready"))
        turn_done, turn_copied, group_used, out_ready, out_free, summed = (
            sem(nm) for nm in ("turn_done", "turn_copied", "group_used", "out_ready", "out_free", "summed"))
        acc_free = sem("acc_free")
        block = ctx.enter_context(nc.Block())
        PARTS = N // (2 * CHUNK)
        GROUPS = N // CHUNK

        def if_any(engine_program):
            def run(eng):
                with eng.If(0 < eng.value_load(count_i[0:1, 0:1], min_val=0, max_val=N)):
                    engine_program(eng)
            return run

        def tile_loop(eng, body):
            tiles = (eng.value_load(count_i[0:1, 0:1], min_val=0, max_val=N) + (P - 1)) // P
            with eng.Fori(0, (tiles + 1) // 2) as i:
                def more(step, t, j):
                    with eng.If(t < tiles):
                        step(t, j)

                body(2 * i, 0, lambda step: more(step, 2 * i + 1, 1))
                with eng.If(2 * i + 1 < tiles):
                    body(2 * i + 1, 1, lambda step: more(step, 2 * i + 2, 0))

        @block.sync
        @if_any
        def _(sp):
            def load_ids(t, j):
                sp.dma_start(ids[j][:, :], order[bass.ds(t * P, P), :]).then_inc(ids_loaded[j], 16)

            def body(t, j, more):
                i = t // 2
                sp.wait_ge(own_loaded[j], 16 * i + 16)
                load_ids(t + 2, j)
                sp.wait_ge(out_free, t + 1)
                sp.dma_start(out_ids[j][:, :], order[bass.ds(t * P, P), :]).then_inc(out_ids_loaded[j], 16)

            for j in range(2):
                load_ids(j, j)
            tile_loop(sp, body)

        @block.gpsimd
        @if_any
        def _(pool):
            def gather(t, j, i):
                if isinstance(t, int):
                    pool.wait_ge(ids_loaded[j], 16 * (i + 1))
                else:
                    wait_apart(pool, ids_loaded[j], 16 * (i + 1))
                pool.indirect_dma_start(own[j][:, :], None, table,
                                        bass.IndirectOffsetOnAxis(ap=ids[j][:, :].bitcast(U32), axis=0)
                                        ).then_inc(own_loaded[j], 16)

            def body(t, j, more):
                i = t // 2
                pool.wait_ge(rest_ready, t + 1)
                nc.gpsimd.tensor_tensor(prob[j][:, :], prob[j][:, :], rest[:, 0:N], ALU.subtract
                                        ).then_inc(kept_ready, 1)
                wait_apart(pool, own_turned, t + 1)
                gather(t + 2, j, i + 1)
                wait_apart(pool, out_ids_loaded[j], 16 * i + 16)
                wait_apart(pool, out_ready, t + 1)
                pool.indirect_dma_start(xa_out, bass.IndirectOffsetOnAxis(ap=out_ids[j][:, :].bitcast(U32), axis=0),
                                        out_tile[j][:, :], None).then_inc(scattered[j], 16)
                wait_apart(pool, scattered[j], 16 * i + 16)
                nc.gpsimd.engine_nop().then_inc(out_free, 1)

            nc.gpsimd.engine_nop().then_inc(out_free, 2)
            nc.gpsimd.engine_nop().then_inc(kept_ready, 1)
            for j in range(2):
                gather(j, j, 0)
            tile_loop(pool, body)

        @block.tensor
        @if_any
        def _(pe):
            def make_q(t, j, i):
                pe.wait_ge(own_loaded[j], 16 * (i + 1))
                if not (isinstance(t, int) and t == 0):
                    pe.wait_ge(q_ready, t)
                nc.tensor.transpose(q_ps[:, 0, :], own[j][:, :], ident[:, :]).then_inc(own_turned, 1)
                pe.wait_ge(own_t_ready, t + 1)
                nc.tensor.matmul(q_ps[0:DA, 1, :], w1_t, own_t[:, :], start=True, stop=True).then_inc(half_done, 1)
                if isinstance(t, int):
                    pe.wait_ge(half_ready, t + 1)
                else:
                    wait_apart(pe, half_ready, t + 1)
                nc.tensor.matmul(q_ps[0:DA, 2, :], w2_t, half[:, :], start=True, stop=True).then_inc(q_done, 1)

            def logits(t, j):
                pe.wait_ge(q_ready, t + 1)
                for c in range(PARTS):
                    if not (isinstance(t, int) and t == 0 and c < 2):
                        pe.wait_ge(logit_copied, PARTS * t + c - 1)
                    for h in range(2):
                        cols = slice((2 * c + h) * CHUNK, (2 * c + h + 1) * CHUNK)
                        last = nc.tensor.matmul(logit_ps[c % 2][:, h * CHUNK:(h + 1) * CHUNK], q_tile[j][:, :],
                                                k_t[:, cols], start=True, stop=True)
                    last.then_inc(logit_done, 1)

            def apply(t, j):
                pe.wait_ge(kept_ready, t + 2)

                def turn(g):
                    pe.wait_ge(turn_copied, GROUPS * t + g + 1)
                    for a in range(4):
                        blk = slice((4 * g + a) * P, (4 * g + a + 1) * P)
                        last = nc.tensor.transpose(turn_ps[g % 2][:, a * P:(a + 1) * P], prob[j][:, blk], ident[:, :])
                    last.then_inc(turn_done, 1)

                turn(0)
                pe.wait_ge(acc_free, t + 1)
                for g in range(GROUPS):
                    if g + 1 < GROUPS:
                        turn(g + 1)
                    pe.wait_ge(turn_copied, GROUPS * t + g + 3)
                    for a in range(4):
                        last = nc.tensor.matmul(acc_ps[:, :], turned[g % 2][:, a * P:(a + 1) * P],
                                                rows[:, 4 * g + a, :], start=(g == 0 and a == 0),
                                                stop=(g == GROUPS - 1 and a == 3))
                    last.then_inc(group_used, 1)

            def body(t, j, more):
                more(logits)
                make_q(t + 2, j, t // 2 + 1)
                apply(t, j)

            for j in range(2):
                make_q(j, j, 0)
            logits(0, 0)
            tile_loop(pe, body)

        @block.scalar
        @if_any
        def _(act):
            def make_q(t, j):
                act.wait_ge(own_turned, t + 1)
                if not (isinstance(t, int) and t == 0):
                    act.wait_ge(half_done, t)
                nc.scalar.copy(own_t[:, :], q_ps[:, 0, :]).then_inc(own_t_ready, 1)
                act.wait_ge(half_done, t + 1)
                if not (isinstance(t, int) and t == 0):
                    act.wait_ge(q_done, t)
                nc.scalar.copy(half[:, :], q_ps[0:DA, 1, :]).then_inc(half_ready, 1)
                act.wait_ge(q_done, t + 1)
                if not (isinstance(t, int) and t < 2):
                    act.wait_ge(logit_done, PARTS * (t - 1))
                nc.scalar.copy(q_tile[j][:, :], q_ps[0:DA, 2, :]).then_inc(q_ready, 1)

            def take(t, j):
                if not (isinstance(t, int) and t == 0):
                    act.wait_ge(exp_ready, 2 * t)
                for c in range(PARTS):
                    act.wait_ge(logit_done, PARTS * t + c + 1)
                    nc.scalar.copy(logit[:, c * 2 * CHUNK:(c + 1) * 2 * CHUNK], logit_ps[c % 2][:, :]
                                   ).then_inc(logit_copied, 1)

            def raise_(t, j):
                act.wait_ge(top_ready, t + 1)
                nc.scalar.activation(exp8[j][:, :], top8[j][:, :], ACT.Exp, bias=neg_top[j][:, :]
                                     ).then_inc(exp_ready, 1)
                nc.scalar.activation(prob[j][:, :], logit[:, :], ACT.Exp, bias=neg_top[j][:, :],
                                     accum_out=mass[j][:, :]).then_inc(exp_ready, 1)

            def copy_groups(t, j):
                for g in range(GROUPS):
                    act.wait_ge(turn_done, GROUPS * t + g + 1)
                    act.wait_ge(group_used, GROUPS * t + g + 1)
                    nc.scalar.copy(turned[g % 2][:, :], turn_ps[g % 2][:, :]).then_inc(turn_copied, 1)

            def body(t, j, more):
                more(take)
                more(raise_)
                make_q(t + 2, j)
                copy_groups(t, j)

            act_spare = sb("act_spare", [P, 1])
            nc.scalar.copy(act_spare[:, :], ident[:, 0:1]).then_inc(turn_copied, 2)
            for j in range(2):
                make_q(j, j)
            take(0, 0)
            raise_(0, 0)
            tile_loop(act, body)

        @block.vector
        @if_any
        def _(dve):
            V = nc.vector
            go = dve.alloc_register(f"{name}_go")
            n_summed = dve.alloc_register(f"{name}_n_summed")
            dve.reg_mov(n_summed, 0)
            V.memset(flags[:, :], 0.0).then_inc(group_used, 2)
            V.memset(at_least[:, :], 0.0).then_inc(acc_free, 1)
            V.drain()

            def find_top(t, j):
                if isinstance(t, int):
                    dve.wait_ge(logit_copied, PARTS * (t + 1))
                else:
                    wait_apart(dve, logit_copied, PARTS * (t + 1))
                V.max(top8[j][:, :], logit[:, :])
                V.drain()
                V.tensor_scalar(neg_top[j][:, :], top8[j][:, 0:1], -1.0, None, ALU.mult).then_inc(top_ready, 1)

            def prefix(values):
                V.tensor_tensor_scan(sums[:, 1:G8 + 1], values, values, sums[:, 0:1], ALU.add, ALU.max)
                V.drain()
                V.tensor_scalar(kept[:, :], sums[:, 0:G8], goal[:, :], None, ALU.is_lt)
                V.drain()

            def bisect(t, j):
                dve.wait_ge(exp_ready, 2 * (t + 1))
                V.tensor_scalar(goal[:, :], mass[j][:, :], TOP_P, None, ALU.mult)
                V.tensor_scalar(lo[:, :], mass[j][:, :], (1.0 - TOP_P) / N * 0.99, None, ALU.mult)
                V.tensor_scalar(floor[j][:, :], mass[j][:, :], 1e-12, None, ALU.mult)
                V.memset(sums[:, 0:1], 0.0)
                V.drain()
                prefix(exp8[j][:, :])
                V.tensor_scalar(w8[:, :], kept[:, :], -BIG, BIG, ALU.mult, ALU.add)
                V.drain()
                V.tensor_tensor(w8[:, :], w8[:, :], exp8[j][:, :], ALU.add)
                V.drain()
                V.tensor_reduce(hi[:, :], w8[:, :], AX.X, ALU.min)
                V.drain()
                for _ in range(halvings):
                    V.tensor_tensor(ends[:, :], lo[:, :].bitcast(I32), hi[:, :].bitcast(I32), ALU.add)
                    V.drain()
                    V.tensor_scalar(mid[:, :].bitcast(I32), ends[:, :], 1, None, ALU.arith_shift_right)
                    V.drain()
                    V.scalar_tensor_tensor(out=junk[:, :], in0=prob[j][:, :], scalar=mid[:, :], in1=prob[j][:, :],
                                           op0=ALU.is_gt, op1=ALU.mult, accum_out=above[:, :])
                    V.drain()
                    V.tensor_tensor(at_least[:, :], above[:, :], goal[:, :], ALU.is_ge)
                    V.drain()
                    V.scalar_tensor_tensor(out=lo[:, :], in0=at_least[:, :], scalar=mid[:, :], in1=lo[:, :],
                                           op0=ALU.mult, op1=ALU.max)
                    V.scalar_tensor_tensor(out=hi2[:, :], in0=at_least[:, :], scalar=BIG, in1=mid[:, :],
                                           op0=ALU.mult, op1=ALU.add)
                    V.drain()
                    V.tensor_tensor(hi[:, :], hi[:, :], hi2[:, :], ALU.min)
                    V.drain()

            def cut(t, j):
                dve.wait_ge(kept_ready, t + 1)
                V.scalar_tensor_tensor(out=rest[:, 0:N], in0=prob[j][:, :], scalar=hi[:, :], in1=prob[j][:, :],
                                       op0=ALU.is_le, op1=ALU.mult, accum_out=below[:, :])
                V.drain()
                V.memset(rest[:, N:], -1.0)
                V.tensor_tensor(base[:, :], mass[j][:, :], below[:, :], ALU.subtract)
                V.drain()
                V.tensor_copy(sums[:, 0:1], base[:, :])
                dve.reg_mov(go, 1)
                with dve.While(lambda: dve.snap(go)):
                    V.max(cand[:, :], rest[:, :])
                    V.drain()
                    prefix(cand[:, :])
                    V.scalar_tensor_tensor(out=kept[:, :], in0=cand[:, :], scalar=lo[:, :], in1=kept[:, :],
                                           op0=ALU.is_gt, op1=ALU.mult)
                    V.drain()
                    V.tensor_tensor(kept_v[:, :], cand[:, :], kept[:, :], ALU.mult)
                    V.tensor_copy(flags[:, 0:1], kept[:, G8 - 1:G8])
                    V.tensor_scalar(chosen[:, :], kept[:, :], -1.0, None, ALU.add)
                    V.drain()
                    V.tensor_tensor(chosen[:, :], chosen[:, :], kept_v[:, :], ALU.add)
                    V.tensor_reduce(gain[:, :], kept_v[:, :], AX.X, ALU.add)
                    V.drain()
                    V.match_replace(rest[:, :], chosen[:, :], rest[:, :], 0.0)
                    V.tensor_tensor(sums[:, 0:1], sums[:, 0:1], gain[:, :], ALU.add)
                    V.drain()
                    V.memset(rest[:, N:], -1.0)
                    any_row(dve, nc, flags, flags_t, total, total_i, go, summed, n_summed)
                V.drain()
                V.engine_nop().then_inc(rest_ready, 1)

            def normalise(t, j):
                dve.wait_ge(group_used, GROUPS * (t + 1) + 2)
                V.tensor_tensor(den[:, :], floor[j][:, :], acc_ps[:, D:D + 1], ALU.max)
                V.drain()
                V.reciprocal(gain[:, :], den[:, :])
                V.drain()
                dve.wait_ge(out_free, t + 1)
                V.tensor_scalar(out_tile[j][:, :], acc_ps[:, 0:D], gain[:, :], None, ALU.mult).then_inc(out_ready, 1)
                V.drain()
                V.engine_nop().then_inc(acc_free, 1)

            def body(t, j, more):
                more(find_top)
                cut(t, j)
                more(bisect)
                normalise(t, j)

            find_top(0, 0)
            bisect(0, 0)
            tile_loop(dve, body)
            V.drain()


def program(nc, a, out):
    lists = nc.dram_tensor("lists", [MAX_UNITS, P, LIST], I32, kind="Internal").ap()
    xa_dram = [nc.dram_tensor(f"xa_dram{s}", [N, D], F32, kind="Internal").ap() for s in range(2)]
    order = [nc.dram_tensor(f"order{s}", [N + 2 * P, 1], I32, kind="Internal").ap() for s in range(2)]
    q_dram = nc.dram_tensor("q_dram", [DA, N], F32, kind="Internal").ap()
    hp_dram = nc.dram_tensor("hp_dram", [N, D + H], F32, kind="Internal").ap()
    kv_dram = nc.dram_tensor("kv_dram", [N, 2 * D], F32, kind="Internal").ap()
    with ExitStack() as ctx:
        def sb(name, shape, dt=F32):
            return ctx.enter_context(nc.sbuf_tensor(name, shape, dt))

        ident = sb("unit_matrix", [P, P])
        z = sb("result", [P, T, D])
        rdeg = sb("rdeg", [P, T])
        units_i = sb("units_i", [P, 1], I32)

        with nc.sbuf_tensor("u_rows", [P, 4, D], F32) as u_t, \
             nc.sbuf_tensor("ln_gb", [P, 2, D], F32) as ln_gb:
            copy_dram(nc, "in0", [
                (ident[:, :], a["ident"]), (z[:, :, :], node_view(a["x"])),
                (u_t[:, 0:2, :], a["U1_t"].rearrange("s i o -> i s o")),
                (u_t[:, 2:4, :], a["U2_t"].rearrange("s i o -> i s o")),
                (ln_gb[:, 0, :], a["ln_g"].partition_broadcast(P)), (ln_gb[:, 1, :], a["ln_b"].partition_broadcast(P)),
            ])
            def nothing(dve):
                pass

            def add_z(weight):
                def evict(g, ps):
                    part = z[:, 4 * g:4 * g + 4, :]
                    return nc.vector.tensor_tensor(part, part, ps[:, :, :], ALU.add)
                return [(weight, evict)]

            with ExitStack() as l0:
                def sb0(name, shape, dt=F32):
                    return l0.enter_context(nc.sbuf_tensor(name, shape, dt))

                w_t = sb0("w_t", [P, 3, DA])
                rows = sb0("rows", [P, T, D + 1])
                xf1 = sb0("xf1", [P, T, D + 1])
                k_t = sb0("k_t", [DA, N])
                below_ones = sb0("below_and_ones", [P, 2, P])
                node_f = sb0("node_numbers", [P, T])
                node_i = sb0("node_numbers_i", [P, T], I32)
                unresolved = sb0("unresolved", [P, T])
                count_i = sb0("count_i", [P, 1], I32)
                copy_dram(nc, "in1", [
                    (rows[:, :, 0:D], node_view(a["x"])), (below_ones[:, :, :], a["below_ones"]),
                    (node_f[:, :], a["node_f"]), (node_i[:, :], a["node_i"]),
                    (w_t[:, 0, :], a["W3_t"]), (w_t[:, 1, :], a["W1_t"]),
                    (w_t[0:DA, 2, :], a["W2_t"]), (w_t[DA:2 * DA, 2, :], a["W2_t"]),
                ])
                weights = (w_t[:, 0:2, :].rearrange("p a b -> p (a b)"), w_t[DA:2 * DA, 2, :])
                with nc.Block() as block:
                    @block.vector
                    def _(dve):
                        V = nc.vector
                        V.memset(rows[:, :, D:D + 1], 1.0)
                        V.drain()

                find_neighbours(nc, a["adj"], a["adj_tiles"], a["tile_ids"], ident, lists, units_i, rows, xf1,
                                rdeg)

                def divide_product(dve):
                    V = nc.vector
                    V.tensor_tensor(xf2[:, :, :], xf2[:, :, :], xf1[:, :, 0:D], ALU.add)
                    V.drain()
                    V.tensor_tensor(xf2[:, :, :], xf2[:, :, :], rdeg[:, :].unsqueeze(2).to_broadcast([P, T, D]),
                                    ALU.mult)

                def step(s, table, beside, xa_out, beside_order):
                    with nc.sbuf_tensor(f"q_t{s}", [DA, N], F32) as q_t:
                        attention_inputs(nc, f"in_s{s}", rows, ident, weights, q_t, k_t, z,
                                         u_t[:, 2, :] if s else None)
                        copy_dram(nc, f"q_out{s}", [(q_dram, q_t[:, :])])
                    with nc.sbuf_tensor(f"attended{s}", [P, T, D + 1], F32) as attended:
                        top_p_rows(nc, f"l{s}", LISTED[s], SKIP_TIES[s], SHARES[s], ident, q_dram, k_t, rows, attended,
                                   unresolved, beside)
                        copy_dram(nc, f"attended_out{s}", [(node_view(xa_out), attended[:, :, 0:D])])
                    unresolved_first(nc, f"o{s}", unresolved, (below_ones, node_f[:, :], node_i), order[s], count_i,
                                     beside_order)
                    full_rows(nc, f"f{s}", BISECTIONS[s], (w_t[:, 1, :], w_t[0:DA, 2, :]), ident, k_t, rows, table, order[s], count_i,
                              xa_out)
                    copy_dram(nc, f"xa{s}", [(rows[:, :, 0:D], node_view(xa_out))])

                with nc.sbuf_tensor("xf2", [P, T, D], F32) as xf2:
                    step(0, a["x"], (0, a["adj_tiles"], xf1, xf2), xa_dram[0], nothing)
                    step(1, xa_dram[0], (1, a["adj_tiles"], xf1, xf2), xa_dram[1], divide_product)
                    project(nc, "u", [xf1[:, :, 0:D], xf2[:, :, :], rows[:, :, 0:D]], ident,
                            [add_z(u_t[:, c, :]) for c in (0, 1, 3)])

            with nc.sbuf_tensor("nodes", [P, T, D], F32) as x:
                copy_dram(nc, "in_x", [(x[:, :, :], node_view(a["x"]))])

                def add_layer0(dve):
                    V = nc.vector
                    V.drain()
                    V.tensor_tensor(z[:, :, :], z[:, :, :], ln_gb[:, 0:1, :].to_broadcast([P, T, D]), ALU.mult)
                    V.drain()
                    V.tensor_tensor(z[:, :, :], z[:, :, :], ln_gb[:, 1:2, :].to_broadcast([P, T, D]), ALU.add)
                    V.drain()
                    V.tensor_tensor(z[:, :, :], z[:, :, :], x[:, :, :], ALU.add)

                layer_norms(nc, "ln0", z[:, :, :], [nothing, add_layer0])

        acc = sb("acc", [P, T, D])
        denom = sb("denom", [P, T, H])

        def normalise_heads(V):
            V.reciprocal(denom[:, :, :], denom[:, :, :])
            V.drain()
            a4 = acc[:, :, :].rearrange("p t (h f) -> p (t h) f", h=H)
            V.tensor_tensor(a4, a4, denom[:, :, :].rearrange("p t h -> p (t h)").unsqueeze(2).to_broadcast(
                [P, T * H, HD]), ALU.mult)
            V.drain()

        with ExitStack() as l1:
            def sb1(name, shape):
                return l1.enter_context(nc.sbuf_tensor(name, shape, F32))

            w = sb1("l1_w", [P, D])
            a_rows = sb1("l1_a", [P, H, 2 * HD])
            hp = sb1("hp", [P, T, D + H])
            prod = sb1("hp_prod", [P, T, D])
            src = sb1("src", [P, T, H])
            copy_dram(nc, "in2", [(w[:, :], a["L1_W"]),
                                  (a_rows[:, :, :], a["L1_a"].rearrange("h f -> (h f)").partition_broadcast(P).rearrange(
                                      "p (h f) -> p h f", h=H))])
            project(nc, "hp", [z[:, :, :]], ident, [[(w[:, :], lambda g, ps: nc.vector.tensor_copy(
                hp[:, 4 * g:4 * g + 4, 0:D], ps[:, :, :]))]])
            with nc.Block() as block:
                @block.vector
                def _(dve):
                    V = nc.vector
                    for half, dst in ((0, src[:, :, :]), (1, hp[:, :, D:D + H])):
                        for h in range(H):
                            V.tensor_tensor(prod[:, :, h * HD:(h + 1) * HD], hp[:, :, h * HD:(h + 1) * HD],
                                            a_rows[:, h:h + 1, half * HD:(half + 1) * HD].to_broadcast([P, T, HD]),
                                            ALU.mult)
                        V.drain()
                        V.tensor_reduce(dst, prod[:, :, :].rearrange("p t (h f) -> p t h f", h=H), AX.X, ALU.add)
                        V.drain()
            copy_dram(nc, "hp_out", [(node_view(hp_dram), hp[:, :, :])])

            def scores1(dve, t, values, got, score, prod_):
                V = nc.vector
                V.tensor_tensor(score[:, :, :], got[:, :, D:D + H],
                                src[:, bass.ds(t, 1), :].to_broadcast([P, G8, H]), ALU.add)
                V.drain()
                V.scalar_tensor_tensor(out=score[:, :, :], in0=score[:, :, :], scalar=0.2, in1=score[:, :, :],
                                       op0=ALU.mult, op1=ALU.max)

            graph_attention(nc, "a1", hp_dram, D + H, 0, scores1, lists, units_i, acc, denom)

        def elu_in_place(name):
            with nc.sbuf_tensor(f"{name}_neg", [P, T, D], F32) as neg, phase_semaphores(nc) as new_sem, \
                 nc.Block() as block:
                neg_ready, neg_raised = new_sem(f"{name}_n"), new_sem(f"{name}_e")

                @block.vector
                def _(dve):
                    V = nc.vector
                    normalise_heads(V)
                    V.tensor_scalar(neg[:, :, :], acc[:, :, :], 0.0, None, ALU.min).then_inc(neg_ready, 1)
                    V.tensor_scalar(acc[:, :, :], acc[:, :, :], 0.0, -1.0, ALU.max, ALU.add)
                    V.drain()
                    V.tensor_tensor(z[:, :, :], z[:, :, :], acc[:, :, :], ALU.add)
                    dve.wait_ge(neg_raised, 1)
                    V.drain()
                    V.tensor_tensor(z[:, :, :], z[:, :, :], neg[:, :, :], ALU.add)
                    V.drain()

                @block.scalar
                def _(act):
                    act.wait_ge(neg_ready, 1)
                    nc.scalar.activation(neg[:, :, :], neg[:, :, :], ACT.Exp).then_inc(neg_raised, 1)

        elu_in_place("elu")
        layer_norms(nc, "ln1", z[:, :, :], [lambda dve: None])

        with ExitStack() as l2:
            def sb2(name, shape):
                return l2.enter_context(nc.sbuf_tensor(name, shape, F32))

            w = sb2("l2_w", [P, 4, D])
            bias = sb2("l2_bias", [P, 4, D])
            g_bias = sb2("g_bias", [P, 1])
            q = sb2("q", [P, T, D])
            copy_dram(nc, "in3", [
                (w[:, 0:3, :], a["Wqkv"].rearrange("i (c o) -> i c o", c=3)), (w[:, 3, :], a["Wout"]),
                (bias[:, 0:3, :], a["bqkv"].partition_broadcast(P).rearrange("p (c o) -> p c o", c=3)),
                (bias[:, 3, :], a["bout"].partition_broadcast(P)), (g_bias[:, :], a["graph_bias"].partition_broadcast(P)),
            ])
            with nc.sbuf_tensor("kv", [P, T, 2 * D], F32) as kv:
                def with_bias(c, dst):
                    return (w[:, c, :], lambda g, ps: nc.vector.tensor_tensor(
                        dst[:, 4 * g:4 * g + 4, :], ps[:, :, :], bias[:, c:c + 1, :].to_broadcast([P, 4, D]), ALU.add))

                project(nc, "qkv", [z[:, :, :]], ident, [[with_bias(0, q[:, :, :]), with_bias(1, kv[:, :, 0:D]),
                                                          with_bias(2, kv[:, :, D:2 * D])]])
                copy_dram(nc, "kv_out", [(node_view(kv_dram), kv[:, :, :])])
            edge = sb2("edge", [P, G8])

            def scores2(dve, t, values, got, score, prod):
                V = nc.vector
                V.tensor_tensor(prod[:, :].rearrange("p (k d) -> p k d", k=G8), got[:, :, 0:D],
                                q[:, bass.ds(t, 1), :].to_broadcast([P, G8, D]), ALU.mult)
                V.tensor_scalar(edge[:, :], values, g_bias[:, :], None, ALU.mult)
                V.drain()
                V.tensor_reduce(score[:, :, :], prod[:, :].rearrange("p (k h f) -> p k h f", k=G8, h=H), AX.X, ALU.add)
                V.drain()
                V.scalar_tensor_tensor(out=score[:, :, :], in0=score[:, :, :], scalar=HD ** -0.5,
                                       in1=edge[:, :].unsqueeze(2).to_broadcast([P, G8, H]),
                                       op0=ALU.mult, op1=ALU.add)

            graph_attention(nc, "a2", kv_dram, 2 * D, D, scores2, lists, units_i, acc, denom)
            with nc.Block() as block:
                @block.vector
                def _(dve):
                    normalise_heads(nc.vector)

            def add_out(g, ps):
                part = z[:, 4 * g:4 * g + 4, :]
                return nc.vector.tensor_tensor(part, part, ps[:, :, :], ALU.add)

            project(nc, "wout", [acc[:, :, :]], ident, [[(w[:, 3, :], add_out)]])
            layer_norms(nc, "ln2", z[:, :, :], [lambda dve: nc.vector.tensor_tensor(
                z[:, :, :], z[:, :, :], bias[:, 3:4, :].to_broadcast([P, T, D]), ALU.add)])

        with ExitStack() as l3:
            w = l3.enter_context(nc.sbuf_tensor("l3_w", [P, D], F32))
            root = l3.enter_context(nc.sbuf_tensor("root", [P, T], F32))
            rooted = l3.enter_context(phase_semaphores(nc))("rooted")
            copy_dram(nc, "in4", [(w[:, :], a["L3_W_t"])])
            project(nc, "support", [z[:, :, :]], ident, [[(w[:, :], lambda g, ps: nc.vector.tensor_copy(
                acc[:, 4 * g:4 * g + 4, :], ps[:, :, :]))]])
            with nc.Block() as block:
                @block.scalar
                def _(act):
                    nc.scalar.activation(root[:, :], rdeg[:, :], ACT.Sqrt).then_inc(rooted, 1)

                @block.vector
                def _(dve):
                    dve.wait_ge(rooted, 1)
                    nc.vector.tensor_tensor(acc[:, :, :], acc[:, :, :],
                                            root[:, :].unsqueeze(2).to_broadcast([P, T, D]), ALU.mult)
                    nc.vector.drain()
            out3 = l3.enter_context(nc.sbuf_tensor("out3", [P, T, D], F32))
            adj_times(nc, "l3", a["adj_tiles"], acc[:, :, :], out3)

            def finish(dve):
                V = nc.vector
                V.tensor_tensor(out3[:, :, :], out3[:, :, :], root[:, :].unsqueeze(2).to_broadcast([P, T, D]),
                                ALU.mult)
                V.drain()
                V.scalar_tensor_tensor(out=z[:, :, :], in0=out3[:, :, :], scalar=0.0, in1=z[:, :, :],
                                       op0=ALU.max, op1=ALU.add)

            layer_norms(nc, "ln3", z[:, :, :], [finish])
        copy_dram(nc, "result", [(node_view(out), z[:, :, :])])


def kernel(**inputs):
    import numpy as np
    import concourse.bacc as bacc
    from concourse.bass_utils import run_bass_kernel_spmd

    def arr(v):
        return np.ascontiguousarray(v)

    i = {k: np.asarray(v) for k, v in inputs.items()}
    arrays = {
        "x": arr(i["x"]), "adj": arr(i["adj"]),
        "adj_tiles": arr(i["adj"].reshape(T, P, T, P).transpose(0, 3, 2, 1)),
        "W1_t": arr(i["L0_gnn_W1"].T), "W2_t": arr(i["L0_gnn_W2"].T), "W3_t": arr(i["L0_gnn_W3"].T),
        "U1_t": arr(i["L0_gnn_U1"].transpose(0, 2, 1)), "U2_t": arr(i["L0_gnn_U2"].transpose(0, 2, 1)),
        "ln_g": arr(i["L0_gnn_ln_g"]), "ln_b": arr(i["L0_gnn_ln_b"]),
        "L1_W": arr(i["L1_gnn_W"]), "L1_a": arr(i["L1_gnn_a"]),
        "Wqkv": arr(i["L2_gnn_Wqkv"]), "bqkv": arr(i["L2_gnn_bqkv"]), "Wout": arr(i["L2_gnn_Wout"]),
        "bout": arr(i["L2_gnn_bout"]), "graph_bias": arr(i["L2_gnn_graph_bias"].reshape(1)),
        "L3_W_t": arr(i["L3_gnn_W"].T),
        "ident": np.eye(P, dtype=np.float32),
        "below_ones": np.stack([np.triu(np.ones((P, P), np.float32), 1), np.ones((P, P), np.float32)], 1),
        "node_f": np.arange(N, dtype=np.float32).reshape(T, P).T.copy(),
        "node_i": np.arange(N, dtype=np.int32).reshape(T, P).T.copy(),
        "tile_ids": np.tile(np.arange(T, dtype=np.int32), (P, 1)),
    }
    nc = bacc.Bacc("TRN2", target_bir_lowering=False, num_devices=1)
    aps = {n: nc.dram_tensor(n, v.shape, mybir.dt.from_np(v.dtype), kind="ExternalInput").ap()
           for n, v in arrays.items()}
    out = nc.dram_tensor("out", (N, D), F32, kind="ExternalOutput").ap()
    program(nc, aps, out)
    r = run_bass_kernel_spmd(nc, [arrays], core_ids=[0])
    return r.results[0]["out"]
```
